# Optimizing a Trainium2 kernel written in Bass

```python
import numpy as np
import jax
import jax.numpy as jnp

def _softmax(x, axis=-1):
    return jax.nn.softmax(x, axis=axis)

def _gelu(x):
    return jax.nn.gelu(x, approximate=True)

def _silu(x):
    return jax.nn.silu(x)

def _sigmoid(x):
    return jax.nn.sigmoid(x)

def _layernorm(x, axis=-1, eps=1e-05):
    m = jnp.mean(x, axis=axis, keepdims=True)
    v = jnp.var(x, axis=axis, keepdims=True)
    return (x - m) / jnp.sqrt(v + eps)

def _scatter_add(tgt, idx, src, axis=0):
    return tgt.at[idx].add(src)

def _segment_sum(src, seg, n):
    return jax.ops.segment_sum(src, seg, n)
kernel_name = 'mk_early_fusion_d1_tok_img256_r4_a3a957'

def setup_inputs(seed: int=0):
    np.random.seed(seed)
    _w = jnp.asarray

    def _rec_inputs():
        import jax
        import jax.numpy as jnp
        _rk = jax.random.key(seed)
        x = 7.57192e-06 + 1.00007 * jax.random.normal(jax.random.fold_in(_rk, 1), (32, 3, 224, 224), jnp.float32)
        txt = 0.00191194 + 0.0219993 * jax.random.normal(jax.random.fold_in(_rk, 2), (32, 128, 64), jnp.float32)
        return (x, txt)
    x, txt = _rec_inputs()

    def _L0_tok_setup():
        import jax, jax.numpy as jnp
        import numpy as np
        import math
        GRID = 28
        NUM_PATCHES = GRID * GRID
        PATCH = 8
        IN_CH = 3
        HIDDEN = 64
        BATCH = 64

        def build_grid_edges():
            edges = []
            for i in range(GRID):
                for j in range(GRID):
                    cur = i * GRID + j
                    if j < GRID - 1:
                        edges.append([cur, cur + 1])
                    if i < GRID - 1:
                        edges.append([cur, cur + GRID])
            e = np.asarray(edges, dtype=np.int32).T
            e = np.concatenate([e, e[::-1]], axis=1)
            return jnp.asarray(e)

        def sin_positional_encoding(n, d):
            pos = jnp.arange(n, dtype=jnp.float32)[:, None]
            div = jnp.exp(jnp.arange(0, d, 2, dtype=jnp.float32) * (-math.log(10000.0) / d))
            pe = jnp.zeros((n, d), dtype=jnp.float32)
            pe = pe.at[:, 0::2].set(jnp.sin(pos * div))
            pe = pe.at[:, 1::2].set(jnp.cos(pos * div))
            return pe
        key = jax.random.key(seed)
        ks = jax.random.split(key, 8)
        s = 0.02
        return {'x': jax.random.normal(ks[0], (BATCH, IN_CH, 224, 224), dtype=jnp.float32), 'W_embed': jax.random.normal(ks[1], (IN_CH * PATCH * PATCH, HIDDEN), dtype=jnp.float32) * s, 'b_embed': jax.random.normal(ks[2], (HIDDEN,), dtype=jnp.float32) * s, 'W_gcn': jax.random.normal(ks[3], (3, HIDDEN, HIDDEN), dtype=jnp.float32) * s, 'b_gcn': jax.random.normal(ks[4], (3, HIDDEN), dtype=jnp.float32) * s, 'W_out': jax.random.normal(ks[5], (HIDDEN, 64), dtype=jnp.float32) * s, 'b_out': jax.random.normal(ks[6], (64,), dtype=jnp.float32) * s, 'edge_index': build_grid_edges()}
    _L0_tok_all = _L0_tok_setup()
    _L0_tok_in = {k: v for k, v in _L0_tok_all.items() if k in ('W_embed', 'b_embed', 'W_gcn', 'b_gcn', 'W_out', 'b_out', 'edge_index')}
    del _L0_tok_all

    def _L0_attn_setup():
        import math
        import jax, jax.numpy as jnp
        import numpy as np
        D_MODEL = 64
        N_HEADS = 4
        HEAD_DIM = D_MODEL // N_HEADS
        MAX_REL = 30

        def _rel_pos_encodings(t, d_model):
            n = 2 * MAX_REL + 1
            positions = jnp.arange(n, dtype=jnp.float32)[:, None]
            div_term = jnp.exp(jnp.arange(0, d_model, 2, dtype=jnp.float32) * (-math.log(10000.0) / d_model))
            ang = positions * div_term
            enc = jnp.stack([jnp.sin(ang), jnp.cos(ang)], axis=-1).reshape(n, d_model)
            rng = jnp.arange(t)
            final_mat = jnp.clip(rng[None, :] - rng[:, None], -MAX_REL, MAX_REL) + MAX_REL
            return enc[final_mat]
        key = jax.random.key(seed)
        ks = jax.random.split(key, 12)
        d = D_MODEL
        s = 1.0 / math.sqrt(d)
        inp = {'inputs': jax.random.normal(ks[0], (16, 128, d), dtype=jnp.float32), 'ln_gamma': jnp.ones((d,), jnp.float32), 'ln_beta': jnp.zeros((d,), jnp.float32), 'Wq': jax.random.normal(ks[1], (d, d), jnp.float32) * s, 'bq': jnp.zeros((d,), jnp.float32), 'Wk': jax.random.normal(ks[2], (d, d), jnp.float32) * s, 'bk': jnp.zeros((d,), jnp.float32), 'Wv': jax.random.normal(ks[3], (d, d), jnp.float32) * s, 'bv': jnp.zeros((d,), jnp.float32), 'Wpos': jax.random.normal(ks[4], (d, d), jnp.float32) * s, 'bpos': jnp.zeros((d,), jnp.float32), 'Wo': jax.random.normal(ks[5], (d, d), jnp.float32) * s, 'bo': jnp.zeros((d,), jnp.float32), 'u_bias': jax.random.normal(ks[6], (1, N_HEADS, 1, HEAD_DIM), jnp.float32) * 0.02, 'v_bias': jax.random.normal(ks[7], (1, N_HEADS, 1, HEAD_DIM), jnp.float32) * 0.02}
        return inp
    _L0_attn_all = _L0_attn_setup()
    _L0_attn_in = {k: v for k, v in _L0_attn_all.items() if k in ('ln_gamma', 'ln_beta', 'Wq', 'bq', 'Wk', 'bk', 'Wv', 'bv', 'Wpos', 'bpos', 'Wo', 'bo', 'u_bias', 'v_bias')}
    del _L0_attn_all

    def _L0_ffn_setup():
        import jax, jax.numpy as jnp
        import numpy as np
        B, S, D, E, H, K = (4, 1024, 64, 8, 128, 2)
        key = jax.random.key(seed)
        ks = jax.random.split(key, 6)
        x = jax.random.normal(ks[0], (B, S, D), jnp.float32)
        Wg = jax.random.normal(ks[1], (D, E), jnp.float32) * 0.02
        bg = jnp.zeros((E,), jnp.float32)
        W1 = jax.random.normal(ks[2], (E, D, H), jnp.float32) * 0.02
        b1 = jnp.zeros((E, H), jnp.float32)
        W2 = jax.random.normal(ks[3], (E, H, D), jnp.float32) * 0.02
        b2 = jnp.zeros((E, D), jnp.float32)
        return {'x': x, 'Wg': Wg, 'bg': bg, 'W1': W1, 'b1': b1, 'W2': W2, 'b2': b2}
    _L0_ffn_all = _L0_ffn_setup()
    _L0_ffn_in = {k: v for k, v in _L0_ffn_all.items() if k in ('Wg', 'bg', 'W1', 'b1', 'W2', 'b2')}
    del _L0_ffn_all
    return {'x': x, 'txt': txt, 'L0_tok_W_embed': _L0_tok_in['W_embed'], 'L0_tok_b_embed': _L0_tok_in['b_embed'], 'L0_tok_W_gcn': _L0_tok_in['W_gcn'], 'L0_tok_b_gcn': _L0_tok_in['b_gcn'], 'L0_tok_W_out': _L0_tok_in['W_out'], 'L0_tok_b_out': _L0_tok_in['b_out'], 'L0_tok_edge_index': _L0_tok_in['edge_index'], 'L0_attn_ln_gamma': _L0_attn_in['ln_gamma'], 'L0_attn_ln_beta': _L0_attn_in['ln_beta'], 'L0_attn_Wq': _L0_attn_in['Wq'], 'L0_attn_bq': _L0_attn_in['bq'], 'L0_attn_Wk': _L0_attn_in['Wk'], 'L0_attn_bk': _L0_attn_in['bk'], 'L0_attn_Wv': _L0_attn_in['Wv'], 'L0_attn_bv': _L0_attn_in['bv'], 'L0_attn_Wpos': _L0_attn_in['Wpos'], 'L0_attn_bpos': _L0_attn_in['bpos'], 'L0_attn_Wo': _L0_attn_in['Wo'], 'L0_attn_bo': _L0_attn_in['bo'], 'L0_attn_u_bias': _L0_attn_in['u_bias'], 'L0_attn_v_bias': _L0_attn_in['v_bias'], 'L0_ffn_Wg': _L0_ffn_in['Wg'], 'L0_ffn_bg': _L0_ffn_in['bg'], 'L0_ffn_W1': _L0_ffn_in['W1'], 'L0_ffn_b1': _L0_ffn_in['b1'], 'L0_ffn_W2': _L0_ffn_in['W2'], 'L0_ffn_b2': _L0_ffn_in['b2']}

def reference(x, txt, L0_tok_W_embed, L0_tok_b_embed, L0_tok_W_gcn, L0_tok_b_gcn, L0_tok_W_out, L0_tok_b_out, L0_tok_edge_index, L0_attn_ln_gamma, L0_attn_ln_beta, L0_attn_Wq, L0_attn_bq, L0_attn_Wk, L0_attn_bk, L0_attn_Wv, L0_attn_bv, L0_attn_Wpos, L0_attn_bpos, L0_attn_Wo, L0_attn_bo, L0_attn_u_bias, L0_attn_v_bias, L0_ffn_Wg, L0_ffn_bg, L0_ffn_W1, L0_ffn_b1, L0_ffn_W2, L0_ffn_b2):
    import jax
    import jax.numpy as jnp

    def _L0_tok_ref(x, W_embed, b_embed, W_gcn, b_gcn, W_out, b_out, edge_index):
        import jax, jax.numpy as jnp
        import numpy as np
        import math
        GRID = 28
        NUM_PATCHES = GRID * GRID
        PATCH = 8
        IN_CH = 3
        HIDDEN = 64
        BATCH = 64

        def build_grid_edges():
            edges = []
            for i in range(GRID):
                for j in range(GRID):
                    cur = i * GRID + j
                    if j < GRID - 1:
                        edges.append([cur, cur + 1])
                    if i < GRID - 1:
                        edges.append([cur, cur + GRID])
            e = np.asarray(edges, dtype=np.int32).T
            e = np.concatenate([e, e[::-1]], axis=1)
            return jnp.asarray(e)

        def sin_positional_encoding(n, d):
            pos = jnp.arange(n, dtype=jnp.float32)[:, None]
            div = jnp.exp(jnp.arange(0, d, 2, dtype=jnp.float32) * (-math.log(10000.0) / d))
            pe = jnp.zeros((n, d), dtype=jnp.float32)
            pe = pe.at[:, 0::2].set(jnp.sin(pos * div))
            pe = pe.at[:, 1::2].set(jnp.cos(pos * div))
            return pe
        B = x.shape[0]
        N = NUM_PATCHES
        p = x.reshape(B, IN_CH, GRID, PATCH, GRID, PATCH)
        p = p.transpose(0, 2, 4, 1, 3, 5).reshape(B, N, IN_CH * PATCH * PATCH)
        h = p @ W_embed + b_embed + sin_positional_encoding(N, HIDDEN)[None]
        src, dst = (edge_index[0], edge_index[1])
        deg = jnp.zeros((N,), dtype=h.dtype).at[dst].add(1.0) + 1.0
        dinv = deg ** (-0.5)
        enorm = (dinv[src] * dinv[dst])[None, :, None]
        snorm = (1.0 / deg)[None, :, None]
        for i in range(3):
            hw = h @ W_gcn[i]
            agg = hw * snorm
            agg = agg.at[:, dst].add(hw[:, src] * enorm)
            h = jax.nn.relu(agg + b_gcn[i])
        return h @ W_out + b_out

    def _L0_attn_ref(inputs, ln_gamma, ln_beta, Wq, bq, Wk, bk, Wv, bv, Wpos, bpos, Wo, bo, u_bias, v_bias):
        import math
        import jax, jax.numpy as jnp
        import numpy as np
        D_MODEL = 64
        N_HEADS = 4
        HEAD_DIM = D_MODEL // N_HEADS
        MAX_REL = 30

        def _rel_pos_encodings(t, d_model):
            n = 2 * MAX_REL + 1
            positions = jnp.arange(n, dtype=jnp.float32)[:, None]
            div_term = jnp.exp(jnp.arange(0, d_model, 2, dtype=jnp.float32) * (-math.log(10000.0) / d_model))
            ang = positions * div_term
            enc = jnp.stack([jnp.sin(ang), jnp.cos(ang)], axis=-1).reshape(n, d_model)
            rng = jnp.arange(t)
            final_mat = jnp.clip(rng[None, :] - rng[:, None], -MAX_REL, MAX_REL) + MAX_REL
            return enc[final_mat]
        b, t, d = inputs.shape
        h, hd = (N_HEADS, HEAD_DIM)
        mu = jnp.mean(inputs, axis=-1, keepdims=True)
        var = jnp.mean(jnp.square(inputs - mu), axis=-1, keepdims=True)
        x = (inputs - mu) * jax.lax.rsqrt(var + 1e-05) * ln_gamma + ln_beta

        def split_heads(y):
            return y.reshape(b, t, h, hd).transpose(0, 2, 1, 3)
        q = split_heads(x @ Wq.T + bq)
        k = split_heads(x @ Wk.T + bk)
        v = split_heads(x @ Wv.T + bv)
        rel = jax.lax.stop_gradient(_rel_pos_encodings(t, d))
        pos = (rel @ Wpos.T + bpos).reshape(t, t, h, hd)
        qk_score = jnp.einsum('bhtd,bhsd->bhts', q + u_bias, k)
        pos_score = jnp.einsum('bhtd,tshd->bhts', q + v_bias, pos)
        scores = (qk_score + pos_score) / math.sqrt(hd)
        attn = jax.nn.softmax(scores, axis=-1)
        ctx = jnp.einsum('bhts,bhsd->bhtd', attn, v)
        ctx = ctx.transpose(0, 2, 1, 3).reshape(b, t, d)
        return ctx @ Wo.T + bo

    def _L0_ffn_ref(x, Wg, bg, W1, b1, W2, b2):
        import jax, jax.numpy as jnp
        import numpy as np
        B, S, D, E, H, K = (4, 1024, 64, 8, 128, 2)
        Bv, Sv, Dv = x.shape
        gate_scores = x @ Wg + bg
        _, idx = jax.lax.top_k(gate_scores, K)
        mask = jax.nn.one_hot(idx, E, dtype=x.dtype).sum(axis=-2)
        xf = x.reshape(-1, Dv)
        mf = mask.reshape(-1, E)
        h = jax.nn.gelu(jnp.einsum('td,edh->teh', xf, W1) + b1[None], approximate=False)
        y = jnp.einsum('teh,ehd->ted', h, W2) + b2[None]
        out = jnp.einsum('ted,te->td', y, mf)
        return out.reshape(Bv, Sv, Dv)
    h = _L0_tok_ref(x, L0_tok_W_embed, L0_tok_b_embed, L0_tok_W_gcn, L0_tok_b_gcn, L0_tok_W_out, L0_tok_b_out, L0_tok_edge_index)
    h = jnp.concatenate([h, txt], axis=1)
    h = h + _L0_attn_ref(_layernorm(h, axis=-1), L0_attn_ln_gamma, L0_attn_ln_beta, L0_attn_Wq, L0_attn_bq, L0_attn_Wk, L0_attn_bk, L0_attn_Wv, L0_attn_bv, L0_attn_Wpos, L0_attn_bpos, L0_attn_Wo, L0_attn_bo, L0_attn_u_bias, L0_attn_v_bias)
    h = h + _L0_ffn_ref(_layernorm(h, axis=-1), L0_ffn_Wg, L0_ffn_bg, L0_ffn_W1, L0_ffn_b1, L0_ffn_W2, L0_ffn_b2)
    return h

_drawn_inputs = setup_inputs


def setup_inputs(seed=0):
    import zlib

    import numpy as np

    out = dict(_drawn_inputs(seed))
    spreads = {'L0_attn_ln_gamma': (1.0, 0.2),
     'L0_attn_ln_beta': (0.0, 0.1),
     'L0_attn_bq': (0.0, 0.1),
     'L0_attn_bk': (0.0, 0.8),
     'L0_attn_bv': (0.0, 0.1),
     'L0_attn_bpos': (0.0, 0.8),
     'L0_attn_bo': (0.0, 0.1),
     'L0_ffn_bg': (0.0, 0.1),
     'L0_ffn_b1': (0.0, 0.439),
     'L0_ffn_b2': (0.0, 0.1)}
    factors = {'x': 8.0,
     'L0_tok_W_embed': 8.0,
     'L0_tok_b_embed': 8.0,
     'L0_tok_W_gcn': 3.045,
     'L0_attn_u_bias': 5.497,
     'L0_attn_v_bias': 8.0}
    for name, (base, spread) in spreads.items():
        noise = np.random.default_rng([zlib.crc32(name.encode()), seed]).standard_normal(out[name].shape)
        drawn = base * np.exp(spread * noise) if base else spread * noise
        out[name] = jnp.asarray(drawn.astype(out[name].dtype))
    for name, factor in factors.items():
        out[name] = (out[name] * factor).astype(out[name].dtype)
    return out
```

```python
from contextlib import ExitStack

import concourse.bass as bass
import numpy as np
from concourse import mybir

F32 = mybir.dt.float32
F32R = mybir.dt.float32r
BF16 = mybir.dt.bfloat16
I32 = mybir.dt.int32
ACT = mybir.ActivationFunctionType
ALU = mybir.AluOpType
AX = mybir.AxisListType

GRID, PATCH, CH = 28, 8, 3
NODES = GRID * GRID
TXT = 128
T = NODES + TXT
D = 64
HEADS, HD = 4, 16
TP, TT = 114, 8
NP_, NT = 112, 7
NH = NODES // 2
TH = T // 2
KIN = CH * PATCH * PATCH
KP = KIN // 2
EC, EP = 24, 126
REL = 30
NR = 2 * REL + 1
BLK = TP // 2
NBLK = T // BLK
WIN = TP + 2 * REL
SROWS = 64 + 2 * NBLK
NE, HID = 8, 128
NPAIR = NE * (NE - 1) // 2
EPS = 1e-5
OFF = -float(2.0 ** 100)


def bcast(ap, shape):
    return ap.to_broadcast(shape)


def wait_apart(eng, semaphore, value, passed):
    eng.wait_ge(semaphore, value)
    eng.sem_inc(passed, 1)


def scratch_tensors(nc, NB):
    def dram(name, shape, dt):
        return nc.dram_tensor(name, shape, dt, kind="Internal").ap()

    return dict(
        tok=dram("tok", (NB, T, D), F32),
        xt=dram("xt", (NB + 1, D, T), F32),
        qst=dram("qst", (NB, SROWS, HEADS, T), F32),
        kst=dram("kst", (NB, 64, HEADS, T), F32),
        vst=dram("vst", (NB, TP, TT, D), F32),
        ring=dram("ring", (2, TP, HEADS, WIN), F32),
        tok2=dram("tok2", (NB, T, D), F32),
    )


class W:
    pass


def alloc_weights(nc, ctx):
    w = W()

    def sb(name, shape, dt=F32):
        return ctx.enter_context(nc.sbuf_tensor(name, shape, dt))

    w.ident = sb("ident", [128, 128])
    w.ones = sb("ones", [128, 1])
    w.adj = sb("adj", [NP_, NT, NODES], F32R)
    w.dinv = sb("dinv", [NP_, NT])
    w.invdeg = sb("invdeg", [NP_, NT])
    w.sq4 = sb("sq4", [4, NODES], F32R)
    w.bg4 = sb("bg4", [4, 3, 128], F32R)
    w.we = sb("we", [KP, 2, D])
    w.etab = sb("etab", [128, NODES])
    w.wg = sb("wg", [128, 4, 128])
    w.bout = sb("bout", [128, 128])
    w.lng = sb("lng", [D, 1])
    w.lnb = sb("lnb", [D, 1])
    w.wqk = sb("wqk", [D + 1, 128])
    w.wdp = sb("wdp", [D + 1, 64])
    w.wv = sb("wv", [D + 1, D])
    w.gpos = sb("gpos", [D + 1, HEADS, NR])
    w.blkmask = sb("blkmask", [64, T])
    w.step = sb("step", [96, T])
    w.bandstep = sb("bandstep", [TP, NR])
    w.wo = sb("wo", [128, D])
    w.w1a = sb("w1a", [128, NE, HID], F32R)
    w.w1b = sb("w1b", [104, NE, HID], F32R)
    w.wga = sb("wga", [128, 128], F32R)
    w.wgb = sb("wgb", [66, 128], F32R)
    w.rank = sb("rank", [NPAIR, NE], BF16)
    w.thr = sb("thr", [NE, 1])
    w.w2 = sb("w2", [HID, NE, D])
    w.b2 = sb("b2", [NE, 128], F32R)
    w.fold = sb("fold", [128, D])
    w.mhalf = sb("mhalf", [128, TT])
    return w


def prepare(nc, w, ins, s, NB):
    A = ins
    with ExitStack() as ctx:
        def sb(name, shape, dt=F32):
            return ctx.enter_context(nc.sbuf_tensor(name, shape, dt))

        def pb(name, shape=(128, 512)):
            return ctx.enter_context(nc.psum_tensor(name, list(shape), F32))

        def sem(name):
            return ctx.enter_context(nc.semaphore(name))

        eidx = sb("eidx", [EP, 2, EC], I32)
        eidf = sb("eidf", [EP, 2, EC])
        iota = sb("iota", [128, NODES])
        onehot = sb("onehot", [EP, 2, EC, NODES], BF16)
        eyeb = sb("eyeb", [NP_, NP_], BF16)
        shift = sb("shift", [NP_, NT, NODES], BF16)
        oneb = sb("oneb", [EP, 4], BF16)
        b128 = sb("b128", [128, 1])
        pe = sb("pe", [128, NODES])
        deg = sb("deg", [NP_, NT])
        sqr = sb("sqr", [4, NODES])
        sqh = sb("sqh", [4, NODES], F32R)
        sql = sb("sql", [4, NODES])
        half4 = sb("half4", [4, NODES])
        bgr = sb("bgr", [4, 3 * 128])
        bgh = sb("bgh", [4, 3 * 128], F32R)
        bgl = sb("bgl", [4, 3 * 128])
        rm = sb("rm", [4, 4])
        wpt = sb("wpt", [D + 1, D])
        relt = sb("relt", [D + 1, NR])
        hm = sb("hm", [D, HEADS])
        pos = sb("pos", [D, NR])
        posd = sb("posd", [D, HEADS, NR])
        wqn = sb("wqn", [D, D + 1])
        vb = sb("vb", [D, 1])
        qb = sb("qb", [D + 1, 3, D])
        w1f = sb("w1f", [128, NE, HID])
        b1r = sb("b1r", [96 + NE, NE, HID])
        gw = sb("gw", [128, NE])
        gbr = sb("gbr", [66, NE])
        gd = sb("gd", [128, 128])
        b2f = sb("b2f", [NE, 2, D])
        zero = sb("zero", [TP, HEADS * T])

        psc = [pb(f"psc{i}") for i in range(2)]
        psd = pb("psd")
        psq = [pb(f"psq{i}") for i in range(2)]
        psp = pb("psp")

        loaded = sem("loaded")
        edges_loaded = sem("edges_loaded")
        cleared = sem("cleared")
        zeroed = sem("zeroed")
        onehots = sem("onehots")
        counts_ready = sem("counts_ready")
        counts_taken = sem("counts_taken")
        deg_ready = sem("deg_ready")
        pos_ready = sem("pos_ready")
        posd_ready = sem("posd_ready")
        gpos_ready = sem("gpos_ready")
        degree_taken = sem("degree_taken")
        powered = sem("powered")
        dchain = sem("dchain")

        loads = [
            (w.ident[:, :], A["c_ident"]), (w.we[:, :, :], A["w_embed"].rearrange("(k p) n -> p k n", k=2)),
            (pe[:, :], A["c_pe"]), (b128[0:64, :], A["b_embed"].rearrange("(p a) -> p a", a=1)),
            (b128[64:128, :], A["b_embed"].rearrange("(p a) -> p a", a=1)),
            (w.lng[:, :], A["ln_gamma"].rearrange("(p a) -> p a", a=1)),
            (w.lnb[:, :], A["ln_beta"].rearrange("(p a) -> p a", a=1)),
            (w.wqk[0:D, 0:D], A["wq_t"]), (w.wqk[0:D, D:128], A["wk_t"]), (w.wv[0:D, :], A["wv_t"]),
            (w.wqk[D:D + 1, D:128], A["bk"].rearrange("(a n) -> a n", a=1)),
            (w.wv[D:D + 1, :], A["bv"].rearrange("(a n) -> a n", a=1)),
            (qb[D:D + 1, 0, :], A["bq_perm"].rearrange("(a n) -> a n", a=1)),
            (qb[D:D + 1, 1, :], A["u_perm"].rearrange("(a n) -> a n", a=1)),
            (w.blkmask[:, :], A["c_blkmask"]), (w.step[64:96, :], A["c_step"]), (w.bandstep[:, :], A["c_bandstep"]),
            (wpt[0:D, :], A["wpos_t"]), (wpt[D:D + 1, :], A["bpos"].rearrange("(a n) -> a n", a=1)),
            (relt[:, :], A["c_rel"]), (hm[:, :], A["c_headmask"]),
            (wqn[:, 0:D], A["wq"]), (wqn[:, D:D + 1], A["bq"].rearrange("(p a) -> p a", a=1)),
            (vb[:, :], A["v_bias"].rearrange("a h b d -> (a h b d)").rearrange("(p a) -> p a", a=1)),
            (w1f[0:D, :, :], A["w1"].rearrange("e d h -> d e h")), (w1f[D:128, :, :], A["w1"].rearrange("e d h -> d e h")),
            (b1r[64:65, :, :], A["b1"].rearrange("(a e) h -> a e h", a=1)),
            (b1r[96:96 + NE, :, :], A["c_off"].rearrange("p (e h) -> p e h", e=NE)),
            (gw[0:D, :], A["wg"]), (gw[D:128, :], A["wg"]), (gbr[64:65, :], A["bg"].rearrange("(a n) -> a n", a=1)),
            (w.thr[:, :], A["c_thr"]), (w.w2[:, :, :], A["w2"].rearrange("e h d -> h e d")),
            (b2f[:, 0, :], A["b2"]), (b2f[:, 1, :], A["b2"]), (w.fold[:, :], A["c_fold"]),
            (rm[:, :], A["c_rows4"]), (gd[0:NPAIR, 0:NE], A["c_rank"]),
        ]
        for l in range(3):
            loads += [(w.wg[64 * q:64 * q + 64, l, 64 * q:64 * q + 64], A["w_gcn"][l]) for q in range(2)]
            loads += [(bgr[:, l * 128 + 64 * q:l * 128 + 64 * q + 64], A["b_gcn"][l:l + 1, :].to_broadcast([4, D])) for q in range(2)]
        loads += [(w.wg[64 * q:64 * q + 64, 3, 64 * q:64 * q + 64], A["w_out"]) for q in range(2)]
        loads += [(w.bout[:, 64 * q:64 * q + 64], A["b_out"].rearrange("(a n) -> a n", a=1).to_broadcast([128, D])) for q in range(2)]
        loads += [(w.wo[32 * h:32 * h + HD, :], A["wo_t"][HD * h:HD * h + HD, :]) for h in range(HEADS)]
        loads += [(w.wo[112:113, :], A["bo"].rearrange("(a n) -> a n", a=1))]
        ALL = 16 * len(loads)

        with nc.Block() as block:
            @block.sync
            def _(sp):
                sp.dma_start(eidx[:, :, :], A["edge_index"].rearrange("a (p c) -> p a c", c=EC)).then_inc(edges_loaded, 16)
                sp.dma_start(iota[:, :], A["c_iota"]).then_inc(edges_loaded, 16)
                sp.dma_start(shift[:, :, :], A["c_shift"].rearrange("p (i n) -> p i n", i=NT)).then_inc(edges_loaded, 16)
                sp.wait_ge(cleared, 4)
                for dst, src in loads:
                    sp.dma_start(dst, src).then_inc(loaded, 16)
                sp.dma_start(s["tok"][:, NODES:T, :], A["txt"]).then_inc(zeroed, 16)
                sp.dma_start(s["ring"][0], zero[:, 0:HEADS * WIN].rearrange("p (h c) -> p h c", h=HEADS)).then_inc(zeroed, 16)
                sp.dma_start(s["ring"][1], zero[:, 0:HEADS * WIN].rearrange("p (h c) -> p h c", h=HEADS)).then_inc(zeroed, 16)
                sp.dma_start(s["xt"][NB], zero[0:D, 0:T]).then_inc(zeroed, 16)
                sp.wait_ge(zeroed, 64)
                sp.wait_ge(loaded, ALL)

            @block.gpsimd
            def _(pool):
                nc.gpsimd.memset(w.wg[:, :, :], 0.0).then_inc(cleared, 1)
                nc.gpsimd.memset(w.wo[:, :], 0.0).then_inc(cleared, 1)
                nc.gpsimd.memset(zero[:, :], 0.0).then_inc(cleared, 1)
                nc.gpsimd.memset(b1r[:, :, :], 0.0).then_inc(cleared, 1)
                nc.gpsimd.memset(w.mhalf[:, :], -0.5)
                nc.gpsimd.memset(half4[:, :], 0.5).then_inc(degree_taken, 1)
                pool.wait_ge(degree_taken, 3)
                nc.gpsimd.tensor_tensor(w.dinv[:, :], deg[:, :], w.mhalf[0:NP_, 0:NT], ALU.pow).then_inc(powered, 1)
                nc.gpsimd.tensor_tensor(sqr[:, :], sql[:, :], half4[:, :], ALU.pow).then_inc(powered, 1)

            @block.tensor
            def _(pe_):
                pe_.wait_ge(loaded, ALL)
                nc.tensor.matmul(psp[0:D, 0:NR], wpt[:, :], relt[:, :], start=True, stop=True).then_inc(pos_ready, 1)
                pe_.wait_ge(posd_ready, 1)
                nc.tensor.matmul(psp[0:D + 1, 64:64 + HEADS * NR], wqn[:, :], posd[:, :, :], start=True, stop=True).then_inc(gpos_ready, 1)
                pe_.wait_ge(edges_loaded, 48)
                pe_.wait_ge(onehots, 2 * EC + 1)
                for i in range(NT):
                    for c in range(EC):
                        mm = nc.tensor.matmul(psd[0:NP_, 4 * i:4 * i + 4], onehot[:, 1, c, i * NP_:(i + 1) * NP_], oneb[:, :],
                                              start=(i == 0 and c == 0), stop=(c == EC - 1), skip_group_check=True)
                mm.then_inc(deg_ready, 1)
                for a in range(2):
                    for c in range(EC):
                        mm = nc.tensor.matmul(psq[a][0:4, 0:NH], oneb[:, :], onehot[:, 1, c, a * NH:(a + 1) * NH],
                                              start=(c == 0), stop=(c == EC - 1))
                    mm.then_inc(deg_ready, 1)
                for i in range(NT):
                    for a in range(2):
                        m = 2 * i + a
                        if m >= 2:
                            pe_.wait_ge(counts_taken, m - 1)
                        for c in range(EC):
                            nc.tensor.matmul(psc[a][0:NP_, 0:NH], onehot[:, 0, c, i * NP_:(i + 1) * NP_],
                                             onehot[:, 1, c, a * NH:(a + 1) * NH], start=(c == 0), stop=False)
                        nc.tensor.matmul(psc[a][0:NP_, 0:NH], shift[:, i, i * NP_:(i + 1) * NP_],
                                         shift[:, i, a * NH:(a + 1) * NH], start=False, stop=True).then_inc(counts_ready, 1)

            @block.scalar
            def _(act):
                for m in range(2 * NT):
                    i, a = divmod(m, 2)
                    act.wait_ge(counts_ready, m + 1)
                    nc.scalar.activation(w.adj[:, i, a * NH:(a + 1) * NH], psc[a][0:NP_, 0:NH], ACT.Copy).then_inc(counts_taken, 1)

            @block.vector
            def _(dve):
                n = [0]

                def link(ins):
                    n[0] += 1
                    ins.then_inc(dchain, 1)
                    dve.wait_ge(dchain, n[0])

                v = nc.vector
                v.memset(oneb[:, :], 1.0)
                v.memset(w.ones[:, :], 1.0).then_inc(onehots, 1)
                dve.wait_ge(edges_loaded, 48)
                link(v.tensor_copy(eidf[:, :, :], eidx[:, :, :]))
                for c in range(EC):
                    for e in range(2):
                        v.tensor_scalar(onehot[:, e, c, :], iota[0:EP, :], eidf[:, e, c:c + 1], None, ALU.is_equal).then_inc(onehots, 1)
                dve.wait_ge(loaded, ALL)
                dve.wait_ge(pos_ready, 1)
                link(v.tensor_copy(pos[:, :], psp[0:D, 0:NR]))
                link(v.tensor_scalar(pos[:, :], pos[:, :], pos[:, NR - 1:NR], None, ALU.subtract))
                link(v.tensor_tensor(wqn[:, D:D + 1], wqn[:, D:D + 1], vb[:, :], ALU.add))
                for h in range(HEADS):
                    last = v.tensor_scalar(posd[:, h, :], pos[:, :], hm[:, h:h + 1], 0.25, ALU.mult, ALU.mult)
                last.then_inc(posd_ready, 1)
                link(v.tensor_tensor(qb[D:D + 1, 2, :], qb[D:D + 1, 0, :], qb[D:D + 1, 1, :], ALU.add))
                link(v.tensor_copy(w.wqk[D:D + 1, 0:D], qb[D:D + 1, 2, :]))
                link(v.tensor_scalar(w.wqk[:, 0:D], w.wqk[:, 0:D], 0.25, None, ALU.mult))
                dve.wait_ge(gpos_ready, 1)
                link(v.tensor_copy(w.gpos[:, :, :], psp[0:D + 1, 64:64 + HEADS * NR].rearrange("p (h r) -> p h r", h=HEADS)))
                v.tensor_copy(w.wdp[:, :].rearrange("p (k h) -> p k h", h=HEADS),
                              w.gpos[:, :, 0].rearrange("p (k h) -> p k h", k=1).to_broadcast([D + 1, NBLK, HEADS]))
                v.tensor_scalar(w.etab[:, :], pe[:, :], b128[:, 0:1], None, ALU.add)
                dve.wait_ge(deg_ready, 3)
                v.tensor_scalar(deg[:, :], psd[0:NP_, 0:4 * NT].rearrange("p (i k) -> p i k", k=4)[:, :, 0], 1.0, None, ALU.add).then_inc(degree_taken, 1)
                v.tensor_scalar(sql[:, 0:NH], psq[0][0:4, 0:NH], 1.0, None, ALU.add)
                v.tensor_scalar(sql[:, NH:NODES], psq[1][0:4, 0:NH], 1.0, None, ALU.add).then_inc(degree_taken, 1)
                dve.wait_ge(degree_taken, 3)
                v.reciprocal(w.invdeg[:, :], deg[:, :])
                dve.wait_ge(powered, 2)
                link(v.tensor_copy(sqh[:, :], sqr[:, :]))
                link(v.tensor_tensor(sql[:, :], sqr[:, :], sqh[:, :].bitcast(F32), ALU.subtract))
                link(v.tensor_scalar(sql[:, :], sql[:, :], rm[:, 1:2], None, ALU.mult))
                v.scalar_tensor_tensor(out=w.sq4[:, :], in0=sqh[:, :].bitcast(F32), scalar=rm[:, 0:1], in1=sql[:, :], op0=ALU.mult, op1=ALU.add)
                link(v.tensor_copy(bgh[:, :], bgr[:, :]))
                link(v.tensor_tensor(bgl[:, :], bgr[:, :], bgh[:, :].bitcast(F32), ALU.subtract))
                link(v.tensor_scalar(bgl[:, :], bgl[:, :], rm[:, 3:4], None, ALU.mult))
                v.scalar_tensor_tensor(out=w.bg4[:, :, :].rearrange("p l n -> p (l n)"), in0=bgh[:, :].bitcast(F32), scalar=rm[:, 2:3], in1=bgl[:, :], op0=ALU.mult, op1=ALU.add)
                link(v.tensor_copy(w.w1a[:, :, :], w1f[:, :, :]))
                link(v.memset(w.w1b[:, :, :].bitcast(F32), 0.0))
                v.tensor_tensor(w.w1b[0:D, :, :], w1f[0:D, :, :], w.w1a[0:D, :, :].bitcast(F32), ALU.subtract)
                v.tensor_copy(w.w1b[96:96 + NE, :, :], b1r[96:96 + NE, :, :])
                link(v.tensor_copy(w.w1b[D:D + 1, :, :], b1r[64:65, :, :]))
                link(v.tensor_tensor(b1r[64:65, :, :], b1r[64:65, :, :], w.w1b[D:D + 1, :, :].bitcast(F32), ALU.subtract))
                link(v.tensor_copy(w.rank[:, :], gd[0:NPAIR, 0:NE]))
                link(v.memset(gd[:, :], 0.0))
                m = 0
                for a in range(NE - 1):
                    k = NE - 1 - a
                    v.tensor_scalar(gd[:, m:m + k], gw[:, a + 1:NE], gw[:, a:a + 1], -1.0, ALU.subtract, ALU.mult)
                    m += k
                link(v.memset(w.wgb[:, :].bitcast(F32), 0.0))
                link(v.tensor_copy(w.wga[:, :], gd[:, :]))
                link(v.tensor_tensor(w.wgb[0:D, :], gd[0:D, :], w.wga[0:D, :].bitcast(F32), ALU.subtract))
                m = 0
                for a in range(NE - 1):
                    k = NE - 1 - a
                    link(v.tensor_scalar(gd[64:65, m:m + k], gbr[64:65, a + 1:NE], gbr[64:65, a:a + 1], -1.0, ALU.subtract, ALU.mult))
                    m += k
                link(v.tensor_copy(w.wgb[64:65, 0:NPAIR], gd[64:65, 0:NPAIR]))
                link(v.tensor_tensor(gd[64:65, 0:NPAIR], gd[64:65, 0:NPAIR], w.wgb[64:65, 0:NPAIR].bitcast(F32), ALU.subtract))
                v.tensor_copy(w.b2[:, 0:D], b2f[:, 0, :])
                link(v.tensor_copy(w.b2[:, D:128], b2f[:, 1, :]))
                link(v.tensor_tensor(w.b2[:, D:128], b2f[:, 1, :], w.b2[:, 0:D].bitcast(F32), ALU.subtract))

        with nc.Block() as block:
            lob = ctx.enter_context(nc.sbuf_tensor("lob", [66, NE * HID + 128], F32R))
            moved = sem("moved")
            rounded = sem("rounded")

            @block.vector
            def _(dve):
                nc.vector.tensor_copy(lob[64:65, 0:NE * HID], b1r[64:65, :, :].rearrange("p e h -> p (e h)"))
                nc.vector.tensor_copy(lob[64:65, NE * HID:NE * HID + NPAIR], gd[64:65, 0:NPAIR]).then_inc(rounded, 1)

            @block.sync
            def _(sp):
                sp.wait_ge(rounded, 1)
                sp.dma_start(w.w1b[65:66, :, :].rearrange("p e h -> p (e h)").bitcast(F32), lob[64:65, 0:NE * HID].bitcast(F32)).then_inc(moved, 16)
                sp.dma_start(w.wgb[65:66, 0:NPAIR].bitcast(F32), lob[64:65, NE * HID:NE * HID + NPAIR].bitcast(F32)).then_inc(moved, 16)
                sp.wait_ge(moved, 32)


def tokens(nc, w, ins, s, NB):
    xp = ins["x_patch"]
    with ExitStack() as ctx:
        def sb(name, shape, dt=F32):
            return ctx.enter_context(nc.sbuf_tensor(name, shape, dt))

        def sem(name):
            return ctx.enter_context(nc.semaphore(name))

        passed = sem("tokens_passed")

        px = [sb(f"px{q}", [KP, 2, 2, NODES]) for q in range(2)]
        r = [sb(f"r{q}", [128, NODES]) for q in range(2)]
        g = [sb(f"g{q}", [NP_, NT, 128]) for q in range(2)]
        ghi = [sb(f"ghi{q}", [NP_, NT, 128], F32R) for q in range(2)]
        glo = [sb(f"glo{q}", [NP_, NT, 128], F32R) for q in range(2)]
        ot = [sb(f"ot{q}", [NP_, NT, 128]) for q in range(2)]
        feat = [ctx.enter_context(nc.psum_tensor(f"feat{q}", [128, 2, 512], F32)) for q in range(2)]
        node = [ctx.enter_context(nc.psum_tensor(f"node{q}", [128, 2 * 512], F32)) for q in range(2)]
        px_loaded = [sem(f"px_loaded{q}") for q in range(2)]
        embedded = [sem(f"embedded{q}") for q in range(2)]
        r_ready = [sem(f"r_ready{q}") for q in range(2)]
        node_ready = [sem(f"node_ready{q}") for q in range(2)]
        g_ready = [sem(f"g_ready{q}") for q in range(2)]
        ghi_ready = [sem(f"ghi_ready{q}") for q in range(2)]
        glo_ready = [sem(f"glo_ready{q}") for q in range(2)]
        agg_ready = [sem(f"agg_ready{q}") for q in range(2)]
        out_scaled = [sem(f"out_scaled{q}") for q in range(2)]
        out_ready = [sem(f"out_ready{q}") for q in range(2)]
        stored = [sem(f"tok_stored{q}") for q in range(2)]
        LOOPS = NB // 4

        with nc.Block() as block:
            @block.sync
            def _(sp):
                with sp.Fori(0, LOOPS) as m:
                    for q in range(2):
                        sp.wait_ge(embedded[q], m)
                        sp.dma_start(px[q][:, :, :, :], xp[:, bass.ds(4 * m + 2 * q, 2), :, :]).then_inc(px_loaded[q], 16)

            @block.tensor
            def _(pe):
                with pe.Fori(0, LOOPS) as m:
                    for q in range(2):
                        pe.wait_ge(px_loaded[q], 16 * (m + 1))
                        pe.wait_ge(r_ready[q], 4 * m)
                        for a in range(2):
                            for k in range(2):
                                for e in range(2):
                                    mm = nc.tensor.matmul(feat[q][64 * e:64 * e + 64, a, 0:NH], w.we[:, k, :],
                                                          px[q][:, e, k, a * NH:(a + 1) * NH], start=(k == 0), stop=(k == 1))
                        mm.then_inc(embedded[q], 1)
                    for l in range(4):
                        for q in range(2):
                            pe.wait_ge(r_ready[q], 4 * m + l + 1)
                            if l:
                                pe.wait_ge(g_ready[q], 3 * m + l)
                            else:
                                pe.wait_ge(out_scaled[q], m)
                            for i in range(NT):
                                mm = nc.tensor.matmul(node[q][0:NP_, i * 128:(i + 1) * 128], r[q][:, i * NP_:(i + 1) * NP_],
                                                      w.wg[:, l, :], start=True, stop=True)
                            mm.then_inc(node_ready[q], 1)
                        if l == 3:
                            continue
                        for q in range(2):
                            pe.wait_ge(ghi_ready[q], 3 * m + l + 1)
                            pe.wait_ge(glo_ready[q], 3 * m + l + 1)
                            for a in range(2):
                                out = feat[q][:, a, 0:NH]
                                nc.tensor.matmul(out, w.bg4[:, l, :], w.sq4[:, a * NH:(a + 1) * NH], start=True, stop=False)
                                for i in range(NT):
                                    nc.tensor.matmul(out, ghi[q][:, i, :], w.adj[:, i, a * NH:(a + 1) * NH], start=False, stop=False)
                                    mm = nc.tensor.matmul(out, glo[q][:, i, :], w.adj[:, i, a * NH:(a + 1) * NH],
                                                          start=False, stop=(i == NT - 1))
                            mm.then_inc(agg_ready[q], 1)

            @block.vector
            def _(dve):
                with dve.Fori(0, LOOPS) as m:
                    for q in range(2):
                        dve.wait_ge(embedded[q], m + 1)
                        dve.wait_ge(node_ready[q], 4 * m)
                        nc.vector.tensor_tensor(r[q][:, :].rearrange("p (a n) -> p a n", a=2), feat[q][:, :, 0:NH],
                                                w.etab[:, :].rearrange("p (a n) -> p a n", a=2), ALU.add).then_inc(r_ready[q], 1)
                    for l in range(4):
                        for q in range(2):
                            dve.wait_ge(node_ready[q], 4 * m + l + 1)
                            src = node[q][0:NP_, 0:NT * 128].rearrange("p (i n) -> p i n", i=NT)
                            if l < 3:
                                scale = w.invdeg if l else w.dinv
                                dve.wait_ge(glo_ready[q], 3 * m + l)
                                nc.vector.tensor_tensor(g[q][:, :, :], src, scale[:, :].rearrange("p (i a) -> p i a", a=1)
                                                        .to_broadcast([NP_, NT, 128]), ALU.mult).then_inc(g_ready[q], 1)
                            else:
                                dve.wait_ge(stored[q], 32 * m)
                                nc.vector.tensor_tensor(ot[q][:, :, :], src, w.dinv[:, :].rearrange("p (i a) -> p i a", a=1)
                                                        .to_broadcast([NP_, NT, 128]), ALU.mult).then_inc(out_scaled[q], 1)

            @block.scalar
            def _(act):
                with act.Fori(0, LOOPS) as m:
                    for l in range(3):
                        for q in range(2):
                            act.wait_ge(g_ready[q], 3 * m + l + 1)
                            act.wait_ge(agg_ready[q], 3 * m + l)
                            nc.scalar.activation(ghi[q][:, :, :], g[q][:, :, :], ACT.Copy).then_inc(ghi_ready[q], 1)
                        for q in range(2):
                            act.wait_ge(agg_ready[q], 3 * m + l + 1)
                            nc.scalar.activation(r[q][:, :].rearrange("p (a n) -> p a n", a=2), feat[q][:, :, 0:NH],
                                                 ACT.Relu).then_inc(r_ready[q], 1)

            @block.gpsimd
            def _(pool):
                with pool.Fori(0, LOOPS) as m:
                    for l in range(3):
                        for q in range(2):
                            wait_apart(pool, ghi_ready[q], 3 * m + l + 1, passed)
                            nc.gpsimd.tensor_tensor(glo[q][:, :, :], g[q][:, :, :], ghi[q][:, :, :].bitcast(F32),
                                                    ALU.subtract).then_inc(glo_ready[q], 1)
                    for q in range(2):
                        wait_apart(pool, out_scaled[q], m + 1, passed)
                        nc.gpsimd.tensor_tensor(ot[q][:, :, :], ot[q][:, :, :], w.bout[0:NP_, :].rearrange("p (a n) -> p a n", a=1)
                                                .to_broadcast([NP_, NT, 128]), ALU.add).then_inc(out_ready[q], 1)
                    for q in range(2):
                        wait_apart(pool, out_ready[q], m + 1, passed)
                        for e in range(2):
                            pool.dma_start(s["tok"][bass.ds(4 * m + 2 * q + e, 1), 0:NODES, :].rearrange("b (i p) f -> p (b i) f", p=NP_),
                                           ot[q][:, :, 64 * e:64 * e + 64]).then_inc(stored[q], 16)
                for q in range(2):
                    pool.wait_ge(stored[q], 32 * LOOPS)


def layer_norm(nc, dve, pool, link, x, xc, sq, st, w, n, base, k, y, ydup=1):
    v = nc.vector
    link(v.tensor_reduce(st[:, 0, :], x, AX.X, ALU.add))
    link(v.tensor_scalar(st[:, 1, :], st[:, 0, :], -1.0 / D, None, ALU.mult))
    link(v.tensor_tensor(xc, x, st[:, 1, :].rearrange("p (n a) -> p n a", a=1).to_broadcast([TP, n, D]), ALU.add))
    link(v.tensor_tensor(sq, xc, xc, ALU.mult))
    v.tensor_reduce(st[:, 2, :], sq, AX.X, ALU.add).then_inc(base, 1)
    dve.wait_ge(pool, k)
    rstd = st[:, 3, :].rearrange("p (n a) -> p n a", a=1)
    return v.tensor_tensor(y, xc, rstd.to_broadcast([TP, n, D]), ALU.mult)


def project(nc, w, s, NB):
    with ExitStack() as ctx:
        def sb(name, shape, dt=F32):
            return ctx.enter_context(nc.sbuf_tensor(name, shape, dt))

        def sem(name):
            return ctx.enter_context(nc.semaphore(name))

        passed = sem("project_passed")

        x = [sb(f"px_{q}", [TP, TT, D]) for q in range(2)]
        xc = sb("xc", [TP, TT, D])
        sq = sb("sqx", [TP, TT, D])
        y1 = sb("y1", [TP, TT, D])
        y2 = [sb(f"y2_{q}", [TP, TT, D]) for q in range(2)]
        st = sb("stats", [TP, 5, TT])
        xt = [sb(f"xt{q}", [D + 1, T]) for q in range(2)]
        qkhi = [sb(f"qkhi{q}", [128, T], F32R) for q in range(2)]
        qklo = [sb(f"qklo{q}", [128, T], F32R) for q in range(2)]
        dpm = [sb(f"dpm{q}", [64, T]) for q in range(2)]
        dphi = [sb(f"dphi{q}", [64, T], F32R) for q in range(2)]
        dplo = [sb(f"dplo{q}", [64, T], F32R) for q in range(2)]
        vv = [sb(f"vv{q}", [TP, TT, D]) for q in range(2)]
        psx = ctx.enter_context(nc.psum_tensor("psx", [128, 2, 512], F32))
        psqk = ctx.enter_context(nc.psum_tensor("psqk", [128, 2, 512], F32))
        psdp = ctx.enter_context(nc.psum_tensor("psdp", [128, 2, 512], F32))
        psv = ctx.enter_context(nc.psum_tensor("psv", [128, 512], F32))
        x_loaded = [sem(f"x_loaded{q}") for q in range(2)]
        x_used = sem("x_used")
        ones_set = sem("ones_set")
        sums = sem("sums")
        rstds = sem("rstds")
        vars_ = sem("vars_")
        y_ready = sem("y_ready")
        yt_ready = sem("yt_ready")
        xt_ready = sem("xt_ready")
        qk_ready = sem("qk_ready")
        dp_ready = sem("dp_ready")
        v_ready = sem("v_ready")
        qkhi_ready = sem("qkhi_ready")
        qklo_ready = sem("qklo_ready")
        v_taken = sem("v_taken")
        dpm_ready = sem("dpm_ready")
        dphi_ready = sem("dphi_ready")
        dplo_ready = sem("dplo_ready")
        saved = [sem(f"saved{q}") for q in range(2)]
        chain = sem("chainp")
        NSAVE = 12
        NLINK = 8

        def two(ap):
            return ap.rearrange("p (a n) -> p a n", a=2)

        with nc.Block() as block:
            @block.sync
            def _(sp):
                with sp.Fori(0, NB // 2) as m:
                    for q in range(2):
                        b = 2 * m + q
                        sp.wait_ge(x_used, 2 * m)
                        sp.dma_start(x[q][:, :, :], s["tok"][bass.ds(b, 1)].rearrange("b (j p) f -> p (b j) f", p=TP)).then_inc(x_loaded[q], 16)
                    for q in range(2):
                        b = 2 * m + q
                        sv = saved[q]

                        def rows(name, r0, n):
                            return s[name][bass.ds(b, 1), r0:r0 + n].rearrange("b r h t -> (b r h) t")

                        sp.wait_ge(xt_ready, b + 1)
                        sp.dma_start(s["xt"][bass.ds(b, 1)].rearrange("b f t -> (b f) t"), xt[q][0:D, :]).then_inc(sv, 16)
                        sp.wait_ge(qkhi_ready, b + 1)
                        for g_ in (0, 1):
                            sp.dma_start(rows("qst", 16 * g_, 16), qkhi[q][0:64, :].bitcast(F32)).then_inc(sv, 16)
                        for g_ in (0, 2):
                            sp.dma_start(rows("kst", 16 * g_, 16), qkhi[q][64:128, :].bitcast(F32)).then_inc(sv, 16)
                        sp.wait_ge(qklo_ready, b + 1)
                        for g_ in (2, 3):
                            sp.dma_start(rows("qst", 16 * g_, 16), qklo[q][0:64, :].bitcast(F32)).then_inc(sv, 16)
                        for g_ in (1, 3):
                            sp.dma_start(rows("kst", 16 * g_, 16), qklo[q][64:128, :].bitcast(F32)).then_inc(sv, 16)
                        sp.wait_ge(v_taken, b + 1)
                        sp.dma_start(s["vst"][bass.ds(b, 1)].rearrange("b p j f -> p (b j) f"), vv[q][:, :, :]).then_inc(sv, 16)
                        sp.wait_ge(dphi_ready, b + 1)
                        sp.dma_start(rows("qst", 64, NBLK), dphi[q][:, :].bitcast(F32)).then_inc(sv, 16)
                        sp.wait_ge(dplo_ready, b + 1)
                        sp.dma_start(rows("qst", 64 + NBLK, NBLK), dplo[q][:, :].bitcast(F32)).then_inc(sv, 16)
                for q in range(2):
                    sp.wait_ge(saved[q], 16 * NSAVE * (NB // 2))

            @block.vector
            def _(dve):
                v = nc.vector
                v.memset(xt[0][D:D + 1, :], 1.0)
                v.memset(xt[1][D:D + 1, :], 1.0).then_inc(ones_set, 1)
                with dve.Fori(0, NB // 2) as m:
                    for q in range(2):
                        b = 2 * m + q
                        n = [0]

                        def link(ins):
                            n[0] += 1
                            ins.then_inc(chain, 1)
                            dve.wait_ge(chain, b * NLINK + n[0])

                        dve.wait_ge(x_loaded[q], 16 * (m + 1))
                        layer_norm(nc, dve, rstds, link, x[q][:, :, :], xc[:, :, :], sq[:, :, :], st, w, TT, sums, 2 * b + 1,
                                   y1[:, :, :]).then_inc(x_used, 1)
                        dve.wait_ge(x_used, b + 1)
                        dve.wait_ge(yt_ready, 2 * m)
                        layer_norm(nc, dve, rstds, link, y1[:, :, :], xc[:, :, :], sq[:, :, :], st, w, TT, sums, 2 * b + 2,
                                   y2[q][:, :, :]).then_inc(y_ready, 1)
                        dve.wait_ge(y_ready, b + 1)
                        assert n[0] == NLINK
                        dve.wait_ge(saved[q], 16 * NSAVE * m)
                        dve.wait_ge(qkhi_ready, b + 1)
                        v.tensor_tensor(two(qklo[q][:, :]), psqk[:, :, 0:TH], two(qkhi[q][:, :].bitcast(F32)), ALU.subtract).then_inc(qklo_ready, 1)
                        dve.wait_ge(dp_ready, b + 1)
                        v.tensor_tensor(two(dpm[q][:, :]), psdp[0:64, :, 0:TH], two(w.blkmask[:, :]), ALU.mult).then_inc(dpm_ready, 1)

            @block.gpsimd
            def _(pool):
                with pool.Fori(0, NB // 2) as m:
                    for q in range(2):
                        b = 2 * m + q
                        for k in range(2):
                            wait_apart(pool, sums, 2 * b + k + 1, passed)
                            nc.gpsimd.tensor_scalar(st[:, 4, :], st[:, 2, :], 1.0 / D, EPS, ALU.mult, ALU.add).then_inc(vars_, 1)
                            wait_apart(pool, vars_, 2 * b + k + 1, passed)
                            nc.gpsimd.tensor_tensor(st[:, 3, :], st[:, 4, :], w.mhalf[0:TP, :], ALU.pow).then_inc(rstds, 1)
                        wait_apart(pool, dphi_ready, b + 1, passed)
                        nc.gpsimd.tensor_tensor(dplo[q][:, :], dpm[q][:, :], dphi[q][:, :].bitcast(F32), ALU.subtract).then_inc(dplo_ready, 1)

            @block.scalar
            def _(act):
                with act.Fori(0, NB // 2) as m:
                    for q in range(2):
                        b = 2 * m + q
                        act.wait_ge(saved[q], 16 * NSAVE * m)
                        act.wait_ge(yt_ready, b + 1)
                        nc.scalar.activation(two(xt[q][0:D, :]), psx[0:D, :, 0:TH], ACT.Identity, bias=w.lnb[:, 0:1],
                                             scale=w.lng[:, 0:1]).then_inc(xt_ready, 1)
                        act.wait_ge(qk_ready, b + 1)
                        nc.scalar.activation(two(qkhi[q][:, :]), psqk[:, :, 0:TH], ACT.Copy).then_inc(qkhi_ready, 1)
                        act.wait_ge(v_ready, b + 1)
                        nc.scalar.activation(vv[q][:, :, :].rearrange("p j f -> p (j f)"), psv[0:TP, :], ACT.Copy).then_inc(v_taken, 1)
                        act.wait_ge(dpm_ready, b + 1)
                        nc.scalar.activation(dphi[q][:, :], dpm[q][:, :], ACT.Copy).then_inc(dphi_ready, 1)

            @block.tensor
            def _(pe):
                pe.wait_ge(ones_set, 1)
                with pe.Fori(0, NB // 2) as m:
                    for q in range(2):
                        b = 2 * m + q
                        pe.wait_ge(xt_ready, b)
                        wait_apart(pe, y_ready, b + 1, passed)
                        for j in range(TT):
                            mm = nc.tensor.transpose(psx[0:D, j // 4, (j % 4) * TP:(j % 4 + 1) * TP], y2[q][:, j, :], w.ident[0:TP, 0:TP])
                        mm.then_inc(yt_ready, 1)
                        pe.wait_ge(xt_ready, b + 1)
                        pe.wait_ge(qklo_ready, b)
                        for a in range(2):
                            mm = nc.tensor.matmul(psqk[:, a, 0:TH], w.wqk[:, :], xt[q][:, a * TH:(a + 1) * TH], start=True, stop=True)
                        mm.then_inc(qk_ready, 1)
                        pe.wait_ge(dpm_ready, b)
                        for a in range(2):
                            mm = nc.tensor.matmul(psdp[0:64, a, 0:TH], w.wdp[:, :], xt[q][:, a * TH:(a + 1) * TH], start=True, stop=True)
                        mm.then_inc(dp_ready, 1)
                        pe.wait_ge(v_taken, b)
                        for j in range(TT):
                            mm = nc.tensor.matmul(psv[0:TP, j * D:(j + 1) * D], xt[q][:, j * TP:(j + 1) * TP], w.wv[:, :], start=True, stop=True)
                        mm.then_inc(v_ready, 1)


def attend(nc, w, s, NB):
    N = NB * TT
    with ExitStack() as ctx:
        def sb(name, shape, dt=F32):
            return ctx.enter_context(nc.sbuf_tensor(name, shape, dt))

        def sem(name):
            return ctx.enter_context(nc.semaphore(name))

        passed = sem("attend_passed")

        def pb(name, shape):
            return ctx.enter_context(nc.psum_tensor(name, shape, F32))

        qst = [sb(f"qst{q}", [SROWS, HEADS, TP], F32R) for q in range(2)]
        kst = sb("kst_sb", [SROWS, 2, HEADS, T], F32R)
        vs = [sb(f"vs{q}", [TP, TT, D]) for q in range(2)]
        xs = [sb(f"xs{q}", [D + 1, TP]) for q in range(2)]
        res = [sb(f"res{q}", [TP, D]) for q in range(2)]
        farband = sb("farband", [TP, HEADS, NR])
        band = [sb(f"band{q}", [TP, HEADS, NR]) for q in range(2)]
        z = [sb(f"z{q}", [TP, HEADS, WIN]) for q in range(2)]
        nmax = sb("nmax", [TP, HEADS])
        p = [sb(f"p{h}", [TP, T]) for h in range(HEADS)]
        sums_ = [sb(f"sums{q}", [TP, HEADS]) for q in range(2)]
        rinv = sb("rinv", [TP, HEADS, 32])
        pt = sb("pt", [TP, HEADS, TT, TP])
        ctxs = sb("ctxs", [112, TP])
        ctxn = sb("ctxn", [128, TP])
        o = [sb(f"o{q}", [TP, D]) for q in range(2)]
        pss = [pb(f"pss{q}", [128, 1024]) for q in range(2)]
        pst = [pb(f"pst{q}", [128, 512]) for q in range(2)]
        pso = pb("pso", [128, 512])
        psb = pb("psb", [128, 512])

        qst_loaded = [sem(f"qst_loaded{q}") for q in range(2)]
        kst_loaded = sem("kst_loaded")
        v_loaded = [sem(f"v_loaded{q}") for q in range(2)]
        xs_loaded = [sem(f"xs_loaded{q}") for q in range(2)]
        res_loaded = [sem(f"res_loaded{q}") for q in range(2)]
        ring_written = sem("ring_written")
        z_loaded = [sem(f"z_loaded{q}") for q in range(2)]
        stored = [sem(f"tok2_stored{q}") for q in range(2)]
        ready0 = sem("ready0")
        scores_ready = sem("scores_ready")
        window_added = sem("window_added")
        nmax_ready = sem("nmax_ready")
        exp_done = sem("exp_done")
        tr_ready = [sem(f"tr_ready{a}") for a in range(2)]
        tr_taken = [sem(f"tr_taken{a}") for a in range(2)]
        ctx_ready = sem("ctx_ready")
        ctx_taken = sem("ctx_taken")
        rinv_ready = sem("rinv_ready")
        rb_ready = sem("rb_ready")
        ctxn_ready = sem("ctxn_ready")
        proj_ready = sem("proj_ready")
        out_ready = sem("out_ready")
        band_ready = sem("band_ready")
        far_ready = sem("far_ready")
        band_done = sem("band_done")

        def at_least(eng, semaphore, value):
            if not isinstance(value, int) or value > 0:
                eng.wait_ge(semaphore, value)

        def pairs(eng, step):
            step(0, 0)
            step(1, 1)
            with eng.Fori(1, N // 2) as m:
                step(2 * m, 0)
                step(2 * m + 1, 1)

        with nc.Block() as block:
            @block.sync
            def _(sp):
                def keys(b, slot):
                    sp.dma_start(kst[0:64, slot, :, :].bitcast(F32), s["kst"][b].rearrange("b r h t -> r (b h) t")).then_inc(kst_loaded, 16)

                def step(b, j, n, k):
                    at_least(sp, scores_ready, 4 * n - 4)
                    sp.sem_inc(passed, 1)
                    sp.dma_start(qst[k][:, :, :].bitcast(F32), s["qst"][b, :, :, bass.ds(j * TP, TP)].rearrange("b r h t -> r (b h) t")).then_inc(qst_loaded[k], 16)
                    at_least(sp, out_ready, n - 1)
                    sp.dma_start(res[k][:, :], s["tok"][b, bass.ds(j * TP, TP), :].rearrange("b t f -> (b t) f")).then_inc(res_loaded[k], 16)
                    at_least(sp, ctx_ready, n - 1)
                    sp.sem_inc(passed, 1)
                    sp.dma_start(vs[k][:, :, :], s["vst"][b].rearrange("b p j f -> p (b j) f")).then_inc(v_loaded[k], 16)

                sp.wait_ge(ready0, 1)
                keys(slice(0, 1), slice(0, 1))
                for n in range(TT):
                    step(slice(0, 1), n, n, n % 2)
                with sp.Fori(1, NB) as b:
                    sp.wait_ge(kst_loaded, 16 * b)
                    sp.wait_ge(scores_ready, 4 * TT * (b - 1))
                    keys(bass.ds(b, 1), bass.ds(b % 2, 1))
                    with sp.Fori(0, TT // 2) as jj:
                        for k in range(2):
                            step(bass.ds(b, 1), 2 * jj + k, b * TT + 2 * jj + k, k)

            @block.gpsimd
            def _(pool):
                def load_xs(n, k):
                    pool.dma_start(xs[k][0:D, :], s["xt"][bass.ds(n // TT, 1), :, bass.ds((n % TT) * TP, TP)]
                                   .rearrange("b f t -> (b f) t")).then_inc(xs_loaded[k], 16)

                def step(n, k):
                    at_least(pool, z_loaded[k], 16 * (n // 2))
                    wait_apart(pool, band_done, n + 1, passed)
                    ring = s["ring"]
                    diag = bass.AP(ring.tensor, k * TP * HEADS * WIN, [[HEADS * WIN + 1, TP], [WIN, HEADS], [1, NR]])
                    pool.dma_start(diag, band[k][:, :, :]).then_inc(ring_written, 16)
                    at_least(pool, window_added, 4 * n - 4)
                    wait_apart(pool, ring_written, 16 * (n + 1), passed)
                    pool.dma_start(z[k][:, :, :], ring[k]).then_inc(z_loaded[k], 16)
                    load_xs(n + 2, k)

                pool.wait_ge(ready0, 1)
                load_xs(0, 0)
                load_xs(1, 1)
                pairs(pool, step)

            @block.tensor
            def _(pe):
                def scores(n, k, h):
                    if h == 0:
                        pe.wait_ge(qst_loaded[k], 16 * (n // 2 + 1))
                        pe.wait_ge(kst_loaded, 16 * (n // TT + 1))
                    at_least(pe, exp_done, 4 * n + h - 1)
                    slot = (n // TT) % 2

                    def ks(a, b_):
                        return kst[:, bass.ds(slot, 1), h, a:b_].rearrange("p a n -> p (a n)")

                    nc.tensor.matmul(pss[h % 2][0:TP, REL:512], qst[k][:, h, :], ks(0, 512 - REL), start=True, stop=True)
                    nc.tensor.matmul(pss[h % 2][0:TP, 512:REL + T], qst[k][:, h, :], ks(512 - REL, T), start=True, stop=True).then_inc(scores_ready, 1)

                def transposes(n, h):
                    for a in range(2):
                        if a == 0:
                            pe.wait_ge(exp_done, 4 * n + h + 1)
                        at_least(pe, tr_taken[a], 4 * n + h)
                        for i in range(4):
                            mm = nc.tensor.transpose(pst[a][0:TP, i * TP:(i + 1) * TP], p[h][:, (4 * a + i) * TP:(4 * a + i + 1) * TP], w.ident[0:TP, 0:TP])
                        mm.then_inc(tr_ready[a], 1)

                def context(n, k):
                    pe.wait_ge(tr_taken[0], 4 * n + 4)
                    pe.wait_ge(tr_taken[1], 4 * n + 4)
                    pe.wait_ge(v_loaded[k], 16 * (n // 2 + 1))
                    at_least(pe, out_ready, n)
                    for i in range(TT):
                        for h in range(HEADS):
                            mm = nc.tensor.matmul(pso[32 * h:32 * h + HD, 0:TP], vs[k][:, i, h * HD:(h + 1) * HD],
                                                  pt[:, h, i, :], start=(i == 0), stop=(i == TT - 1))
                    mm.then_inc(ctx_ready, 1)

                def reciprocals(n):
                    pe.wait_ge(rinv_ready, n + 1)
                    pe.wait_ge(band_done, n + 3)
                    nc.tensor.matmul(psb[0:112, 0:TP], rinv[:, :, :].rearrange("p h d -> p (h d)")[:, 0:112], w.ident[0:TP, 0:TP],
                                     start=True, stop=True).then_inc(rb_ready, 1)

                def project_out(n):
                    pe.wait_ge(ctxn_ready, n + 1)
                    nc.tensor.matmul(pso[0:TP, 128:128 + D], ctxn[:, :], w.wo[:, :], start=True, stop=True).then_inc(proj_ready, 1)

                def band_terms(n, k):
                    pe.wait_ge(xs_loaded[k], 16 * (n // 2 + 1))
                    at_least(pe, band_done, n)
                    if not isinstance(n, int) or n > 2:
                        pe.wait_ge(ctxn_ready, n - 2)
                    nc.tensor.matmul(psb[0:TP, 128:128 + HEADS * NR], xs[k][:, :], w.gpos[:, :, :].rearrange("p h r -> p (h r)"),
                                     start=True, stop=True).then_inc(band_ready, 1)

                def step(n, k):
                    before = not isinstance(n, int) or n > 0
                    scores(n, k, 0)
                    if before:
                        transposes(n - 1, 2)
                    scores(n, k, 1)
                    if before:
                        transposes(n - 1, 3)
                        context(n - 1, 1 - k)
                    scores(n, k, 2)
                    transposes(n, 0)
                    if before:
                        reciprocals(n - 1)
                    scores(n, k, 3)
                    transposes(n, 1)
                    if before:
                        project_out(n - 1)
                    band_terms(n + 2, k)

                pe.wait_ge(ready0, 1)
                band_terms(0, 0)
                band_terms(1, 1)
                pairs(pe, step)
                transposes(N - 1, 2)
                transposes(N - 1, 3)
                context(N - 1, 1)
                reciprocals(N - 1)
                project_out(N - 1)

            @block.vector
            def _(dve):
                v = nc.vector

                def window_and_max(n, k, h):
                    if h == 0:
                        dve.wait_ge(z_loaded[k], 16 * (n // 2 + 1))
                    dve.wait_ge(scores_ready, 4 * n + h + 1)
                    win = pss[h % 2][0:TP, bass.ds((n % TT) * TP, WIN)]
                    v.tensor_tensor(win, win, z[k][:, h, :], ALU.add).then_inc(window_added, 1)
                    dve.wait_ge(window_added, 4 * n + h + 1)
                    v.tensor_reduce(nmax[:, h:h + 1], pss[h % 2][0:TP, REL:REL + T], AX.X, ALU.max, negate=True).then_inc(nmax_ready, 1)

                def copy_out(n, h):
                    dve.wait_ge(tr_ready[1], 4 * n + h + 1)
                    v.tensor_copy(pt[:, h, 4:8, :].rearrange("p i t -> p (i t)"), pst[1][0:TP, 0:4 * TP]).then_inc(tr_taken[1], 1)

                def invert(n, k):
                    dve.wait_ge(exp_done, 4 * n + 4)
                    v.reciprocal(rinv[:, :, :], sums_[k][:, :].rearrange("p (h a) -> p h a", a=1).to_broadcast([TP, HEADS, 32])).then_inc(rinv_ready, 1)

                def normalise(n):
                    dve.wait_ge(ctx_taken, n + 1)
                    dve.wait_ge(rb_ready, n + 1)
                    v.tensor_tensor(ctxn[0:112, :], ctxs[:, :], psb[0:112, 0:TP], ALU.mult).then_inc(ctxn_ready, 1)

                def residual(n, k):
                    dve.wait_ge(proj_ready, n + 1)
                    dve.wait_ge(res_loaded[k], 16 * (n // 2 + 1))
                    at_least(dve, stored[k], 16 * (n // 2))
                    v.tensor_tensor(o[k][:, :], pso[0:TP, 128:128 + D], res[k][:, :], ALU.add).then_inc(out_ready, 1)

                def band_out(n, k):
                    dve.wait_ge(band_ready, n + 1)
                    src = psb[0:TP, 128:128 + HEADS * NR].rearrange("p (h r) -> p h r", h=HEADS)
                    v.tensor_tensor(farband[:, :, :], w.bandstep[:, :].rearrange("p (a r) -> p a r", a=1).to_broadcast([TP, HEADS, NR]),
                                    src[:, :, 0:1].to_broadcast([TP, HEADS, NR]), ALU.mult).then_inc(far_ready, 1)
                    dve.wait_ge(far_ready, n + 1)
                    at_least(dve, ring_written, 16 * (n - 1))
                    v.tensor_tensor(band[k][:, :, :], src, farband[:, :, :], ALU.subtract).then_inc(band_done, 1)

                def step(n, k):
                    before = not isinstance(n, int) or n > 0
                    window_and_max(n, k, 0)
                    if before:
                        invert(n - 1, 1 - k)
                    window_and_max(n, k, 1)
                    if before:
                        copy_out(n - 1, 3)
                    window_and_max(n, k, 2)
                    if before:
                        normalise(n - 1)
                    window_and_max(n, k, 3)
                    copy_out(n, 1)
                    if before:
                        residual(n - 1, 1 - k)
                    band_out(n + 2, k)

                for q in range(2):
                    v.memset(pss[q][:, :], 0.0)
                    v.memset(xs[q][D:D + 1, :], 1.0)
                v.memset(pso[:, :], 0.0)
                v.memset(ctxn[96:128, :], 1.0)
                for q in range(2):
                    for h in range(HEADS):
                        last = v.tensor_copy(kst[64:96, q, h, :], w.step[64:96, :])
                last.then_inc(ready0, 1)
                band_out(0, 0)
                band_out(1, 1)
                pairs(dve, step)
                invert(N - 1, 1)
                copy_out(N - 1, 3)
                normalise(N - 1)
                residual(N - 1, 1)

            @block.scalar
            def _(act):
                def softmax(n, k, h):
                    act.wait_ge(nmax_ready, 4 * n + h + 1)
                    at_least(act, tr_ready[1], 4 * n + h - 3)
                    nc.scalar.activation(p[h][:, :], pss[h % 2][0:TP, REL:REL + T], ACT.Exp, bias=nmax[:, h:h + 1],
                                         scale=1.0, accum_out=sums_[k][:, h:h + 1]).then_inc(exp_done, 1)

                def copy_out(n, h, halves):
                    for a in halves:
                        act.wait_ge(tr_ready[a], 4 * n + h + 1)
                        nc.scalar.activation(pt[:, h, 4 * a:4 * a + 4, :].rearrange("p i t -> p (i t)"), pst[a][0:TP, 0:4 * TP],
                                             ACT.Copy).then_inc(tr_taken[a], 1)

                def context_out(n):
                    act.wait_ge(ctx_ready, n + 1)
                    at_least(act, ctxn_ready, n)
                    nc.scalar.activation(ctxs[:, :], pso[0:112, 0:TP], ACT.Copy).then_inc(ctx_taken, 1)

                def store(n, k):
                    act.wait_ge(out_ready, n + 1)
                    act.dma_start(s["tok2"][bass.ds(n // TT, 1), bass.ds((n % TT) * TP, TP), :].rearrange("b t f -> (b t) f"),
                                  o[k][:, :]).then_inc(stored[k], 16)

                def step(n, k):
                    before = not isinstance(n, int) or n > 0
                    softmax(n, k, 0)
                    if before:
                        copy_out(n - 1, 2, (0, 1))
                    softmax(n, k, 1)
                    if before:
                        copy_out(n - 1, 3, (0,))
                        context_out(n - 1)
                    softmax(n, k, 2)
                    if not isinstance(n, int) or n > 1:
                        store(n - 2, k)
                    copy_out(n, 0, (0, 1))
                    softmax(n, k, 3)
                    copy_out(n, 1, (0,))

                pairs(act, step)
                copy_out(N - 1, 2, (0, 1))
                copy_out(N - 1, 3, (0,))
                context_out(N - 1)
                store(N - 2, 0)
                store(N - 1, 1)
                for q in range(2):
                    act.wait_ge(stored[q], 16 * (N // 2))


def experts(nc, w, s, out, NB):
    G = NB * TT // 4
    GT = 4
    GN = GT * TP
    with ExitStack() as ctx:
        def sb(name, shape, dt=F32):
            return ctx.enter_context(nc.sbuf_tensor(name, shape, dt))

        def sem(name):
            return ctx.enter_context(nc.semaphore(name))

        passed = sem("experts_passed")

        def pb(name):
            return ctx.enter_context(nc.psum_tensor(name, [128, 512], F32))

        x = [sb(f"ex{q}", [TP, GT, D]) for q in range(2)]
        res = [sb(f"eres{q}", [TP, GT, D]) for q in range(2)]
        xc = sb("exc", [TP, GT, D])
        sq = sb("esq", [TP, GT, D])
        st = sb("est", [TP, 5, GT])
        y = [sb(f"ey{q}", [TP, GT, 2, D]) for q in range(2)]
        xh = [sb(f"xh{q}", [128, GN], F32R) for q in range(2)]
        xa = [sb(f"xa{q}", [128, GN], F32R) for q in range(2)]
        xb = [sb(f"xb{q}", [104, GN], F32R) for q in range(2)]
        ge = [sb(f"ge{q}", [NPAIR, GN], BF16) for q in range(2)]
        mk = [sb(f"mk{q}", [NE, GN], F32R) for q in range(2)]
        hs = [sb(f"hs{i}", [HID, GN]) for i in range(4)]
        os_ = [sb(f"os{q}", [128, GN]) for q in range(2)]
        o = [sb(f"eo{q}", [TP, GT, D]) for q in range(2)]
        psy, psg, psr, psf = pb("psy"), pb("psg"), pb("psr"), pb("psf")
        psh = [pb(f"psh{q}") for q in range(2)]
        pso = [pb(f"epso{q}") for q in range(2)]

        x_loaded = [sem(f"ex_loaded{q}") for q in range(2)]
        r_loaded = [sem(f"er_loaded{q}") for q in range(2)]
        stored = [sem(f"out_stored{q}") for q in range(2)]
        ones_set = sem("eones_set")
        chain = sem("echain")
        sums = sem("esums")
        vars_ = sem("evars")
        rstds = sem("erstds")
        y_ready = sem("ey_ready")
        yt_ready = sem("eyt_ready")
        xh_ready = sem("xh_ready")
        xl_ready = sem("xl_ready")
        xcopied = sem("xcopied")
        gate_ready = sem("gate_ready")
        ge_ready = sem("ge_ready")
        rank_ready = sem("rank_ready")
        masks_ready = sem("masks_ready")
        hid_ready = sem("hid_ready")
        hid_done = sem("hid_done")
        exp_ready = sem("exp_ready")
        os_ready = sem("os_ready")
        fold_ready = sem("fold_ready")
        o_ready = sem("o_ready")
        NLINK = 4

        tok2 = s["tok2"].rearrange("b (g j p) f -> (b g) p j f", j=GT, p=TP)
        outv = out.rearrange("b (g j p) f -> (b g) p j f", j=GT, p=TP)

        def at_least(eng, semaphore, value):
            if not isinstance(value, int) or value > 0:
                eng.wait_ge(semaphore, value)

        def steps(eng, front, middle, back):
            front(0, 0)
            front(1, 1)
            middle(0, 0)
            with eng.Fori(1, G // 2) as m:
                for k in range(2):
                    front(2 * m + k, k)
                    middle(2 * m + k - 1, 1 - k)
                    back(2 * m + k - 2, k)
            middle(G - 1, 1)
            back(G - 2, 0)
            back(G - 1, 1)

        def nothing(g, q):
            pass

        with nc.Block() as block:
            @block.sync
            def _(sp):
                def front(g, q):
                    at_least(sp, y_ready, g - 1)
                    sp.dma_start(x[q][:, :, :], tok2[bass.ds(g, 1)].rearrange("g p j f -> p (g j) f")).then_inc(x_loaded[q], 16)

                def middle(g, q):
                    at_least(sp, o_ready, g - 1)
                    sp.dma_start(res[q][:, :, :], tok2[bass.ds(g, 1)].rearrange("g p j f -> p (g j) f")).then_inc(r_loaded[q], 16)

                def back(g, q):
                    sp.wait_ge(o_ready, g + 1)
                    sp.dma_start(outv[bass.ds(g, 1)].rearrange("g p j f -> p (g j) f"), o[q][:, :, :]).then_inc(stored[q], 16)

                steps(sp, front, middle, back)
                for q in range(2):
                    sp.wait_ge(stored[q], 16 * (G // 2))

            @block.vector
            def _(dve):
                v = nc.vector

                def front(g, q):
                    n = [0]

                    def link(ins):
                        n[0] += 1
                        ins.then_inc(chain, 1)
                        dve.wait_ge(chain, g * NLINK + n[0])

                    dve.wait_ge(x_loaded[q], 16 * (g // 2 + 1))
                    at_least(dve, yt_ready, g - 1)
                    link(v.tensor_reduce(st[:, 0, :], x[q][:, :, :], AX.X, ALU.add))
                    link(v.tensor_scalar(st[:, 1, :], st[:, 0, :], -1.0 / D, None, ALU.mult))
                    link(v.tensor_tensor(xc[:, :, :], x[q][:, :, :], st[:, 1, :].rearrange("p (n a) -> p n a", a=1).to_broadcast([TP, GT, D]), ALU.add))
                    link(v.tensor_tensor(sq[:, :, :], xc[:, :, :], xc[:, :, :], ALU.mult))
                    v.tensor_reduce(st[:, 2, :], sq[:, :, :], AX.X, ALU.add).then_inc(sums, 1)
                    dve.wait_ge(rstds, g + 1)
                    rstd = st[:, 3, :].rearrange("p (n a) -> p n a", a=1).to_broadcast([TP, GT, D])
                    for t in range(2):
                        last = v.tensor_tensor(y[q][:, :, t, :], xc[:, :, :], rstd, ALU.mult)
                    last.then_inc(y_ready, 1)
                    dve.wait_ge(xh_ready, g + 1)
                    at_least(dve, hid_ready, NE * (g - 1))
                    v.tensor_tensor(xa[q][64:128, :], psy[64:128, 0:GN], xh[q][64:128, :].bitcast(F32), ALU.subtract).then_inc(xl_ready, 1)
                    dve.wait_ge(gate_ready, g + 1)
                    v.tensor_scalar(ge[q][:, :], psg[0:NPAIR, 0:GN], 0.0, None, ALU.is_ge).then_inc(ge_ready, 1)
                    dve.wait_ge(rank_ready, g + 1)
                    v.tensor_scalar(xb[q][96:96 + NE, :], psr[0:NE, 0:GN], w.thr[:, 0:1], None, ALU.is_ge)
                    v.tensor_scalar(mk[q][:, :], psr[0:NE, 0:GN], w.thr[:, 0:1], None, ALU.is_lt).then_inc(masks_ready, 1)

                def back(g, q):
                    dve.wait_ge(fold_ready, g + 1)
                    dve.wait_ge(r_loaded[q], 16 * (g // 2 + 1))
                    at_least(dve, stored[q], 16 * (g // 2))
                    v.tensor_tensor(o[q][:, :, :], psf[0:TP, 0:GT * D].rearrange("p (j f) -> p j f", j=GT), res[q][:, :, :], ALU.add).then_inc(o_ready, 1)

                for q in range(2):
                    v.memset(xb[q][D:96, :].bitcast(F32), 0.0).then_inc(ones_set, 1)
                dve.wait_ge(ones_set, 2)
                for q in range(2):
                    v.memset(xb[q][D:D + 2, :].bitcast(F32), 1.0).then_inc(ones_set, 1)
                steps(dve, front, nothing, back)

            @block.gpsimd
            def _(pool):
                def front(g, q):
                    wait_apart(pool, sums, g + 1, passed)
                    nc.gpsimd.tensor_scalar(st[:, 4, :], st[:, 2, :], 1.0 / D, EPS, ALU.mult, ALU.add).then_inc(vars_, 1)
                    wait_apart(pool, vars_, g + 1, passed)
                    nc.gpsimd.tensor_tensor(st[:, 3, :], st[:, 4, :], w.mhalf[0:TP, 0:GT], ALU.pow).then_inc(rstds, 1)
                    at_least(pool, hid_ready, NE * (g - 1))
                    wait_apart(pool, xh_ready, g + 1, passed)
                    nc.gpsimd.tensor_copy(xa[q][0:D, :], xh[q][0:D, :].bitcast(F32))
                    nc.gpsimd.tensor_copy(xb[q][0:D, :], xh[q][0:D, :].bitcast(F32)).then_inc(xcopied, 1)

                steps(pool, front, nothing, nothing)

            @block.scalar
            def _(act):
                def front(g, q):
                    act.wait_ge(yt_ready, g + 1)
                    at_least(act, xcopied, g - 1)
                    at_least(act, xl_ready, g - 1)
                    nc.scalar.activation(xh[q][:, :], psy[:, 0:GN], ACT.Copy).then_inc(xh_ready, 1)

                def middle(g, q):
                    for e in range(NE):
                        act.wait_ge(hid_ready, g * NE + e + 1)
                        nc.scalar.activation(hs[e % 4][:, :], psh[e % 2][:, 0:GN], ACT.Gelu).then_inc(hid_done, 1)
                    act.wait_ge(exp_ready, g + 1)
                    at_least(act, fold_ready, g - 1)
                    nc.scalar.activation(os_[q][:, :], pso[q][:, 0:GN], ACT.Copy).then_inc(os_ready, 1)

                steps(act, front, middle, nothing)

            @block.tensor
            def _(pe):
                def front(g, q):
                    pe.wait_ge(y_ready, g + 1)
                    at_least(pe, xh_ready, g)
                    at_least(pe, xl_ready, g)
                    for j in range(GT):
                        mm = nc.tensor.transpose(psy[:, j * TP:(j + 1) * TP], y[q][:, j, :, :].rearrange("p a f -> p (a f)"), w.ident[0:TP, 0:TP])
                    mm.then_inc(yt_ready, 1)
                    pe.wait_ge(xl_ready, g + 1)
                    pe.wait_ge(xcopied, g + 1)
                    nc.tensor.matmul(psg[:, 0:GN], w.wga[:, :], xa[q][:, :], start=True, stop=False)
                    nc.tensor.matmul(psg[:, 0:GN], w.wgb[:, :], xb[q][0:D + 2, :], start=False, stop=True).then_inc(gate_ready, 1)
                    wait_apart(pe, ge_ready, g + 1, passed)
                    nc.tensor.matmul(psr[0:NE, 0:GN], w.rank[:, :], ge[q][:, :], start=True, stop=True).then_inc(rank_ready, 1)

                def middle(g, q):
                    pe.wait_ge(masks_ready, g + 1)
                    at_least(pe, os_ready, g - 1)
                    nc.tensor.matmul(pso[q][:, 0:GN], w.b2[:, :], mk[q][:, :], start=True, stop=False)
                    for e2 in range(0, NE + 2, 2):
                        for e in (e2, e2 + 1):
                            if e < NE:
                                at_least(pe, hid_done, g * NE + e - 1)
                                nc.tensor.matmul(psh[e % 2][:, 0:GN], w.w1a[:, e, :], xa[q][:, :], start=True, stop=False)
                                nc.tensor.matmul(psh[e % 2][:, 0:GN], w.w1b[:, e, :], xb[q][:, :], start=False, stop=True).then_inc(hid_ready, 1)
                        for e in (e2 - 2, e2 - 1):
                            if e >= 0:
                                pe.wait_ge(hid_done, g * NE + e + 1)
                                mm = nc.tensor.matmul(pso[q][64 * (e % 2):64 * (e % 2) + 64, 0:GN], w.w2[:, e, :], hs[e % 4][:, :],
                                                      start=False, stop=(e >= NE - 2))
                    mm.then_inc(exp_ready, 1)

                def back(g, q):
                    pe.wait_ge(os_ready, g + 1)
                    at_least(pe, o_ready, g)
                    for j in range(GT):
                        mm = nc.tensor.matmul(psf[0:TP, j * D:(j + 1) * D], os_[q][:, j * TP:(j + 1) * TP], w.fold[:, :], start=True, stop=True)
                    mm.then_inc(fold_ready, 1)

                pe.wait_ge(ones_set, 4)
                steps(pe, front, middle, back)


def constants():
    f = np.float32

    def encoding(n):
        div = np.exp(np.arange(0, D, 2, dtype=f) * f(-np.log(10000.0) / D)).astype(f)
        ang = np.arange(n, dtype=f)[:, None] * div
        out = np.zeros((n, D), f)
        out[:, 0::2], out[:, 1::2] = np.sin(ang), np.cos(ang)
        return out

    t = np.arange(T)
    theta = BLK * np.arange(NBLK) + REL - 2
    step = (t[None, :] < theta[:, None]).astype(f)
    tau, r = np.arange(TP)[:, None], np.arange(NR)[None, :]
    off = np.zeros((NE, NE, HID), f)
    off[np.arange(NE), np.arange(NE), :] = OFF
    rank = np.zeros((NPAIR, NE), f)
    m = 0
    for a in range(NE - 1):
        for b in range(a + 1, NE):
            rank[m, a], rank[m, b] = -1, 1
            m += 1
    shift = np.zeros((NP_, NT, NODES), f)
    for i in range(NT):
        shift[np.arange(NP_), i, i * NP_ + np.arange(NP_)] = 1
    return dict(
        c_ident=np.eye(128, dtype=f), c_iota=np.tile(np.arange(NODES, dtype=f), (128, 1)),
        c_shift=shift.reshape(NP_, -1), c_pe=np.tile(encoding(NODES).T, (2, 1)),
        c_rel=np.concatenate([encoding(NR).T, np.ones((1, NR), f)]),
        c_headmask=np.repeat(np.eye(HEADS, dtype=f), HD, axis=0),
        c_blkmask=np.repeat((t[None, :] // BLK == np.arange(NBLK)[:, None]).astype(f), HEADS, axis=0),
        c_step=np.concatenate([step, step]),
        c_bandstep=(tau + r - REL < BLK * (tau // BLK) + REL - 2).astype(f),
        c_off=off.reshape(NE, -1), c_rank=rank, c_thr=(np.arange(NE, dtype=f) - 5)[:, None],
        c_fold=np.concatenate([np.eye(D, dtype=f)] * 2),
        c_rows4=np.array([[1, 0, 1, 0], [0, 1, 1, 0], [1, 0, 0, 1], [0, 1, 0, 1]], f),
    )


def layouts(a):
    NB = a["x"].shape[0]

    def by_dim(m):
        return np.ascontiguousarray(m.reshape(HEADS, HD, -1).transpose(1, 0, 2).reshape(D, -1))

    x = a["x"].reshape(NB, CH, GRID, PATCH, GRID, PATCH).transpose(1, 3, 5, 0, 2, 4).reshape(2, KP, NB, NODES)
    return dict(
        x_patch=np.ascontiguousarray(x.transpose(1, 2, 0, 3)), txt=a["txt"],
        w_embed=a["L0_tok_W_embed"], b_embed=a["L0_tok_b_embed"], w_gcn=a["L0_tok_W_gcn"], b_gcn=a["L0_tok_b_gcn"],
        w_out=a["L0_tok_W_out"], b_out=a["L0_tok_b_out"], edge_index=a["L0_tok_edge_index"],
        ln_gamma=a["L0_attn_ln_gamma"], ln_beta=a["L0_attn_ln_beta"],
        wq=a["L0_attn_Wq"], wq_t=np.ascontiguousarray(by_dim(a["L0_attn_Wq"]).T), bq=a["L0_attn_bq"],
        bq_perm=by_dim(a["L0_attn_bq"]).ravel(), u_perm=by_dim(a["L0_attn_u_bias"]).ravel(),
        wk_t=np.ascontiguousarray(by_dim(a["L0_attn_Wk"]).T), bk=by_dim(a["L0_attn_bk"]).ravel(),
        wv_t=np.ascontiguousarray(a["L0_attn_Wv"].T), bv=a["L0_attn_bv"],
        wpos_t=np.ascontiguousarray(a["L0_attn_Wpos"].T), bpos=a["L0_attn_bpos"],
        wo_t=np.ascontiguousarray(a["L0_attn_Wo"].T), bo=a["L0_attn_bo"], v_bias=a["L0_attn_v_bias"],
        wg=a["L0_ffn_Wg"], bg=a["L0_ffn_bg"], w1=a["L0_ffn_W1"], b1=a["L0_ffn_b1"], w2=a["L0_ffn_W2"], b2=a["L0_ffn_b2"],
    )


def build(nc, ins, out, NB):
    s = scratch_tensors(nc, NB)
    with ExitStack() as ctx:
        w = alloc_weights(nc, ctx)
        prepare(nc, w, ins, s, NB)
        tokens(nc, w, ins, s, NB)
        project(nc, w, s, NB)
        attend(nc, w, s, NB)
        experts(nc, w, s, out, NB)


def kernel(**inputs):
    import concourse.bacc as bacc
    from concourse.bass_utils import run_bass_kernel_spmd

    nc = bacc.Bacc("TRN2", target_bir_lowering=False, num_devices=1)
    a = {k: np.asarray(v) for k, v in inputs.items()}
    arrays = {**layouts(a), **constants()}
    import ml_dtypes
    arrays["c_shift"] = arrays["c_shift"].astype(ml_dtypes.bfloat16)
    arrays = {f"in_{k}": np.ascontiguousarray(v) for k, v in arrays.items()}
    ins = {k[3:]: nc.dram_tensor(k, v.shape, mybir.dt.from_np(v.dtype), kind="ExternalInput").ap() for k, v in arrays.items()}
    NB = a["x"].shape[0]
    out = nc.dram_tensor("out_tokens", (NB, T, D), F32, kind="ExternalOutput").ap()
    build(nc, ins, out, NB)
    r = run_bass_kernel_spmd(nc, [arrays], core_ids=[0])
    return r.results[0]["out_tokens"]
```

```python
from contextlib import ExitStack

import concourse.bass as bass
import numpy as np
from concourse import mybir

F32 = mybir.dt.float32
F32R = mybir.dt.float32r
BF16 = mybir.dt.bfloat16
I32 = mybir.dt.int32
ACT = mybir.ActivationFunctionType
ALU = mybir.AluOpType
AX = mybir.AxisListType

GRID, PATCH, CH = 28, 8, 3
NODES = GRID * GRID
TXT = 128
T = NODES + TXT
D = 64
HEADS, HD = 4, 16
TP, TT = 114, 8
NP_, NT = 112, 7
NH = NODES // 2
TH = T // 2
KIN = CH * PATCH * PATCH
KP = KIN // 2
EC, EP = 24, 126
REL = 30
NR = 2 * REL + 1
BLK = TP // 2
NBLK = T // BLK
WIN = TP + 2 * REL
SROWS = 64 + 2 * NBLK
NE, HID = 8, 128
NPAIR = NE * (NE - 1) // 2
EPS = 1e-5
OFF = -float(2.0 ** 100)


def bcast(ap, shape):
    return ap.to_broadcast(shape)


def wait_apart(eng, semaphore, value, passed):
    eng.wait_ge(semaphore, value)
    eng.sem_inc(passed, 1)


def scratch_tensors(nc, NB):
    def dram(name, shape, dt):
        return nc.dram_tensor(name, shape, dt, kind="Internal").ap()

    return dict(
        tok=dram("tok", (NB, T, D), F32),
        xt=dram("xt", (NB + 1, D, T), F32),
        qst=dram("qst", (NB, SROWS, HEADS, T), F32),
        kst=dram("kst", (NB, 64, HEADS, T), F32),
        vst=dram("vst", (NB, TP, TT, D), F32),
        ring=dram("ring", (2, TP, HEADS, WIN), F32),
        tok2=dram("tok2", (NB, T, D), F32),
    )


class W:
    pass


def alloc_weights(nc, ctx):
    w = W()

    def sb(name, shape, dt=F32):
        return ctx.enter_context(nc.sbuf_tensor(name, shape, dt))

    w.ident = sb("ident", [128, 128])
    w.ones = sb("ones", [128, 1])
    w.adj = sb("adj", [NP_, NT, NODES], F32R)
    w.dinv = sb("dinv", [NP_, NT])
    w.invdeg = sb("invdeg", [NP_, NT])
    w.sq4 = sb("sq4", [4, NODES], F32R)
    w.bg4 = sb("bg4", [4, 3, 128], F32R)
    w.we = sb("we", [KP, 2, D])
    w.etab = sb("etab", [128, NODES])
    w.wg = sb("wg", [128, 4, 128])
    w.bout = sb("bout", [128, 128])
    w.lng = sb("lng", [D, 1])
    w.lnb = sb("lnb", [D, 1])
    w.wqk = sb("wqk", [D + 1, 128])
    w.wdp = sb("wdp", [D + 1, 64])
    w.wv = sb("wv", [D + 1, D])
    w.gpos = sb("gpos", [D + 1, HEADS, NR])
    w.blkmask = sb("blkmask", [64, T])
    w.step = sb("step", [96, T])
    w.bandstep = sb("bandstep", [TP, NR])
    w.wo = sb("wo", [128, D])
    w.w1a = sb("w1a", [128, NE, HID], F32R)
    w.w1b = sb("w1b", [104, NE, HID], F32R)
    w.wga = sb("wga", [128, 128], F32R)
    w.wgb = sb("wgb", [66, 128], F32R)
    w.rank = sb("rank", [NPAIR, NE], BF16)
    w.thr = sb("thr", [NE, 1])
    w.w2 = sb("w2", [HID, NE, D])
    w.b2 = sb("b2", [NE, 128], F32R)
    w.fold = sb("fold", [128, D])
    w.mhalf = sb("mhalf", [128, TT])
    return w


def prepare(nc, w, ins, s, NB):
    A = ins
    with ExitStack() as ctx:
        def sb(name, shape, dt=F32):
            return ctx.enter_context(nc.sbuf_tensor(name, shape, dt))

        def pb(name, shape=(128, 512)):
            return ctx.enter_context(nc.psum_tensor(name, list(shape), F32))

        def sem(name):
            return ctx.enter_context(nc.semaphore(name))

        eidx = sb("eidx", [EP, 2, EC], I32)
        eidf = sb("eidf", [EP, 2, EC])
        iota = sb("iota", [128, NODES])
        onehot = sb("onehot", [EP, 2, EC, NODES], BF16)
        eyeb = sb("eyeb", [NP_, NP_], BF16)
        shift = sb("shift", [NP_, NT, NODES], BF16)
        oneb = sb("oneb", [EP, 4], BF16)
        b128 = sb("b128", [128, 1])
        pe = sb("pe", [128, NODES])
        deg = sb("deg", [NP_, NT])
        sqr = sb("sqr", [4, NODES])
        sqh = sb("sqh", [4, NODES], F32R)
        sql = sb("sql", [4, NODES])
        half4 = sb("half4", [4, NODES])
        bgr = sb("bgr", [4, 3 * 128])
        bgh = sb("bgh", [4, 3 * 128], F32R)
        bgl = sb("bgl", [4, 3 * 128])
        rm = sb("rm", [4, 4])
        wpt = sb("wpt", [D + 1, D])
        relt = sb("relt", [D + 1, NR])
        hm = sb("hm", [D, HEADS])
        pos = sb("pos", [D, NR])
        posd = sb("posd", [D, HEADS, NR])
        wqn = sb("wqn", [D, D + 1])
        vb = sb("vb", [D, 1])
        qb = sb("qb", [D + 1, 3, D])
        w1f = sb("w1f", [128, NE, HID])
        b1r = sb("b1r", [96 + NE, NE, HID])
        gw = sb("gw", [128, NE])
        gbr = sb("gbr", [66, NE])
        gd = sb("gd", [128, 128])
        b2f = sb("b2f", [NE, 2, D])
        zero = sb("zero", [TP, HEADS * T])

        psc = [pb(f"psc{i}") for i in range(2)]
        psd = pb("psd")
        psq = [pb(f"psq{i}") for i in range(2)]
        psp = pb("psp")

        loaded = sem("loaded")
        edges_loaded = sem("edges_loaded")
        cleared = sem("cleared")
        zeroed = sem("zeroed")
        onehots = sem("onehots")
        counts_ready = sem("counts_ready")
        counts_taken = sem("counts_taken")
        deg_ready = sem("deg_ready")
        pos_ready = sem("pos_ready")
        posd_ready = sem("posd_ready")
        gpos_ready = sem("gpos_ready")
        degree_taken = sem("degree_taken")
        powered = sem("powered")
        dchain = sem("dchain")

        loads = [
            (w.ident[:, :], A["c_ident"]), (w.we[:, :, :], A["w_embed"].rearrange("(k p) n -> p k n", k=2)),
            (pe[:, :], A["c_pe"]), (b128[0:64, :], A["b_embed"].rearrange("(p a) -> p a", a=1)),
            (b128[64:128, :], A["b_embed"].rearrange("(p a) -> p a", a=1)),
            (w.lng[:, :], A["ln_gamma"].rearrange("(p a) -> p a", a=1)),
            (w.lnb[:, :], A["ln_beta"].rearrange("(p a) -> p a", a=1)),
            (w.wqk[0:D, 0:D], A["wq_t"]), (w.wqk[0:D, D:128], A["wk_t"]), (w.wv[0:D, :], A["wv_t"]),
            (w.wqk[D:D + 1, D:128], A["bk"].rearrange("(a n) -> a n", a=1)),
            (w.wv[D:D + 1, :], A["bv"].rearrange("(a n) -> a n", a=1)),
            (qb[D:D + 1, 0, :], A["bq_perm"].rearrange("(a n) -> a n", a=1)),
            (qb[D:D + 1, 1, :], A["u_perm"].rearrange("(a n) -> a n", a=1)),
            (w.blkmask[:, :], A["c_blkmask"]), (w.step[64:96, :], A["c_step"]), (w.bandstep[:, :], A["c_bandstep"]),
            (wpt[0:D, :], A["wpos_t"]), (wpt[D:D + 1, :], A["bpos"].rearrange("(a n) -> a n", a=1)),
            (relt[:, :], A["c_rel"]), (hm[:, :], A["c_headmask"]),
            (wqn[:, 0:D], A["wq"]), (wqn[:, D:D + 1], A["bq"].rearrange("(p a) -> p a", a=1)),
            (vb[:, :], A["v_bias"].rearrange("a h b d -> (a h b d)").rearrange("(p a) -> p a", a=1)),
            (w1f[0:D, :, :], A["w1"].rearrange("e d h -> d e h")), (w1f[D:128, :, :], A["w1"].rearrange("e d h -> d e h")),
            (b1r[64:65, :, :], A["b1"].rearrange("(a e) h -> a e h", a=1)),
            (b1r[96:96 + NE, :, :], A["c_off"].rearrange("p (e h) -> p e h", e=NE)),
            (gw[0:D, :], A["wg"]), (gw[D:128, :], A["wg"]), (gbr[64:65, :], A["bg"].rearrange("(a n) -> a n", a=1)),
            (w.thr[:, :], A["c_thr"]), (w.w2[:, :, :], A["w2"].rearrange("e h d -> h e d")),
            (b2f[:, 0, :], A["b2"]), (b2f[:, 1, :], A["b2"]), (w.fold[:, :], A["c_fold"]),
            (rm[:, :], A["c_rows4"]), (gd[0:NPAIR, 0:NE], A["c_rank"]),
        ]
        for l in range(3):
            loads += [(w.wg[64 * q:64 * q + 64, l, 64 * q:64 * q + 64], A["w_gcn"][l]) for q in range(2)]
            loads += [(bgr[:, l * 128 + 64 * q:l * 128 + 64 * q + 64], A["b_gcn"][l:l + 1, :].to_broadcast([4, D])) for q in range(2)]
        loads += [(w.wg[64 * q:64 * q + 64, 3, 64 * q:64 * q + 64], A["w_out"]) for q in range(2)]
        loads += [(w.bout[:, 64 * q:64 * q + 64], A["b_out"].rearrange("(a n) -> a n", a=1).to_broadcast([128, D])) for q in range(2)]
        loads += [(w.wo[32 * h:32 * h + HD, :], A["wo_t"][HD * h:HD * h + HD, :]) for h in range(HEADS)]
        loads += [(w.wo[112:113, :], A["bo"].rearrange("(a n) -> a n", a=1))]
        ALL = 16 * len(loads)

        with nc.Block() as block:
            @block.sync
            def _(sp):
                sp.dma_start(eidx[:, :, :], A["edge_index"].rearrange("a (p c) -> p a c", c=EC)).then_inc(edges_loaded, 16)
                sp.dma_start(iota[:, :], A["c_iota"]).then_inc(edges_loaded, 16)
                sp.dma_start(shift[:, :, :], A["c_shift"].rearrange("p (i n) -> p i n", i=NT)).then_inc(edges_loaded, 16)
                sp.wait_ge(cleared, 4)
                for dst, src in loads:
                    sp.dma_start(dst, src).then_inc(loaded, 16)
                sp.dma_start(s["tok"][:, NODES:T, :], A["txt"]).then_inc(zeroed, 16)
                sp.dma_start(s["ring"][0], zero[:, 0:HEADS * WIN].rearrange("p (h c) -> p h c", h=HEADS)).then_inc(zeroed, 16)
                sp.dma_start(s["ring"][1], zero[:, 0:HEADS * WIN].rearrange("p (h c) -> p h c", h=HEADS)).then_inc(zeroed, 16)
                sp.dma_start(s["xt"][NB], zero[0:D, 0:T]).then_inc(zeroed, 16)
                sp.wait_ge(zeroed, 64)
                sp.wait_ge(loaded, ALL)

            @block.gpsimd
            def _(pool):
                nc.gpsimd.memset(w.wg[:, :, :], 0.0).then_inc(cleared, 1)
                nc.gpsimd.memset(w.wo[:, :], 0.0).then_inc(cleared, 1)
                nc.gpsimd.memset(zero[:, :], 0.0).then_inc(cleared, 1)
                nc.gpsimd.memset(b1r[:, :, :], 0.0).then_inc(cleared, 1)
                nc.gpsimd.memset(w.mhalf[:, :], -0.5)
                nc.gpsimd.memset(half4[:, :], 0.5).then_inc(degree_taken, 1)
                pool.wait_ge(degree_taken, 3)
                nc.gpsimd.tensor_tensor(w.dinv[:, :], deg[:, :], w.mhalf[0:NP_, 0:NT], ALU.pow).then_inc(powered, 1)
                nc.gpsimd.tensor_tensor(sqr[:, :], sql[:, :], half4[:, :], ALU.pow).then_inc(powered, 1)

            @block.tensor
            def _(pe_):
                pe_.wait_ge(loaded, ALL)
                nc.tensor.matmul(psp[0:D, 0:NR], wpt[:, :], relt[:, :], start=True, stop=True).then_inc(pos_ready, 1)
                pe_.wait_ge(posd_ready, 1)
                nc.tensor.matmul(psp[0:D + 1, 64:64 + HEADS * NR], wqn[:, :], posd[:, :, :], start=True, stop=True).then_inc(gpos_ready, 1)
                pe_.wait_ge(edges_loaded, 48)
                pe_.wait_ge(onehots, 2 * EC + 1)
                for i in range(NT):
                    for c in range(EC):
                        mm = nc.tensor.matmul(psd[0:NP_, 4 * i:4 * i + 4], onehot[:, 1, c, i * NP_:(i + 1) * NP_], oneb[:, :],
                                              start=(i == 0 and c == 0), stop=(c == EC - 1), skip_group_check=True)
                mm.then_inc(deg_ready, 1)
                for a in range(2):
                    for c in range(EC):
                        mm = nc.tensor.matmul(psq[a][0:4, 0:NH], oneb[:, :], onehot[:, 1, c, a * NH:(a + 1) * NH],
                                              start=(c == 0), stop=(c == EC - 1))
                    mm.then_inc(deg_ready, 1)
                for i in range(NT):
                    for a in range(2):
                        m = 2 * i + a
                        if m >= 2:
                            pe_.wait_ge(counts_taken, m - 1)
                        for c in range(EC):
                            nc.tensor.matmul(psc[a][0:NP_, 0:NH], onehot[:, 0, c, i * NP_:(i + 1) * NP_],
                                             onehot[:, 1, c, a * NH:(a + 1) * NH], start=(c == 0), stop=False)
                        nc.tensor.matmul(psc[a][0:NP_, 0:NH], shift[:, i, i * NP_:(i + 1) * NP_],
                                         shift[:, i, a * NH:(a + 1) * NH], start=False, stop=True).then_inc(counts_ready, 1)

            @block.scalar
            def _(act):
                for m in range(2 * NT):
                    i, a = divmod(m, 2)
                    act.wait_ge(counts_ready, m + 1)
                    nc.scalar.activation(w.adj[:, i, a * NH:(a + 1) * NH], psc[a][0:NP_, 0:NH], ACT.Copy).then_inc(counts_taken, 1)

            @block.vector
            def _(dve):
                n = [0]

                def link(ins):
                    n[0] += 1
                    ins.then_inc(dchain, 1)
                    dve.wait_ge(dchain, n[0])

                v = nc.vector
                v.memset(oneb[:, :], 1.0)
                v.memset(w.ones[:, :], 1.0).then_inc(onehots, 1)
                dve.wait_ge(edges_loaded, 48)
                link(v.tensor_copy(eidf[:, :, :], eidx[:, :, :]))
                for c in range(EC):
                    for e in range(2):
                        v.tensor_scalar(onehot[:, e, c, :], iota[0:EP, :], eidf[:, e, c:c + 1], None, ALU.is_equal).then_inc(onehots, 1)
                dve.wait_ge(loaded, ALL)
                dve.wait_ge(pos_ready, 1)
                link(v.tensor_copy(pos[:, :], psp[0:D, 0:NR]))
                link(v.tensor_scalar(pos[:, :], pos[:, :], pos[:, NR - 1:NR], None, ALU.subtract))
                link(v.tensor_tensor(wqn[:, D:D + 1], wqn[:, D:D + 1], vb[:, :], ALU.add))
                for h in range(HEADS):
                    last = v.tensor_scalar(posd[:, h, :], pos[:, :], hm[:, h:h + 1], 0.25, ALU.mult, ALU.mult)
                last.then_inc(posd_ready, 1)
                link(v.tensor_tensor(qb[D:D + 1, 2, :], qb[D:D + 1, 0, :], qb[D:D + 1, 1, :], ALU.add))
                link(v.tensor_copy(w.wqk[D:D + 1, 0:D], qb[D:D + 1, 2, :]))
                link(v.tensor_scalar(w.wqk[:, 0:D], w.wqk[:, 0:D], 0.25, None, ALU.mult))
                dve.wait_ge(gpos_ready, 1)
                link(v.tensor_copy(w.gpos[:, :, :], psp[0:D + 1, 64:64 + HEADS * NR].rearrange("p (h r) -> p h r", h=HEADS)))
                v.tensor_copy(w.wdp[:, :].rearrange("p (k h) -> p k h", h=HEADS),
                              w.gpos[:, :, 0].rearrange("p (k h) -> p k h", k=1).to_broadcast([D + 1, NBLK, HEADS]))
                v.tensor_scalar(w.etab[:, :], pe[:, :], b128[:, 0:1], None, ALU.add)
                dve.wait_ge(deg_ready, 3)
                v.tensor_scalar(deg[:, :], psd[0:NP_, 0:4 * NT].rearrange("p (i k) -> p i k", k=4)[:, :, 0], 1.0, None, ALU.add).then_inc(degree_taken, 1)
                v.tensor_scalar(sql[:, 0:NH], psq[0][0:4, 0:NH], 1.0, None, ALU.add)
                v.tensor_scalar(sql[:, NH:NODES], psq[1][0:4, 0:NH], 1.0, None, ALU.add).then_inc(degree_taken, 1)
                dve.wait_ge(degree_taken, 3)
                v.reciprocal(w.invdeg[:, :], deg[:, :])
                dve.wait_ge(powered, 2)
                link(v.tensor_copy(sqh[:, :], sqr[:, :]))
                link(v.tensor_tensor(sql[:, :], sqr[:, :], sqh[:, :].bitcast(F32), ALU.subtract))
                link(v.tensor_scalar(sql[:, :], sql[:, :], rm[:, 1:2], None, ALU.mult))
                v.scalar_tensor_tensor(out=w.sq4[:, :], in0=sqh[:, :].bitcast(F32), scalar=rm[:, 0:1], in1=sql[:, :], op0=ALU.mult, op1=ALU.add)
                link(v.tensor_copy(bgh[:, :], bgr[:, :]))
                link(v.tensor_tensor(bgl[:, :], bgr[:, :], bgh[:, :].bitcast(F32), ALU.subtract))
                link(v.tensor_scalar(bgl[:, :], bgl[:, :], rm[:, 3:4], None, ALU.mult))
                v.scalar_tensor_tensor(out=w.bg4[:, :, :].rearrange("p l n -> p (l n)"), in0=bgh[:, :].bitcast(F32), scalar=rm[:, 2:3], in1=bgl[:, :], op0=ALU.mult, op1=ALU.add)
                link(v.tensor_copy(w.w1a[:, :, :], w1f[:, :, :]))
                link(v.memset(w.w1b[:, :, :].bitcast(F32), 0.0))
                v.tensor_tensor(w.w1b[0:D, :, :], w1f[0:D, :, :], w.w1a[0:D, :, :].bitcast(F32), ALU.subtract)
                v.tensor_copy(w.w1b[96:96 + NE, :, :], b1r[96:96 + NE, :, :])
                link(v.tensor_copy(w.w1b[D:D + 1, :, :], b1r[64:65, :, :]))
                link(v.tensor_tensor(b1r[64:65, :, :], b1r[64:65, :, :], w.w1b[D:D + 1, :, :].bitcast(F32), ALU.subtract))
                link(v.tensor_copy(w.rank[:, :], gd[0:NPAIR, 0:NE]))
                link(v.memset(gd[:, :], 0.0))
                m = 0
                for a in range(NE - 1):
                    k = NE - 1 - a
                    v.tensor_scalar(gd[:, m:m + k], gw[:, a + 1:NE], gw[:, a:a + 1], -1.0, ALU.subtract, ALU.mult)
                    m += k
                link(v.memset(w.wgb[:, :].bitcast(F32), 0.0))
                link(v.tensor_copy(w.wga[:, :], gd[:, :]))
                link(v.tensor_tensor(w.wgb[0:D, :], gd[0:D, :], w.wga[0:D, :].bitcast(F32), ALU.subtract))
                m = 0
                for a in range(NE - 1):
                    k = NE - 1 - a
                    link(v.tensor_scalar(gd[64:65, m:m + k], gbr[64:65, a + 1:NE], gbr[64:65, a:a + 1], -1.0, ALU.subtract, ALU.mult))
                    m += k
                link(v.tensor_copy(w.wgb[64:65, 0:NPAIR], gd[64:65, 0:NPAIR]))
                link(v.tensor_tensor(gd[64:65, 0:NPAIR], gd[64:65, 0:NPAIR], w.wgb[64:65, 0:NPAIR].bitcast(F32), ALU.subtract))
                v.tensor_copy(w.b2[:, 0:D], b2f[:, 0, :])
                link(v.tensor_copy(w.b2[:, D:128], b2f[:, 1, :]))
                link(v.tensor_tensor(w.b2[:, D:128], b2f[:, 1, :], w.b2[:, 0:D].bitcast(F32), ALU.subtract))

        with nc.Block() as block:
            lob = ctx.enter_context(nc.sbuf_tensor("lob", [66, NE * HID + 128], F32R))
            moved = sem("moved")
            rounded = sem("rounded")

            @block.vector
            def _(dve):
                nc.vector.tensor_copy(lob[64:65, 0:NE * HID], b1r[64:65, :, :].rearrange("p e h -> p (e h)"))
                nc.vector.tensor_copy(lob[64:65, NE * HID:NE * HID + NPAIR], gd[64:65, 0:NPAIR]).then_inc(rounded, 1)

            @block.sync
            def _(sp):
                sp.wait_ge(rounded, 1)
                sp.dma_start(w.w1b[65:66, :, :].rearrange("p e h -> p (e h)").bitcast(F32), lob[64:65, 0:NE * HID].bitcast(F32)).then_inc(moved, 16)
                sp.dma_start(w.wgb[65:66, 0:NPAIR].bitcast(F32), lob[64:65, NE * HID:NE * HID + NPAIR].bitcast(F32)).then_inc(moved, 16)
                sp.wait_ge(moved, 32)


def tokens(nc, w, ins, s, NB):
    xp = ins["x_patch"]
    with ExitStack() as ctx:
        def sb(name, shape, dt=F32):
            return ctx.enter_context(nc.sbuf_tensor(name, shape, dt))

        def sem(name):
            return ctx.enter_context(nc.semaphore(name))

        passed = sem("tokens_passed")

        px = [sb(f"px{q}", [KP, 2, 2, NODES]) for q in range(2)]
        r = [sb(f"r{q}", [128, NODES]) for q in range(2)]
        g = [sb(f"g{q}", [NP_, NT, 128]) for q in range(2)]
        ghi = [sb(f"ghi{q}", [NP_, NT, 128], F32R) for q in range(2)]
        glo = [sb(f"glo{q}", [NP_, NT, 128], F32R) for q in range(2)]
        ot = [sb(f"ot{q}", [NP_, NT, 128]) for q in range(2)]
        feat = [ctx.enter_context(nc.psum_tensor(f"feat{q}", [128, 2, 512], F32)) for q in range(2)]
        node = [ctx.enter_context(nc.psum_tensor(f"node{q}", [128, 2 * 512], F32)) for q in range(2)]
        px_loaded = [sem(f"px_loaded{q}") for q in range(2)]
        embedded = [sem(f"embedded{q}") for q in range(2)]
        r_ready = [sem(f"r_ready{q}") for q in range(2)]
        node_ready = [sem(f"node_ready{q}") for q in range(2)]
        g_ready = [sem(f"g_ready{q}") for q in range(2)]
        ghi_ready = [sem(f"ghi_ready{q}") for q in range(2)]
        glo_ready = [sem(f"glo_ready{q}") for q in range(2)]
        agg_ready = [sem(f"agg_ready{q}") for q in range(2)]
        out_scaled = [sem(f"out_scaled{q}") for q in range(2)]
        out_ready = [sem(f"out_ready{q}") for q in range(2)]
        stored = [sem(f"tok_stored{q}") for q in range(2)]
        LOOPS = NB // 4

        with nc.Block() as block:
            @block.sync
            def _(sp):
                with sp.Fori(0, LOOPS) as m:
                    for q in range(2):
                        sp.wait_ge(embedded[q], m)
                        sp.dma_start(px[q][:, :, :, :], xp[:, bass.ds(4 * m + 2 * q, 2), :, :]).then_inc(px_loaded[q], 16)

            @block.tensor
            def _(pe):
                with pe.Fori(0, LOOPS) as m:
                    for q in range(2):
                        pe.wait_ge(px_loaded[q], 16 * (m + 1))
                        pe.wait_ge(r_ready[q], 4 * m)
                        for a in range(2):
                            for k in range(2):
                                for e in range(2):
                                    mm = nc.tensor.matmul(feat[q][64 * e:64 * e + 64, a, 0:NH], w.we[:, k, :],
                                                          px[q][:, e, k, a * NH:(a + 1) * NH], start=(k == 0), stop=(k == 1))
                        mm.then_inc(embedded[q], 1)
                    for l in range(4):
                        for q in range(2):
                            pe.wait_ge(r_ready[q], 4 * m + l + 1)
                            if l:
                                pe.wait_ge(g_ready[q], 3 * m + l)
                            else:
                                pe.wait_ge(out_scaled[q], m)
                            for i in range(NT):
                                mm = nc.tensor.matmul(node[q][0:NP_, i * 128:(i + 1) * 128], r[q][:, i * NP_:(i + 1) * NP_],
                                                      w.wg[:, l, :], start=True, stop=True)
                            mm.then_inc(node_ready[q], 1)
                        if l == 3:
                            continue
                        for q in range(2):
                            pe.wait_ge(ghi_ready[q], 3 * m + l + 1)
                            pe.wait_ge(glo_ready[q], 3 * m + l + 1)
                            for a in range(2):
                                out = feat[q][:, a, 0:NH]
                                nc.tensor.matmul(out, w.bg4[:, l, :], w.sq4[:, a * NH:(a + 1) * NH], start=True, stop=False)
                                for i in range(NT):
                                    nc.tensor.matmul(out, ghi[q][:, i, :], w.adj[:, i, a * NH:(a + 1) * NH], start=False, stop=False)
                                    mm = nc.tensor.matmul(out, glo[q][:, i, :], w.adj[:, i, a * NH:(a + 1) * NH],
                                                          start=False, stop=(i == NT - 1))
                            mm.then_inc(agg_ready[q], 1)

            @block.vector
            def _(dve):
                with dve.Fori(0, LOOPS) as m:
                    for q in range(2):
                        dve.wait_ge(embedded[q], m + 1)
                        dve.wait_ge(node_ready[q], 4 * m)
                        nc.vector.tensor_tensor(r[q][:, :].rearrange("p (a n) -> p a n", a=2), feat[q][:, :, 0:NH],
                                                w.etab[:, :].rearrange("p (a n) -> p a n", a=2), ALU.add).then_inc(r_ready[q], 1)
                    for l in range(4):
                        for q in range(2):
                            dve.wait_ge(node_ready[q], 4 * m + l + 1)
                            src = node[q][0:NP_, 0:NT * 128].rearrange("p (i n) -> p i n", i=NT)
                            if l < 3:
                                scale = w.invdeg if l else w.dinv
                                dve.wait_ge(glo_ready[q], 3 * m + l)
                                nc.vector.tensor_tensor(g[q][:, :, :], src, scale[:, :].rearrange("p (i a) -> p i a", a=1)
                                                        .to_broadcast([NP_, NT, 128]), ALU.mult).then_inc(g_ready[q], 1)
                            else:
                                dve.wait_ge(stored[q], 32 * m)
                                nc.vector.tensor_tensor(ot[q][:, :, :], src, w.dinv[:, :].rearrange("p (i a) -> p i a", a=1)
                                                        .to_broadcast([NP_, NT, 128]), ALU.mult).then_inc(out_scaled[q], 1)

            @block.scalar
            def _(act):
                with act.Fori(0, LOOPS) as m:
                    for l in range(3):
                        for q in range(2):
                            act.wait_ge(g_ready[q], 3 * m + l + 1)
                            act.wait_ge(agg_ready[q], 3 * m + l)
                            nc.scalar.activation(ghi[q][:, :, :], g[q][:, :, :], ACT.Copy).then_inc(ghi_ready[q], 1)
                        for q in range(2):
                            act.wait_ge(agg_ready[q], 3 * m + l + 1)
                            nc.scalar.activation(r[q][:, :].rearrange("p (a n) -> p a n", a=2), feat[q][:, :, 0:NH],
                                                 ACT.Relu).then_inc(r_ready[q], 1)

            @block.gpsimd
            def _(pool):
                with pool.Fori(0, LOOPS) as m:
                    for l in range(3):
                        for q in range(2):
                            wait_apart(pool, ghi_ready[q], 3 * m + l + 1, passed)
                            nc.gpsimd.tensor_tensor(glo[q][:, :, :], g[q][:, :, :], ghi[q][:, :, :].bitcast(F32),
                                                    ALU.subtract).then_inc(glo_ready[q], 1)
                    for q in range(2):
                        wait_apart(pool, out_scaled[q], m + 1, passed)
                        nc.gpsimd.tensor_tensor(ot[q][:, :, :], ot[q][:, :, :], w.bout[0:NP_, :].rearrange("p (a n) -> p a n", a=1)
                                                .to_broadcast([NP_, NT, 128]), ALU.add).then_inc(out_ready[q], 1)
                    for q in range(2):
                        wait_apart(pool, out_ready[q], m + 1, passed)
                        for e in range(2):
                            pool.dma_start(s["tok"][bass.ds(4 * m + 2 * q + e, 1), 0:NODES, :].rearrange("b (i p) f -> p (b i) f", p=NP_),
                                           ot[q][:, :, 64 * e:64 * e + 64]).then_inc(stored[q], 16)
                for q in range(2):
                    pool.wait_ge(stored[q], 32 * LOOPS)


def project(nc, w, s, NB):
    with ExitStack() as ctx:
        def sb(name, shape, dt=F32):
            return ctx.enter_context(nc.sbuf_tensor(name, shape, dt))

        def sem(name):
            return ctx.enter_context(nc.semaphore(name))

        passed = sem("project_passed")

        x = [sb(f"px_{q}", [TP, TT, D]) for q in range(2)]
        xc = sb("xc", [TP, TT, D])
        sq = sb("sqx", [TP, TT, D])
        y1 = sb("y1", [TP, TT, D])
        y2 = sb("y2", [TP, TT, D])
        st = sb("stats", [TP, 5, TT])
        xt = [sb(f"xt{q}", [D + 1, T]) for q in range(2)]
        qkhi = [sb(f"qkhi{q}", [128, T], F32R) for q in range(2)]
        qklo = [sb(f"qklo{q}", [128, T], F32R) for q in range(2)]
        dpm = sb("dpm", [64, T])
        dphi = [sb(f"dphi{q}", [64, T], F32R) for q in range(2)]
        dplo = [sb(f"dplo{q}", [64, T], F32R) for q in range(2)]
        vv = [sb(f"vv{q}", [TP, TT, D]) for q in range(2)]
        psx = ctx.enter_context(nc.psum_tensor("psx", [128, 2, 512], F32))
        psqk = ctx.enter_context(nc.psum_tensor("psqk", [128, 2, 512], F32))
        psdp = ctx.enter_context(nc.psum_tensor("psdp", [128, 2, 512], F32))
        psv = ctx.enter_context(nc.psum_tensor("psv", [128, 512], F32))
        x_loaded = [sem(f"x_loaded{q}") for q in range(2)]
        x_used = sem("x_used")
        ones_set = sem("ones_set")
        vars_ = sem("vars_")
        rstds = sem("rstds")
        y_ready = sem("y_ready")
        yt_ready = sem("yt_ready")
        xt_ready = sem("xt_ready")
        qk_ready = sem("qk_ready")
        dp_ready = sem("dp_ready")
        v_ready = sem("v_ready")
        qkhi_ready = sem("qkhi_ready")
        qklo_ready = sem("qklo_ready")
        v_taken = sem("v_taken")
        dpm_ready = sem("dpm_ready")
        dphi_ready = sem("dphi_ready")
        dplo_ready = sem("dplo_ready")
        saved = [sem(f"saved{q}") for q in range(2)]
        chain = sem("chainp")
        NSAVE = 8
        NLINK = 10

        def two(ap):
            return ap.rearrange("p (a n) -> p a n", a=2)

        def twice(ap):
            return ap.rearrange("p (a n) -> p a n", a=1).to_broadcast([64, 2, T])

        def at_least(eng, semaphore, value):
            if not isinstance(value, int) or value > 0:
                eng.wait_ge(semaphore, value)

        def steps(eng, step):
            for b in range(4):
                step(b, b % 2, b < NB - 1)
            if NB > 4:
                with eng.Fori(2, NB // 2 - 1) as m:
                    step(2 * m, 0, True)
                    step(2 * m + 1, 1, True)
                step(NB - 2, 0, True)
                step(NB - 1, 1, False)

        with nc.Block() as block:
            @block.sync
            def _(sp):
                def load(b, q):
                    at_least(sp, x_used, b - 1)
                    sp.dma_start(x[q][:, :, :], s["tok"][bass.ds(b, 1)].rearrange("b (j p) f -> p (b j) f", p=TP)).then_inc(x_loaded[q], 16)

                def rows(name, b, r0, n):
                    return s[name][bass.ds(b, 1), r0:r0 + n].rearrange("b r h t -> (b r h) t")

                def step(b, q, ahead):
                    sv = saved[q]
                    if not isinstance(b, int) or b < NB - 2:
                        load(b + 2, q)
                    sp.wait_ge(xt_ready, b + 1)
                    sp.dma_start(s["xt"][bass.ds(b, 1)].rearrange("b f t -> (b f) t"), xt[q][0:D, :]).then_inc(sv, 16)
                    q_rows = s["qst"][bass.ds(b, 1), 0:64].rearrange("b (u g r) h t -> u (r h) (b g) t", u=2, g=2)
                    k_rows = s["kst"][bass.ds(b, 1)].rearrange("b (g u r) h t -> u (r h) (b g) t", g=2, u=2)
                    sp.wait_ge(qkhi_ready, b + 1)
                    sp.dma_start(q_rows[0], twice(qkhi[q][0:64, :].bitcast(F32))).then_inc(sv, 16)
                    sp.dma_start(k_rows[0], twice(qkhi[q][64:128, :].bitcast(F32))).then_inc(sv, 16)
                    sp.wait_ge(qklo_ready, b + 1)
                    sp.dma_start(q_rows[1], twice(qklo[q][0:64, :].bitcast(F32))).then_inc(sv, 16)
                    sp.dma_start(k_rows[1], twice(qklo[q][64:128, :].bitcast(F32))).then_inc(sv, 16)
                    sp.wait_ge(v_taken, b + 1)
                    sp.dma_start(s["vst"][bass.ds(b, 1)].rearrange("b p j f -> p (b j) f"), vv[q][:, :, :]).then_inc(sv, 16)
                    sp.wait_ge(dphi_ready, b + 1)
                    sp.dma_start(rows("qst", b, 64, NBLK), dphi[q][:, :].bitcast(F32)).then_inc(sv, 16)
                    sp.wait_ge(dplo_ready, b + 1)
                    sp.dma_start(rows("qst", b, 64 + NBLK, NBLK), dplo[q][:, :].bitcast(F32)).then_inc(sv, 16)

                load(0, 0)
                load(1, 1)
                steps(sp, step)
                for q in range(2):
                    sp.wait_ge(saved[q], 16 * NSAVE * (NB // 2))

            @block.vector
            def _(dve):
                v = nc.vector

                def link(ins, b, i):
                    ins.then_inc(chain, 1)
                    dve.wait_ge(chain, b * NLINK + i)

                def moments(b, k, src):
                    i = 5 * k
                    link(v.tensor_reduce(st[:, 0, :], src, AX.X, ALU.add), b, i + 1)
                    link(v.tensor_scalar(st[:, 1, :], st[:, 0, :], -1.0 / D, None, ALU.mult), b, i + 2)
                    link(v.tensor_tensor(xc[:, :, :], src, st[:, 1, :].rearrange("p (n a) -> p n a", a=1).to_broadcast([TP, TT, D]), ALU.add), b, i + 3)
                    link(v.tensor_tensor(sq[:, :, :], xc[:, :, :], xc[:, :, :], ALU.mult), b, i + 4)
                    link(v.tensor_reduce(st[:, 2, :], sq[:, :, :], AX.X, ALU.add), b, i + 5)
                    v.tensor_scalar(st[:, 4, :], st[:, 2, :], 1.0 / D, EPS, ALU.mult, ALU.add).then_inc(vars_, 1)

                def scaled(b, k, dst):
                    dve.wait_ge(rstds, 2 * b + k + 1)
                    return v.tensor_tensor(dst, xc[:, :, :], st[:, 3, :].rearrange("p (n a) -> p n a", a=1).to_broadcast([TP, TT, D]), ALU.mult)

                def first_moments(b, q):
                    dve.wait_ge(x_loaded[q], 16 * (b // 2 + 1))
                    moments(b, 0, x[q][:, :, :])

                def second_moments(b):
                    scaled(b, 0, y1[:, :, :]).then_inc(x_used, 1)
                    dve.wait_ge(x_used, b + 1)
                    moments(b, 1, y1[:, :, :])

                def normalised(b):
                    at_least(dve, yt_ready, b)
                    scaled(b, 1, y2[:, :, :]).then_inc(y_ready, 1)

                def low_half(b, q):
                    at_least(dve, saved[q], 16 * NSAVE * (b // 2))
                    dve.wait_ge(qkhi_ready, b + 1)
                    v.tensor_tensor(two(qklo[q][:, :]), psqk[:, :, 0:TH], two(qkhi[q][:, :].bitcast(F32)), ALU.subtract).then_inc(qklo_ready, 1)

                def mask_blocks(b):
                    dve.wait_ge(dp_ready, b + 1)
                    at_least(dve, dphi_ready, b)
                    at_least(dve, dplo_ready, b)
                    v.tensor_tensor(two(dpm[:, :]), psdp[0:64, :, 0:TH], two(w.blkmask[:, :]), ALU.mult).then_inc(dpm_ready, 1)

                def step(b, q, ahead):
                    if ahead:
                        first_moments(b + 1, 1 - q)
                        second_moments(b + 1)
                    low_half(b, q)
                    mask_blocks(b)
                    if ahead:
                        normalised(b + 1)

                v.memset(xt[0][D:D + 1, :], 1.0)
                v.memset(xt[1][D:D + 1, :], 1.0).then_inc(ones_set, 1)
                first_moments(0, 0)
                second_moments(0)
                normalised(0)
                steps(dve, step)

            @block.gpsimd
            def _(pool):
                def power(k):
                    wait_apart(pool, vars_, k + 1, passed)
                    nc.gpsimd.tensor_tensor(st[:, 3, :], st[:, 4, :], w.mhalf[0:TP, :], ALU.pow).then_inc(rstds, 1)

                def step(b, q, ahead):
                    if ahead:
                        power(2 * b + 2)
                        power(2 * b + 3)
                    at_least(pool, saved[q], 16 * NSAVE * (b // 2))
                    wait_apart(pool, dphi_ready, b + 1, passed)
                    nc.gpsimd.tensor_tensor(dplo[q][:, :], dpm[:, :], dphi[q][:, :].bitcast(F32), ALU.subtract).then_inc(dplo_ready, 1)

                power(0)
                power(1)
                steps(pool, step)

            @block.scalar
            def _(act):
                def transposed(b, q):
                    at_least(act, saved[q], 16 * NSAVE * (b // 2))
                    act.wait_ge(yt_ready, b + 1)
                    nc.scalar.activation(two(xt[q][0:D, :]), psx[0:D, :, 0:TH], ACT.Identity, bias=w.lnb[:, 0:1],
                                         scale=w.lng[:, 0:1]).then_inc(xt_ready, 1)

                def step(b, q, ahead):
                    act.wait_ge(qk_ready, b + 1)
                    nc.scalar.activation(two(qkhi[q][:, :]), psqk[:, :, 0:TH], ACT.Copy).then_inc(qkhi_ready, 1)
                    act.wait_ge(v_ready, b + 1)
                    nc.scalar.activation(vv[q][:, :, :].rearrange("p j f -> p (j f)"), psv[0:TP, :], ACT.Copy).then_inc(v_taken, 1)
                    act.wait_ge(dpm_ready, b + 1)
                    nc.scalar.activation(dphi[q][:, :], dpm[:, :], ACT.Copy).then_inc(dphi_ready, 1)
                    if ahead:
                        transposed(b + 1, 1 - q)

                transposed(0, 0)
                steps(act, step)

            @block.tensor
            def _(pe):
                def transposes(b):
                    at_least(pe, xt_ready, b)
                    wait_apart(pe, y_ready, b + 1, passed)
                    for j in range(TT):
                        mm = nc.tensor.transpose(psx[0:D, j // 4, (j % 4) * TP:(j % 4 + 1) * TP], y2[:, j, :], w.ident[0:TP, 0:TP])
                    mm.then_inc(yt_ready, 1)

                def step(b, q, ahead):
                    pe.wait_ge(xt_ready, b + 1)
                    at_least(pe, qklo_ready, b)
                    for a in range(2):
                        mm = nc.tensor.matmul(psqk[:, a, 0:TH], w.wqk[:, :], xt[q][:, a * TH:(a + 1) * TH], start=True, stop=True)
                    mm.then_inc(qk_ready, 1)
                    at_least(pe, dpm_ready, b)
                    for a in range(2):
                        mm = nc.tensor.matmul(psdp[0:64, a, 0:TH], w.wdp[:, :], xt[q][:, a * TH:(a + 1) * TH], start=True, stop=True)
                    mm.then_inc(dp_ready, 1)
                    at_least(pe, v_taken, b)
                    for j in range(TT):
                        mm = nc.tensor.matmul(psv[0:TP, j * D:(j + 1) * D], xt[q][:, j * TP:(j + 1) * TP], w.wv[:, :], start=True, stop=True)
                    mm.then_inc(v_ready, 1)
                    if ahead:
                        transposes(b + 1)

                pe.wait_ge(ones_set, 1)
                transposes(0)
                steps(pe, step)


def attend(nc, w, s, NB):
    N = NB * TT
    with ExitStack() as ctx:
        def sb(name, shape, dt=F32):
            return ctx.enter_context(nc.sbuf_tensor(name, shape, dt))

        def sem(name):
            return ctx.enter_context(nc.semaphore(name))

        passed = sem("attend_passed")

        def pb(name, shape):
            return ctx.enter_context(nc.psum_tensor(name, shape, F32))

        qst = [sb(f"qst{q}", [SROWS, HEADS, TP], F32R) for q in range(2)]
        kst = sb("kst_sb", [SROWS, 2, HEADS, T], F32R)
        vs = [sb(f"vs{q}", [TP, TT, D]) for q in range(2)]
        xs = [sb(f"xs{q}", [D + 1, TP]) for q in range(2)]
        res = [sb(f"res{q}", [TP, D]) for q in range(2)]
        farband = sb("farband", [TP, HEADS, NR])
        band = [sb(f"band{q}", [TP, HEADS, NR]) for q in range(2)]
        z = [sb(f"z{q}", [TP, HEADS, WIN]) for q in range(2)]
        nmax = sb("nmax", [TP, HEADS])
        p = [sb(f"p{h}", [TP, T]) for h in range(HEADS)]
        sums_ = [sb(f"sums{q}", [TP, HEADS]) for q in range(2)]
        rinv = [sb(f"rinv{q}", [TP, HEADS, 32]) for q in range(2)]
        pt = [sb(f"pt{q}", [TP, HEADS, TT, TP]) for q in range(2)]
        ctxs = sb("ctxs", [112, TP])
        ctxn = sb("ctxn", [128, TP])
        o = [sb(f"o{q}", [TP, D]) for q in range(2)]
        pss = [pb(f"pss{q}", [128, 1024]) for q in range(2)]
        pst = [pb(f"pst{q}", [128, 512]) for q in range(2)]
        pso = pb("pso", [128, 512])
        psb = pb("psb", [128, 512])

        qst_loaded = [sem(f"qst_loaded{q}") for q in range(2)]
        kst_loaded = sem("kst_loaded")
        v_loaded = [sem(f"v_loaded{q}") for q in range(2)]
        xs_loaded = [sem(f"xs_loaded{q}") for q in range(2)]
        res_loaded = [sem(f"res_loaded{q}") for q in range(2)]
        ring_written = [sem(f"ring_written{q}") for q in range(2)]
        z_loaded = [sem(f"z_loaded{q}") for q in range(2)]
        stored = [sem(f"tok2_stored{q}") for q in range(2)]
        ready0 = sem("ready0")
        scores_ready = sem("scores_ready")
        window_added = sem("window_added")
        nmax_ready = sem("nmax_ready")
        exp_done = sem("exp_done")
        tr_ready = [sem(f"tr_ready{a}") for a in range(2)]
        tr_taken = [sem(f"tr_taken{a}") for a in range(2)]
        ctx_ready = sem("ctx_ready")
        ctx_taken = sem("ctx_taken")
        rinv_ready = sem("rinv_ready")
        rb_ready = sem("rb_ready")
        ctxn_ready = sem("ctxn_ready")
        proj_ready = sem("proj_ready")
        out_ready = sem("out_ready")
        band_ready = sem("band_ready")
        far_ready = sem("far_ready")
        band_done = sem("band_done")

        def at_least(eng, semaphore, value):
            if not isinstance(value, int) or value > 0:
                eng.wait_ge(semaphore, value)

        def pairs(eng, step):
            step(0, 0, True, False, False)
            step(1, 1, True, True, False)
            step(2, 0, True, True, True)
            step(3, 1, True, True, True)
            with eng.Fori(2, N // 2) as m:
                step(2 * m, 0, True, True, True)
                step(2 * m + 1, 1, True, True, True)
            step(N, 0, False, True, True)
            step(N + 1, 1, False, False, True)

        with nc.Block() as block:
            @block.sync
            def _(sp):
                def wait(semaphore, value):
                    if isinstance(value, int):
                        at_least(sp, semaphore, value)
                    else:
                        wait_apart(sp, semaphore, value, passed)

                def place(n):
                    return bass.ds(n // TT, 1), bass.ds((n % TT) * TP, TP)

                def load_xs(n, k):
                    wait(band_done, n - 1)
                    b, t = place(n)
                    sp.dma_start(xs[k][0:D, :], s["xt"][b, :, t].rearrange("b f t -> (b f) t")).then_inc(xs_loaded[k], 16)

                def load_queries(n, k):
                    wait(scores_ready, 4 * n - 4)
                    b, t = place(n)
                    sp.dma_start(qst[k][:, :, :].bitcast(F32), s["qst"][b, :, :, t].rearrange("b r h t -> r (b h) t")).then_inc(qst_loaded[k], 16)

                def load_window(n, k):
                    wait(ring_written[k], 16 * (n // 2 + 1))
                    wait(window_added, 4 * n - 4)
                    sp.dma_start(z[k][:, :, :], s["ring"][k]).then_inc(z_loaded[k], 16)

                def load_values(n, k):
                    wait(ctx_ready, n - 1)
                    sp.dma_start(vs[k][:, :, :], s["vst"][bass.ds(n // TT, 1)].rearrange("b p j f -> p (b j) f")).then_inc(v_loaded[k], 16)

                def load_residual(n, k):
                    wait(out_ready, n - 1)
                    b, t = place(n)
                    sp.dma_start(res[k][:, :], s["tok"][b, t, :].rearrange("b t f -> (b t) f")).then_inc(res_loaded[k], 16)

                def store(n, k):
                    wait(out_ready, n + 1)
                    b, t = place(n)
                    sp.dma_start(s["tok2"][b, t, :].rearrange("b t f -> (b t) f"), o[k][:, :]).then_inc(stored[k], 16)

                def step(n, k, more=True):
                    load_xs(n + 2, k)
                    if more:
                        load_queries(n + 1, 1 - k)
                        load_window(n + 1, 1 - k)
                    if not isinstance(n, int) or n > 2:
                        store(n - 3, 1 - k)
                    load_values(n, k)
                    if not isinstance(n, int) or n > 0:
                        load_residual(n - 1, 1 - k)

                sp.wait_ge(ready0, 1)
                load_xs(0, 0)
                load_xs(1, 1)
                load_queries(0, 0)
                load_window(0, 0)
                for n in range(4):
                    step(n, n % 2)
                with sp.Fori(2, N // 2 - 1) as m:
                    step(2 * m, 0)
                    step(2 * m + 1, 1)
                step(N - 2, 0)
                step(N - 1, 1, more=False)
                load_residual(N - 1, 1)
                for n in range(N - 3, N):
                    store(n, n % 2)
                for q in range(2):
                    sp.wait_ge(stored[q], 16 * (N // 2))

            @block.gpsimd
            def _(pool):
                def keys(b, slot):
                    pool.dma_start(kst[0:64, slot, :, :].bitcast(F32), s["kst"][b].rearrange("b r h t -> r (b h) t")).then_inc(kst_loaded, 16)

                def skew(n, k):
                    at_least(pool, z_loaded[k], 16 * (n // 2))
                    wait_apart(pool, band_done, n + 1, passed)
                    diag = bass.AP(s["ring"].tensor, k * TP * HEADS * WIN, [[HEADS * WIN + 1, TP], [WIN, HEADS], [1, NR]])
                    pool.dma_start(diag, band[k][:, :, :]).then_inc(ring_written[k], 16)

                def skews(b, first):
                    with pool.Fori(first, TT // 2) as jj:
                        skew(b * TT + 2 * jj, 0)
                        skew(b * TT + 2 * jj + 1, 1)

                pool.wait_ge(ready0, 1)
                keys(slice(0, 1), slice(0, 1))
                skew(0, 0)
                skew(1, 1)
                pool.wait_ge(scores_ready, 1)
                keys(slice(1, 2), slice(1, 2))
                skews(0, 1)
                with pool.Fori(1, NB - 1) as b:
                    skew(b * TT, 0)
                    skew(b * TT + 1, 1)
                    wait_apart(pool, kst_loaded, 16 * (b + 1), passed)
                    wait_apart(pool, scores_ready, 4 * TT * b + 1, passed)
                    keys(bass.ds(b + 1, 1), bass.ds((b + 1) % 2, 1))
                    skews(b, 1)
                skews(NB - 1, 0)

            @block.tensor
            def _(pe):
                def scores(n, k, h):
                    if h == 0:
                        pe.wait_ge(qst_loaded[k], 16 * (n // 2 + 1))
                        pe.wait_ge(kst_loaded, 16 * (n // TT + 1))
                    at_least(pe, exp_done, 4 * n + h - 1)
                    slot = (n // TT) % 2

                    def ks(a, b_):
                        return kst[:, bass.ds(slot, 1), h, a:b_].rearrange("p a n -> p (a n)")

                    nc.tensor.matmul(pss[h % 2][0:TP, REL:512], qst[k][:, h, :], ks(0, 512 - REL), start=True, stop=True)
                    nc.tensor.matmul(pss[h % 2][0:TP, 512:REL + T], qst[k][:, h, :], ks(512 - REL, T), start=True, stop=True).then_inc(scores_ready, 1)

                def transposes(n, h):
                    for a in range(2):
                        if a == 0:
                            pe.wait_ge(exp_done, 4 * n + h + 1)
                        at_least(pe, tr_taken[a], 4 * n + h)
                        for i in range(4):
                            mm = nc.tensor.transpose(pst[a][0:TP, i * TP:(i + 1) * TP], p[h][:, (4 * a + i) * TP:(4 * a + i + 1) * TP], w.ident[0:TP, 0:TP])
                        mm.then_inc(tr_ready[a], 1)

                def context(n, k, c):
                    if c == 0:
                        pe.wait_ge(tr_taken[0], 4 * n + 4)
                        pe.wait_ge(tr_taken[1], 4 * n + 4)
                        pe.wait_ge(v_loaded[k], 16 * (n // 2 + 1))
                        at_least(pe, ctx_taken, n)
                    for i in range(2 * c, 2 * c + 2):
                        for h in range(HEADS):
                            mm = nc.tensor.matmul(pso[32 * h:32 * h + HD, 0:TP], vs[k][:, i, h * HD:(h + 1) * HD],
                                                  pt[k][:, h, i, :], start=(i == 0), stop=(i == TT - 1))
                    if c == TT // 2 - 1:
                        mm.then_inc(ctx_ready, 1)

                def reciprocals(n, k):
                    pe.wait_ge(rinv_ready, n + 1)
                    pe.wait_ge(band_done, min(n + 5, N + 2) if isinstance(n, int) else n + 5)
                    at_least(pe, out_ready, n)
                    nc.tensor.matmul(psb[0:112, 0:TP], rinv[k][:, :, :].rearrange("p h d -> p (h d)")[:, 0:112], w.ident[0:TP, 0:TP],
                                     start=True, stop=True).then_inc(rb_ready, 1)

                def project_out(n):
                    pe.wait_ge(ctxn_ready, n + 1)
                    nc.tensor.matmul(psb[0:TP, 384:384 + D], ctxn[:, :], w.wo[:, :], start=True, stop=True).then_inc(proj_ready, 1)

                def band_terms(n, k):
                    pe.wait_ge(xs_loaded[k], 16 * (n // 2 + 1))
                    at_least(pe, band_done, n)
                    at_least(pe, out_ready, n - 4)
                    nc.tensor.matmul(psb[0:TP, 128:128 + HEADS * NR], xs[k][:, :], w.gpos[:, :, :].rearrange("p h r -> p (h r)"),
                                     start=True, stop=True).then_inc(band_ready, 1)

                def step(n, k, new, last, older):
                    for h in range(HEADS):
                        if new:
                            scores(n, k, h)
                        if h < 2 and last:
                            transposes(n - 1, 2 + h)
                        if h >= 2 and new:
                            transposes(n, h - 2)
                        if h == 1 and new:
                            band_terms(n + 2, k)
                        if h == 2 and older:
                            reciprocals(n - 2, k)
                        if h < 2 and older:
                            context(n - 2, k, 2 + h)
                        if h >= 2 and last:
                            context(n - 1, 1 - k, h - 2)
                        if h == 3 and older:
                            project_out(n - 2)

                pe.wait_ge(ready0, 1)
                band_terms(0, 0)
                band_terms(1, 1)
                pairs(pe, step)

            @block.vector
            def _(dve):
                v = nc.vector

                def window_and_max(n, k, h):
                    if h == 0:
                        dve.wait_ge(z_loaded[k], 16 * (n // 2 + 1))
                    dve.wait_ge(scores_ready, 4 * n + h + 1)
                    win = pss[h % 2][0:TP, bass.ds((n % TT) * TP, WIN)]
                    v.tensor_tensor(win, win, z[k][:, h, :], ALU.add).then_inc(window_added, 1)
                    dve.wait_ge(window_added, 4 * n + h + 1)
                    v.tensor_reduce(nmax[:, h:h + 1], pss[h % 2][0:TP, REL:REL + T], AX.X, ALU.max, negate=True).then_inc(nmax_ready, 1)

                def copy_out(n, k, h):
                    dve.wait_ge(tr_ready[1], 4 * n + h + 1)
                    at_least(dve, ctx_ready, n - 1)
                    v.tensor_copy(pt[k][:, h, 4:8, :].rearrange("p i t -> p (i t)"), pst[1][0:TP, 0:4 * TP]).then_inc(tr_taken[1], 1)

                def invert(n, k):
                    dve.wait_ge(exp_done, 4 * n + 4)
                    at_least(dve, rb_ready, n - 1)
                    v.reciprocal(rinv[k][:, :, :], sums_[k][:, :].rearrange("p (h a) -> p h a", a=1).to_broadcast([TP, HEADS, 32])).then_inc(rinv_ready, 1)

                def normalise(n):
                    dve.wait_ge(ctx_taken, n + 1)
                    dve.wait_ge(rb_ready, n + 1)
                    v.tensor_tensor(ctxn[0:112, :], ctxs[:, :], psb[0:112, 0:TP], ALU.mult).then_inc(ctxn_ready, 1)

                def residual(n, k):
                    dve.wait_ge(proj_ready, n + 1)
                    dve.wait_ge(res_loaded[k], 16 * (n // 2 + 1))
                    at_least(dve, stored[k], 16 * (n // 2))
                    v.tensor_tensor(o[k][:, :], psb[0:TP, 384:384 + D], res[k][:, :], ALU.add).then_inc(out_ready, 1)

                def band_out(n, k):
                    dve.wait_ge(band_ready, n + 1)
                    src = psb[0:TP, 128:128 + HEADS * NR].rearrange("p (h r) -> p h r", h=HEADS)
                    v.tensor_tensor(farband[:, :, :], w.bandstep[:, :].rearrange("p (a r) -> p a r", a=1).to_broadcast([TP, HEADS, NR]),
                                    src[:, :, 0:1].to_broadcast([TP, HEADS, NR]), ALU.mult).then_inc(far_ready, 1)
                    dve.wait_ge(far_ready, n + 1)
                    at_least(dve, ring_written[k], 16 * (n // 2))
                    v.tensor_tensor(band[k][:, :, :], src, farband[:, :, :], ALU.subtract).then_inc(band_done, 1)

                def step(n, k, new, last, older):
                    if new:
                        window_and_max(n, k, 0)
                    if last:
                        invert(n - 1, 1 - k)
                    if new:
                        window_and_max(n, k, 1)
                    if last:
                        copy_out(n - 1, 1 - k, 3)
                    if new:
                        band_out(n + 2, k)
                    if new:
                        window_and_max(n, k, 2)
                    if older:
                        normalise(n - 2)
                    if new:
                        window_and_max(n, k, 3)
                    if older:
                        residual(n - 2, k)

                for q in range(2):
                    v.memset(pss[q][:, :], 0.0)
                    v.memset(xs[q][D:D + 1, :], 1.0)
                v.memset(pso[:, :], 0.0)
                v.memset(ctxn[96:128, :], 1.0)
                for q in range(2):
                    for h in range(HEADS):
                        last = v.tensor_copy(kst[64:96, q, h, :], w.step[64:96, :])
                last.then_inc(ready0, 1)
                band_out(0, 0)
                band_out(1, 1)
                pairs(dve, step)

            @block.scalar
            def _(act):
                def softmax(n, k, h):
                    act.wait_ge(nmax_ready, 4 * n + h + 1)
                    at_least(act, tr_ready[1], 4 * n + h - 3)
                    nc.scalar.activation(p[h][:, :], pss[h % 2][0:TP, REL:REL + T], ACT.Exp, bias=nmax[:, h:h + 1],
                                         scale=1.0, accum_out=sums_[k][:, h:h + 1]).then_inc(exp_done, 1)

                def copy_out(n, k, h, halves):
                    if h == 0:
                        at_least(act, ctx_ready, n - 1)
                    for a in halves:
                        act.wait_ge(tr_ready[a], 4 * n + h + 1)
                        nc.scalar.activation(pt[k][:, h, 4 * a:4 * a + 4, :].rearrange("p i t -> p (i t)"), pst[a][0:TP, 0:4 * TP],
                                             ACT.Copy).then_inc(tr_taken[a], 1)

                def context_out(n):
                    act.wait_ge(ctx_ready, n + 1)
                    at_least(act, ctxn_ready, n)
                    nc.scalar.activation(ctxs[:, :], pso[0:112, 0:TP], ACT.Copy).then_inc(ctx_taken, 1)

                def step(n, k, new, last, older):
                    for h in range(HEADS):
                        if h == 2 and older:
                            context_out(n - 2)
                        if h < 2 and last:
                            copy_out(n - 1, 1 - k, 2 + h, (0, 1) if h == 0 else (0,))
                        if h >= 2 and new:
                            copy_out(n, k, h - 2, (0, 1))
                        if new:
                            softmax(n, k, h)

                pairs(act, step)


def experts(nc, w, s, out, NB):
    G = NB * TT // 4
    GT = 4
    GN = GT * TP
    with ExitStack() as ctx:
        def sb(name, shape, dt=F32):
            return ctx.enter_context(nc.sbuf_tensor(name, shape, dt))

        def sem(name):
            return ctx.enter_context(nc.semaphore(name))

        passed = sem("experts_passed")

        def pb(name):
            return ctx.enter_context(nc.psum_tensor(name, [128, 512], F32))

        x = [sb(f"ex{q}", [TP, GT, D]) for q in range(2)]
        res = [sb(f"eres{q}", [TP, GT, D]) for q in range(2)]
        xc = sb("exc", [TP, GT, D])
        sq = sb("esq", [TP, GT, D])
        st = sb("est", [TP, 5, GT])
        y = [sb(f"ey{q}", [TP, GT, 2, D]) for q in range(2)]
        xh = sb("xh", [128, GN], F32R)
        xa = [sb(f"xa{q}", [128, GN], F32R) for q in range(2)]
        xb = [sb(f"xb{q}", [104, GN], F32R) for q in range(2)]
        ge = [sb(f"ge{q}", [NPAIR, GN], BF16) for q in range(2)]
        mk = [sb(f"mk{q}", [NE, GN], F32R) for q in range(2)]
        hs = [sb(f"hs{i}", [HID, GN]) for i in range(4)]
        os_ = [sb(f"os{q}", [128, GN]) for q in range(2)]
        o = [sb(f"eo{q}", [TP, GT, D]) for q in range(2)]
        psy, psg, psr, psf = pb("psy"), pb("psg"), pb("psr"), pb("psf")
        psh = [pb(f"psh{q}") for q in range(2)]
        pso = [pb(f"epso{q}") for q in range(2)]

        x_loaded = [sem(f"ex_loaded{q}") for q in range(2)]
        r_loaded = [sem(f"er_loaded{q}") for q in range(2)]
        stored = [sem(f"out_stored{q}") for q in range(2)]
        ones_set = sem("eones_set")
        chain = sem("echain")
        vars_ = sem("evars")
        rstds = sem("erstds")
        y_ready = sem("ey_ready")
        yt_ready = sem("eyt_ready")
        xh_ready = sem("xh_ready")
        xl_ready = sem("xl_ready")
        gate_ready = sem("gate_ready")
        ge_ready = sem("ge_ready")
        rank_ready = sem("rank_ready")
        masks_ready = sem("masks_ready")
        hid_ready = sem("hid_ready")
        hid_done = sem("hid_done")
        exp_ready = sem("exp_ready")
        os_ready = sem("os_ready")
        fold_ready = sem("fold_ready")
        o_ready = sem("o_ready")
        NLINK = 5

        tok2 = s["tok2"].rearrange("b (g j p) f -> (b g) p j f", j=GT, p=TP)
        outv = out.rearrange("b (g j p) f -> (b g) p j f", j=GT, p=TP)

        def at_least(eng, semaphore, value):
            if not isinstance(value, int) or value > 0:
                eng.wait_ge(semaphore, value)

        def steps(eng, step):
            step(0, 0, True, False, False, True)
            step(1, 1, True, True, False, True)
            step(2, 0, True, True, True, True)
            step(3, 1, True, True, True, True)
            with eng.Fori(2, G // 2 - 1) as m:
                for k in range(2):
                    step(2 * m + k, k, True, True, True, True)
            step(G - 2, 0, True, True, True, True)
            step(G - 1, 1, True, True, True, False)
            step(G, 0, False, True, True, False)
            step(G + 1, 1, False, False, True, False)

        with nc.Block() as block:
            @block.sync
            def _(sp):
                def load_x(g, q):
                    at_least(sp, y_ready, g - 1)
                    sp.dma_start(x[q][:, :, :], tok2[bass.ds(g, 1)].rearrange("g p j f -> p (g j) f")).then_inc(x_loaded[q], 16)

                def load_residual(g, q):
                    at_least(sp, o_ready, g - 1)
                    sp.dma_start(res[q][:, :, :], tok2[bass.ds(g, 1)].rearrange("g p j f -> p (g j) f")).then_inc(r_loaded[q], 16)

                def store(g, q):
                    sp.wait_ge(o_ready, g + 1)
                    sp.dma_start(outv[bass.ds(g, 1)].rearrange("g p j f -> p (g j) f"), o[q][:, :, :]).then_inc(stored[q], 16)

                def step(g, k, new, running, finishing, ahead):
                    if ahead:
                        load_x(g + 1, 1 - k)
                    if running:
                        load_residual(g - 1, 1 - k)
                    if finishing:
                        store(g - 2, k)

                load_x(0, 0)
                steps(sp, step)
                for q in range(2):
                    sp.wait_ge(stored[q], 16 * (G // 2))

            @block.vector
            def _(dve):
                v = nc.vector

                def normalise(g, q):
                    n = [0]

                    def link(ins):
                        n[0] += 1
                        ins.then_inc(chain, 1)
                        dve.wait_ge(chain, g * NLINK + n[0])

                    dve.wait_ge(x_loaded[q], 16 * (g // 2 + 1))
                    at_least(dve, yt_ready, g - 1)
                    link(v.tensor_reduce(st[:, 0, :], x[q][:, :, :], AX.X, ALU.add))
                    link(v.tensor_scalar(st[:, 1, :], st[:, 0, :], -1.0 / D, None, ALU.mult))
                    link(v.tensor_tensor(xc[:, :, :], x[q][:, :, :], st[:, 1, :].rearrange("p (n a) -> p n a", a=1).to_broadcast([TP, GT, D]), ALU.add))
                    link(v.tensor_tensor(sq[:, :, :], xc[:, :, :], xc[:, :, :], ALU.mult))
                    link(v.tensor_reduce(st[:, 2, :], sq[:, :, :], AX.X, ALU.add))
                    v.tensor_scalar(st[:, 4, :], st[:, 2, :], 1.0 / D, EPS, ALU.mult, ALU.add).then_inc(vars_, 1)
                    dve.wait_ge(rstds, g + 1)
                    rstd = st[:, 3, :].rearrange("p (n a) -> p n a", a=1).to_broadcast([TP, GT, D])
                    for t in range(2):
                        last = v.tensor_tensor(y[q][:, :, t, :], xc[:, :, :], rstd, ALU.mult)
                    last.then_inc(y_ready, 1)

                def low_half(g, q):
                    dve.wait_ge(xh_ready, g + 1)
                    at_least(dve, hid_ready, NE * (g - 1))
                    v.tensor_tensor(xa[q][64:128, :], psy[64:128, 0:GN], xh[64:128, :].bitcast(F32), ALU.subtract).then_inc(xl_ready, 1)

                def gate(g, q):
                    dve.wait_ge(gate_ready, g + 1)
                    v.tensor_scalar(ge[q][:, :], psg[0:NPAIR, 0:GN], 0.0, None, ALU.is_ge).then_inc(ge_ready, 1)

                def masks(g, q):
                    dve.wait_ge(rank_ready, g + 1)
                    v.tensor_scalar(xb[q][96:96 + NE, :], psr[0:NE, 0:GN], w.thr[:, 0:1], None, ALU.is_ge)
                    v.tensor_scalar(mk[q][:, :], psr[0:NE, 0:GN], w.thr[:, 0:1], None, ALU.is_lt).then_inc(masks_ready, 1)

                def residual(g, q):
                    dve.wait_ge(fold_ready, g + 1)
                    dve.wait_ge(r_loaded[q], 16 * (g // 2 + 1))
                    at_least(dve, stored[q], 16 * (g // 2))
                    v.tensor_tensor(o[q][:, :, :], psf[0:TP, 0:GT * D].rearrange("p (j f) -> p j f", j=GT), res[q][:, :, :], ALU.add).then_inc(o_ready, 1)

                def step(g, k, new, running, finishing, ahead):
                    if new:
                        low_half(g, k)
                    if ahead:
                        normalise(g + 1, 1 - k)
                    if finishing:
                        residual(g - 2, k)
                    if new:
                        gate(g, k)
                        masks(g, k)

                for q in range(2):
                    v.memset(xb[q][D:96, :].bitcast(F32), 0.0).then_inc(ones_set, 1)
                dve.wait_ge(ones_set, 2)
                for q in range(2):
                    v.memset(xb[q][D:D + 2, :].bitcast(F32), 1.0).then_inc(ones_set, 1)
                normalise(0, 0)
                steps(dve, step)

            @block.gpsimd
            def _(pool):
                def power(g):
                    wait_apart(pool, vars_, g + 1, passed)
                    nc.gpsimd.tensor_tensor(st[:, 3, :], st[:, 4, :], w.mhalf[0:TP, 0:GT], ALU.pow).then_inc(rstds, 1)

                def step(g, k, new, running, finishing, ahead):
                    if ahead:
                        power(g + 1)

                power(0)
                steps(pool, step)

            @block.scalar
            def _(act):
                def high_half(g, q):
                    act.wait_ge(yt_ready, g + 1)
                    at_least(act, xl_ready, g)
                    at_least(act, hid_ready, NE * (g - 1))
                    nc.scalar.activation(xh[64:128, :], psy[64:128, 0:GN], ACT.Copy)
                    nc.scalar.activation(xa[q][0:D, :], psy[0:D, 0:GN], ACT.Copy)
                    nc.scalar.activation(xb[q][0:D, :], psy[0:D, 0:GN], ACT.Copy).then_inc(xh_ready, 1)

                def gelus(g):
                    for e in range(NE):
                        act.wait_ge(hid_ready, g * NE + e + 1)
                        nc.scalar.activation(hs[e % 4][:, :], psh[e % 2][:, 0:GN], ACT.Gelu).then_inc(hid_done, 1)

                def sums_out(g, q):
                    act.wait_ge(exp_ready, g + 1)
                    at_least(act, fold_ready, g - 1)
                    nc.scalar.activation(os_[q][:, :], pso[q][:, 0:GN], ACT.Copy).then_inc(os_ready, 1)

                def step(g, k, new, running, finishing, ahead):
                    if finishing:
                        sums_out(g - 2, k)
                    if new:
                        high_half(g, k)
                    if running:
                        gelus(g - 1)

                steps(act, step)

            @block.tensor
            def _(pe):
                def transposes(g, q):
                    pe.wait_ge(y_ready, g + 1)
                    at_least(pe, xh_ready, g)
                    at_least(pe, xl_ready, g)
                    for j in range(GT):
                        mm = nc.tensor.transpose(psy[:, j * TP:(j + 1) * TP], y[q][:, j, :, :].rearrange("p a f -> p (a f)"), w.ident[0:TP, 0:TP])
                    mm.then_inc(yt_ready, 1)

                def differences(g, q):
                    pe.wait_ge(xh_ready, g + 1)
                    pe.wait_ge(xl_ready, g + 1)
                    nc.tensor.matmul(psg[:, 0:GN], w.wga[:, :], xa[q][:, :], start=True, stop=False)
                    nc.tensor.matmul(psg[:, 0:GN], w.wgb[:, :], xb[q][0:D + 2, :], start=False, stop=True).then_inc(gate_ready, 1)

                def ranks(g, q):
                    wait_apart(pe, ge_ready, g + 1, passed)
                    nc.tensor.matmul(psr[0:NE, 0:GN], w.rank[:, :], ge[q][:, :], start=True, stop=True).then_inc(rank_ready, 1)

                def biases(g, q):
                    pe.wait_ge(masks_ready, g + 1)
                    at_least(pe, os_ready, g - 1)
                    nc.tensor.matmul(pso[q][:, 0:GN], w.b2[:, :], mk[q][:, :], start=True, stop=False)

                def hidden(g, q, e):
                    at_least(pe, hid_done, g * NE + e - 1)
                    nc.tensor.matmul(psh[e % 2][:, 0:GN], w.w1a[:, e, :], xa[q][:, :], start=True, stop=False)
                    nc.tensor.matmul(psh[e % 2][:, 0:GN], w.w1b[:, e, :], xb[q][:, :], start=False, stop=True).then_inc(hid_ready, 1)

                def outputs(g, q, e):
                    pe.wait_ge(hid_done, g * NE + e + 1)
                    mm = nc.tensor.matmul(pso[q][64 * (e % 2):64 * (e % 2) + 64, 0:GN], w.w2[:, e, :], hs[e % 4][:, :],
                                          start=False, stop=(e >= NE - 2))
                    if e == NE - 1:
                        mm.then_inc(exp_ready, 1)

                def folds(g, q):
                    pe.wait_ge(os_ready, g + 1)
                    at_least(pe, o_ready, g)
                    for j in range(GT):
                        mm = nc.tensor.matmul(psf[0:TP, j * D:(j + 1) * D], os_[q][:, j * TP:(j + 1) * TP], w.fold[:, :], start=True, stop=True)
                    mm.then_inc(fold_ready, 1)

                def step(g, k, new, running, finishing, ahead):
                    if new:
                        transposes(g, k)
                    if running:
                        biases(g - 1, 1 - k)
                        hidden(g - 1, 1 - k, 0)
                        hidden(g - 1, 1 - k, 1)
                    if finishing:
                        folds(g - 2, k)
                    for e2 in range(2, NE + 2, 2):
                        if new and e2 == 4:
                            differences(g, k)
                        if new and e2 == 6:
                            ranks(g, k)
                        for e in (e2, e2 + 1):
                            if running and e < NE:
                                hidden(g - 1, 1 - k, e)
                        for e in (e2 - 2, e2 - 1):
                            if running:
                                outputs(g - 1, 1 - k, e)

                pe.wait_ge(ones_set, 4)
                steps(pe, step)


def constants():
    f = np.float32

    def encoding(n):
        div = np.exp(np.arange(0, D, 2, dtype=f) * f(-np.log(10000.0) / D)).astype(f)
        ang = np.arange(n, dtype=f)[:, None] * div
        out = np.zeros((n, D), f)
        out[:, 0::2], out[:, 1::2] = np.sin(ang), np.cos(ang)
        return out

    t = np.arange(T)
    theta = BLK * np.arange(NBLK) + REL - 2
    step = (t[None, :] < theta[:, None]).astype(f)
    tau, r = np.arange(TP)[:, None], np.arange(NR)[None, :]
    off = np.zeros((NE, NE, HID), f)
    off[np.arange(NE), np.arange(NE), :] = OFF
    rank = np.zeros((NPAIR, NE), f)
    m = 0
    for a in range(NE - 1):
        for b in range(a + 1, NE):
            rank[m, a], rank[m, b] = -1, 1
            m += 1
    shift = np.zeros((NP_, NT, NODES), f)
    for i in range(NT):
        shift[np.arange(NP_), i, i * NP_ + np.arange(NP_)] = 1
    return dict(
        c_ident=np.eye(128, dtype=f), c_iota=np.tile(np.arange(NODES, dtype=f), (128, 1)),
        c_shift=shift.reshape(NP_, -1), c_pe=np.tile(encoding(NODES).T, (2, 1)),
        c_rel=np.concatenate([encoding(NR).T, np.ones((1, NR), f)]),
        c_headmask=np.repeat(np.eye(HEADS, dtype=f), HD, axis=0),
        c_blkmask=np.repeat((t[None, :] // BLK == np.arange(NBLK)[:, None]).astype(f), HEADS, axis=0),
        c_step=np.concatenate([step, step]),
        c_bandstep=(tau + r - REL < BLK * (tau // BLK) + REL - 2).astype(f),
        c_off=off.reshape(NE, -1), c_rank=rank, c_thr=(np.arange(NE, dtype=f) - 5)[:, None],
        c_fold=np.concatenate([np.eye(D, dtype=f)] * 2),
        c_rows4=np.array([[1, 0, 1, 0], [0, 1, 1, 0], [1, 0, 0, 1], [0, 1, 0, 1]], f),
    )


def layouts(a):
    NB = a["x"].shape[0]

    def by_dim(m):
        return np.ascontiguousarray(m.reshape(HEADS, HD, -1).transpose(1, 0, 2).reshape(D, -1))

    x = a["x"].reshape(NB, CH, GRID, PATCH, GRID, PATCH).transpose(1, 3, 5, 0, 2, 4).reshape(2, KP, NB, NODES)
    return dict(
        x_patch=np.ascontiguousarray(x.transpose(1, 2, 0, 3)), txt=a["txt"],
        w_embed=a["L0_tok_W_embed"], b_embed=a["L0_tok_b_embed"], w_gcn=a["L0_tok_W_gcn"], b_gcn=a["L0_tok_b_gcn"],
        w_out=a["L0_tok_W_out"], b_out=a["L0_tok_b_out"], edge_index=a["L0_tok_edge_index"],
        ln_gamma=a["L0_attn_ln_gamma"], ln_beta=a["L0_attn_ln_beta"],
        wq=a["L0_attn_Wq"], wq_t=np.ascontiguousarray(by_dim(a["L0_attn_Wq"]).T), bq=a["L0_attn_bq"],
        bq_perm=by_dim(a["L0_attn_bq"]).ravel(), u_perm=by_dim(a["L0_attn_u_bias"]).ravel(),
        wk_t=np.ascontiguousarray(by_dim(a["L0_attn_Wk"]).T), bk=by_dim(a["L0_attn_bk"]).ravel(),
        wv_t=np.ascontiguousarray(a["L0_attn_Wv"].T), bv=a["L0_attn_bv"],
        wpos_t=np.ascontiguousarray(a["L0_attn_Wpos"].T), bpos=a["L0_attn_bpos"],
        wo_t=np.ascontiguousarray(a["L0_attn_Wo"].T), bo=a["L0_attn_bo"], v_bias=a["L0_attn_v_bias"],
        wg=a["L0_ffn_Wg"], bg=a["L0_ffn_bg"], w1=a["L0_ffn_W1"], b1=a["L0_ffn_b1"], w2=a["L0_ffn_W2"], b2=a["L0_ffn_b2"],
    )


def build(nc, ins, out, NB):
    s = scratch_tensors(nc, NB)
    with ExitStack() as ctx:
        w = alloc_weights(nc, ctx)
        prepare(nc, w, ins, s, NB)
        tokens(nc, w, ins, s, NB)
        project(nc, w, s, NB)
        attend(nc, w, s, NB)
        experts(nc, w, s, out, NB)


def kernel(**inputs):
    import concourse.bacc as bacc
    from concourse.bass_utils import run_bass_kernel_spmd

    nc = bacc.Bacc("TRN2", target_bir_lowering=False, num_devices=1)
    a = {k: np.asarray(v) for k, v in inputs.items()}
    arrays = {**layouts(a), **constants()}
    import ml_dtypes
    arrays["c_shift"] = arrays["c_shift"].astype(ml_dtypes.bfloat16)
    arrays = {f"in_{k}": np.ascontiguousarray(v) for k, v in arrays.items()}
    ins = {k[3:]: nc.dram_tensor(k, v.shape, mybir.dt.from_np(v.dtype), kind="ExternalInput").ap() for k, v in arrays.items()}
    NB = a["x"].shape[0]
    out = nc.dram_tensor("out_tokens", (NB, T, D), F32, kind="ExternalOutput").ap()
    build(nc, ins, out, NB)
    r = run_bass_kernel_spmd(nc, [arrays], core_ids=[0])
    return r.results[0]["out_tokens"]
```

```python
from contextlib import ExitStack

import concourse.bass as bass
import numpy as np
from concourse import mybir

F32 = mybir.dt.float32
F32R = mybir.dt.float32r
BF16 = mybir.dt.bfloat16
I32 = mybir.dt.int32
ACT = mybir.ActivationFunctionType
ALU = mybir.AluOpType
AX = mybir.AxisListType

GRID, PATCH, CH = 28, 8, 3
NODES = GRID * GRID
TXT = 128
T = NODES + TXT
D = 64
HEADS, HD = 4, 16
TP, TT = 114, 8
NP_, NT = 112, 7
NH = NODES // 2
TH = T // 2
KIN = CH * PATCH * PATCH
KP = KIN // 2
EC, EP = 24, 126
REL = 30
NR = 2 * REL + 1
BLK = TP // 2
NBLK = T // BLK
WIN = TP + 2 * REL
SROWS = 64 + 2 * NBLK
NE, HID = 8, 128
NPAIR = NE * (NE - 1) // 2
EPS = 1e-5
OFF = -float(2.0 ** 100)


def wait_apart(eng, semaphore, value, passed):
    eng.wait_ge(semaphore, value)
    eng.sem_inc(passed, 1)


def scratch_tensors(nc, NB):
    def dram(name, shape, dt):
        return nc.dram_tensor(name, shape, dt, kind="Internal").ap()

    return dict(
        tok=dram("tok", (NB, T, D), F32),
        xt=dram("xt", (NB + 1, D, T), F32),
        qst=dram("qst", (NB, SROWS, HEADS, T), F32),
        kst=dram("kst", (NB, 64, HEADS, T), F32),
        vst=dram("vst", (NB, TP, TT, D), F32),
        ring=dram("ring", (2, TP, HEADS, WIN), F32),
        tok2=dram("tok2", (NB, T, D), F32),
    )


class W:
    pass


def alloc_weights(nc, ctx):
    w = W()

    def sb(name, shape, dt=F32):
        return ctx.enter_context(nc.sbuf_tensor(name, shape, dt))

    w.ident = sb("ident", [128, 128])
    w.adj = sb("adj", [NP_, NT, NODES], F32R)
    w.dinv = sb("dinv", [NP_, NT])
    w.invdeg = sb("invdeg", [NP_, NT])
    w.sq4 = sb("sq4", [4, NODES], F32R)
    w.bg4 = sb("bg4", [4, 4, 128], F32R)
    w.we = sb("we", [KP, 2, D])
    w.etab = sb("etab", [128, NODES])
    w.wg = sb("wg", [128, 4, 128])
    w.lng = sb("lng", [D, 1])
    w.lnb = sb("lnb", [D, 1])
    w.wqk = sb("wqk", [D + 1, 128])
    w.wdp = sb("wdp", [D + 1, 64])
    w.wv = sb("wv", [D + 1, D])
    w.gpos = sb("gpos", [D + 1, HEADS, NR])
    w.blkmask = sb("blkmask", [64, T])
    w.step = sb("step", [96, T])
    w.bandstep = sb("bandstep", [TP, NR])
    w.wo = sb("wo", [128, D])
    w.w1a = sb("w1a", [128, NE, HID], F32R)
    w.w1b = sb("w1b", [104, NE, HID], F32R)
    w.wga = sb("wga", [128, 128], F32R)
    w.wgb = sb("wgb", [66, 128], F32R)
    w.rank = sb("rank", [NPAIR, NE], BF16)
    w.thr = sb("thr", [NE, 1])
    w.w2 = sb("w2", [HID, NE, D])
    w.b2 = sb("b2", [NE, 128], F32R)
    w.fold = sb("fold", [128, D])
    w.mhalf = sb("mhalf", [128, TT])
    return w


def prepare(nc, w, ins, s, NB):
    A = ins
    with ExitStack() as ctx:
        def sb(name, shape, dt=F32):
            return ctx.enter_context(nc.sbuf_tensor(name, shape, dt))

        def pb(name, shape=(128, 512)):
            return ctx.enter_context(nc.psum_tensor(name, list(shape), F32))

        def sem(name):
            return ctx.enter_context(nc.semaphore(name))

        eidx = sb("eidx", [EP, 2, EC], I32)
        eidf = sb("eidf", [EP, 2, EC])
        iota = sb("iota", [128, NODES])
        onehot = sb("onehot", [EP, 2, EC, NODES], BF16)
        shift = sb("shift", [NP_, NT, NODES], BF16)
        oneb = sb("oneb", [EP, 4], BF16)
        b128 = sb("b128", [128, 1])
        pe = sb("pe", [128, NODES])
        deg = sb("deg", [NP_, NT])
        sqr = sb("sqr", [4, NODES])
        sqh = sb("sqh", [4, NODES], F32R)
        sql = sb("sql", [4, NODES])
        root = sb("root", [NP_, NT])
        diag = sb("diag", [NP_, NODES])
        ones4 = sb("ones4", [NP_, 4])
        bgr = sb("bgr", [4, 4 * 128])
        bgh = sb("bgh", [4, 4 * 128], F32R)
        bgl = sb("bgl", [4, 4 * 128])
        rm = sb("rm", [4, 4])
        wpt = sb("wpt", [D + 1, D])
        relt = sb("relt", [D + 1, NR])
        hm = sb("hm", [D, HEADS])
        pos = sb("pos", [D, NR])
        posd = sb("posd", [D, HEADS, NR])
        wqn = sb("wqn", [D, D + 1])
        vb = sb("vb", [D, 1])
        qb = sb("qb", [D + 1, 3, D])
        w1f = sb("w1f", [128, NE, HID])
        b1r = sb("b1r", [96 + NE, NE, HID])
        gw = sb("gw", [128, NE])
        gbr = sb("gbr", [66, NE])
        gd = sb("gd", [128, 128])
        b2f = sb("b2f", [NE, 2, D])
        zero = sb("zero", [TP, HEADS * T])

        psc = [pb(f"psc{i}") for i in range(2)]
        psd = pb("psd")
        psq = [pb(f"psq{i}") for i in range(2)]
        psp = pb("psp")

        loaded = sem("loaded")
        edges_loaded = sem("edges_loaded")
        cleared = sem("cleared")
        zeroed = sem("zeroed")
        onehots = sem("onehots")
        counts_ready = sem("counts_ready")
        counts_taken = sem("counts_taken")
        deg_ready = sem("deg_ready")
        pos_ready = sem("pos_ready")
        posd_ready = sem("posd_ready")
        gpos_ready = sem("gpos_ready")
        degree_taken = sem("degree_taken")
        powered = sem("powered")
        diag_ready = sem("diag_ready")
        roots_ready = sem("roots_ready")
        dchain = sem("dchain")

        loads = [
            (w.ident[:, :], A["c_ident"]), (w.we[:, :, :], A["w_embed"].rearrange("(k p) n -> p k n", k=2)),
            (pe[:, :], A["c_pe"]), (b128[0:64, :], A["b_embed"].rearrange("(p a) -> p a", a=1)),
            (b128[64:128, :], A["b_embed"].rearrange("(p a) -> p a", a=1)),
            (w.lng[:, :], A["ln_gamma"].rearrange("(p a) -> p a", a=1)),
            (w.lnb[:, :], A["ln_beta"].rearrange("(p a) -> p a", a=1)),
            (w.wqk[0:D, 0:D], A["wq_t"]), (w.wqk[0:D, D:128], A["wk_t"]), (w.wv[0:D, :], A["wv_t"]),
            (w.wqk[D:D + 1, D:128], A["bk"].rearrange("(a n) -> a n", a=1)),
            (w.wv[D:D + 1, :], A["bv"].rearrange("(a n) -> a n", a=1)),
            (qb[D:D + 1, 0, :], A["bq_perm"].rearrange("(a n) -> a n", a=1)),
            (qb[D:D + 1, 1, :], A["u_perm"].rearrange("(a n) -> a n", a=1)),
            (w.blkmask[:, :], A["c_blkmask"]), (w.step[64:96, :], A["c_step"]), (w.bandstep[:, :], A["c_bandstep"]),
            (wpt[0:D, :], A["wpos_t"]), (wpt[D:D + 1, :], A["bpos"].rearrange("(a n) -> a n", a=1)),
            (relt[:, :], A["c_rel"]), (hm[:, :], A["c_headmask"]),
            (wqn[:, 0:D], A["wq"]), (wqn[:, D:D + 1], A["bq"].rearrange("(p a) -> p a", a=1)),
            (vb[:, :], A["v_bias"].rearrange("a h b d -> (a h b d)").rearrange("(p a) -> p a", a=1)),
            (w1f[0:D, :, :], A["w1"].rearrange("e d h -> d e h")), (w1f[D:128, :, :], A["w1"].rearrange("e d h -> d e h")),
            (b1r[64:65, :, :], A["b1"].rearrange("(a e) h -> a e h", a=1)),
            (b1r[96:96 + NE, :, :], A["c_off"].rearrange("p (e h) -> p e h", e=NE)),
            (gw[0:D, :], A["wg"]), (gw[D:128, :], A["wg"]), (gbr[64:65, :], A["bg"].rearrange("(a n) -> a n", a=1)),
            (w.thr[:, :], A["c_thr"]), (w.w2[:, :, :], A["w2"].rearrange("e h d -> h e d")),
            (b2f[:, 0, :], A["b2"]), (b2f[:, 1, :], A["b2"]), (w.fold[:, :], A["c_fold"]),
            (rm[:, :], A["c_rows4"]), (gd[0:NPAIR, 0:NE], A["c_rank"]),
        ]
        for l in range(3):
            loads += [(w.wg[64 * q:64 * q + 64, l, 64 * q:64 * q + 64], A["w_gcn"][l]) for q in range(2)]
            loads += [(bgr[:, l * 128 + 64 * q:l * 128 + 64 * q + 64], A["b_gcn"][l:l + 1, :].to_broadcast([4, D])) for q in range(2)]
        loads += [(w.wg[64 * q:64 * q + 64, 3, 64 * q:64 * q + 64], A["w_out"]) for q in range(2)]
        loads += [(bgr[:, 384 + 64 * q:448 + 64 * q], A["b_out"].rearrange("(a n) -> a n", a=1).to_broadcast([4, D])) for q in range(2)]
        loads += [(w.wo[32 * h:32 * h + HD, :], A["wo_t"][HD * h:HD * h + HD, :]) for h in range(HEADS)]
        loads += [(w.wo[112:113, :], A["bo"].rearrange("(a n) -> a n", a=1))]
        ALL = 16 * len(loads)

        with nc.Block() as block:
            @block.sync
            def _(sp):
                sp.dma_start(eidx[:, :, :], A["edge_index"].rearrange("a (p c) -> p a c", c=EC)).then_inc(edges_loaded, 16)
                sp.dma_start(iota[:, :], A["c_iota"]).then_inc(edges_loaded, 16)
                sp.dma_start(shift[:, :, :], A["c_shift"].rearrange("p (i n) -> p i n", i=NT)).then_inc(edges_loaded, 16)
                sp.wait_ge(cleared, 4)
                for dst, src in loads:
                    sp.dma_start(dst, src).then_inc(loaded, 16)
                sp.dma_start(s["tok"][:, NODES:T, :], A["txt"]).then_inc(zeroed, 16)
                sp.dma_start(s["ring"][0], zero[:, 0:HEADS * WIN].rearrange("p (h c) -> p h c", h=HEADS)).then_inc(zeroed, 16)
                sp.dma_start(s["ring"][1], zero[:, 0:HEADS * WIN].rearrange("p (h c) -> p h c", h=HEADS)).then_inc(zeroed, 16)
                sp.dma_start(s["xt"][NB], zero[0:D, 0:T]).then_inc(zeroed, 16)
                sp.wait_ge(zeroed, 64)
                sp.wait_ge(loaded, ALL)

            @block.gpsimd
            def _(pool):
                nc.gpsimd.memset(w.wg[:, :, :], 0.0).then_inc(cleared, 1)
                nc.gpsimd.memset(w.wo[:, :], 0.0).then_inc(cleared, 1)
                nc.gpsimd.memset(zero[:, :], 0.0).then_inc(cleared, 1)
                nc.gpsimd.memset(b1r[:, :, :], 0.0).then_inc(cleared, 1)
                nc.gpsimd.memset(w.mhalf[:, :], -0.5).then_inc(degree_taken, 1)
                pool.wait_ge(degree_taken, 2)
                nc.gpsimd.tensor_tensor(w.dinv[:, :], deg[:, :], w.mhalf[0:NP_, 0:NT], ALU.pow).then_inc(powered, 1)

            @block.tensor
            def _(pe_):
                pe_.wait_ge(loaded, ALL)
                nc.tensor.matmul(psp[0:D, 0:NR], wpt[:, :], relt[:, :], start=True, stop=True).then_inc(pos_ready, 1)
                pe_.wait_ge(posd_ready, 1)
                nc.tensor.matmul(psp[0:D + 1, 64:64 + HEADS * NR], wqn[:, :], posd[:, :, :], start=True, stop=True).then_inc(gpos_ready, 1)
                pe_.wait_ge(edges_loaded, 48)
                pe_.wait_ge(onehots, 2 * EC + 1)
                for i in range(NT):
                    for c in range(EC):
                        mm = nc.tensor.matmul(psd[0:NP_, 4 * i:4 * i + 4], onehot[:, 1, c, i * NP_:(i + 1) * NP_], oneb[:, :],
                                              start=(i == 0 and c == 0), stop=(c == EC - 1), skip_group_check=True)
                mm.then_inc(deg_ready, 1)
                for i in range(NT):
                    for a in range(2):
                        m = 2 * i + a
                        if m >= 2:
                            pe_.wait_ge(counts_taken, m - 1)
                        for c in range(EC):
                            nc.tensor.matmul(psc[a][0:NP_, 0:NH], onehot[:, 0, c, i * NP_:(i + 1) * NP_],
                                             onehot[:, 1, c, a * NH:(a + 1) * NH], start=(c == 0), stop=False)
                        nc.tensor.matmul(psc[a][0:NP_, 0:NH], shift[:, i, i * NP_:(i + 1) * NP_],
                                         shift[:, i, a * NH:(a + 1) * NH], start=False, stop=True).then_inc(counts_ready, 1)
                pe_.wait_ge(diag_ready, 1)
                for i in range(NT):
                    mm = nc.tensor.matmul(psq[i // 4][0:4, (i % 4) * NP_:(i % 4 + 1) * NP_], ones4[:, :], diag[:, i * NP_:(i + 1) * NP_],
                                          start=True, stop=True)
                mm.then_inc(roots_ready, 1)

            @block.scalar
            def _(act):
                for m in range(2 * NT):
                    i, a = divmod(m, 2)
                    act.wait_ge(counts_ready, m + 1)
                    nc.scalar.activation(w.adj[:, i, a * NH:(a + 1) * NH], psc[a][0:NP_, 0:NH], ACT.Copy).then_inc(counts_taken, 1)

            @block.vector
            def _(dve):
                n = [0]

                def link(ins):
                    n[0] += 1
                    ins.then_inc(dchain, 1)
                    dve.wait_ge(dchain, n[0])

                v = nc.vector
                v.memset(oneb[:, :], 1.0)
                v.memset(ones4[:, :], 1.0).then_inc(onehots, 1)
                dve.wait_ge(edges_loaded, 48)
                link(v.tensor_copy(eidf[:, :, :], eidx[:, :, :]))
                for c in range(EC):
                    for e in range(2):
                        v.tensor_scalar(onehot[:, e, c, :], iota[0:EP, :], eidf[:, e, c:c + 1], None, ALU.is_equal).then_inc(onehots, 1)
                dve.wait_ge(loaded, ALL)
                dve.wait_ge(pos_ready, 1)
                link(v.tensor_copy(pos[:, :], psp[0:D, 0:NR]))
                link(v.tensor_scalar(pos[:, :], pos[:, :], pos[:, NR - 1:NR], None, ALU.subtract))
                link(v.tensor_tensor(wqn[:, D:D + 1], wqn[:, D:D + 1], vb[:, :], ALU.add))
                for h in range(HEADS):
                    last = v.tensor_scalar(posd[:, h, :], pos[:, :], hm[:, h:h + 1], 0.25, ALU.mult, ALU.mult)
                last.then_inc(posd_ready, 1)
                link(v.tensor_tensor(qb[D:D + 1, 2, :], qb[D:D + 1, 0, :], qb[D:D + 1, 1, :], ALU.add))
                link(v.tensor_copy(w.wqk[D:D + 1, 0:D], qb[D:D + 1, 2, :]))
                link(v.tensor_scalar(w.wqk[:, 0:D], w.wqk[:, 0:D], 0.25, None, ALU.mult))
                dve.wait_ge(gpos_ready, 1)
                link(v.tensor_copy(w.gpos[:, :, :], psp[0:D + 1, 64:64 + HEADS * NR].rearrange("p (h r) -> p h r", h=HEADS)))
                v.tensor_copy(w.wdp[:, :].rearrange("p (k h) -> p k h", h=HEADS),
                              w.gpos[:, :, 0].rearrange("p (k h) -> p k h", k=1).to_broadcast([D + 1, NBLK, HEADS]))
                v.tensor_scalar(w.etab[:, :], pe[:, :], b128[:, 0:1], None, ALU.add)
                dve.wait_ge(deg_ready, 1)
                v.tensor_scalar(deg[:, :], psd[0:NP_, 0:4 * NT].rearrange("p (i k) -> p i k", k=4)[:, :, 0], 1.0, None, ALU.add).then_inc(degree_taken, 1)
                dve.wait_ge(degree_taken, 2)
                v.reciprocal(w.invdeg[:, :], deg[:, :])
                dve.wait_ge(powered, 1)
                link(v.tensor_tensor(root[:, :], deg[:, :], w.dinv[:, :], ALU.mult))
                for i in range(NT):
                    last = v.tensor_scalar(diag[:, i * NP_:(i + 1) * NP_], w.ident[0:NP_, 0:NP_], root[:, i:i + 1], None, ALU.mult)
                last.then_inc(diag_ready, 1)
                link(v.tensor_copy(w.w1a[:, :, :], w1f[:, :, :]))
                link(v.memset(w.w1b[:, :, :].bitcast(F32), 0.0))
                v.tensor_tensor(w.w1b[0:D, :, :], w1f[0:D, :, :], w.w1a[0:D, :, :].bitcast(F32), ALU.subtract)
                v.tensor_copy(w.w1b[96:96 + NE, :, :], b1r[96:96 + NE, :, :])
                link(v.tensor_copy(w.w1b[D:D + 1, :, :], b1r[64:65, :, :]))
                link(v.tensor_tensor(b1r[64:65, :, :], b1r[64:65, :, :], w.w1b[D:D + 1, :, :].bitcast(F32), ALU.subtract))
                link(v.tensor_copy(w.rank[:, :], gd[0:NPAIR, 0:NE]))
                link(v.memset(gd[:, :], 0.0))
                m = 0
                for a in range(NE - 1):
                    k = NE - 1 - a
                    v.tensor_scalar(gd[:, m:m + k], gw[:, a + 1:NE], gw[:, a:a + 1], -1.0, ALU.subtract, ALU.mult)
                    m += k
                link(v.memset(w.wgb[:, :].bitcast(F32), 0.0))
                link(v.tensor_copy(w.wga[:, :], gd[:, :]))
                link(v.tensor_tensor(w.wgb[0:D, :], gd[0:D, :], w.wga[0:D, :].bitcast(F32), ALU.subtract))
                m = 0
                for a in range(NE - 1):
                    k = NE - 1 - a
                    link(v.tensor_scalar(gd[64:65, m:m + k], gbr[64:65, a + 1:NE], gbr[64:65, a:a + 1], -1.0, ALU.subtract, ALU.mult))
                    m += k
                link(v.tensor_copy(w.wgb[64:65, 0:NPAIR], gd[64:65, 0:NPAIR]))
                link(v.tensor_tensor(gd[64:65, 0:NPAIR], gd[64:65, 0:NPAIR], w.wgb[64:65, 0:NPAIR].bitcast(F32), ALU.subtract))
                v.tensor_copy(w.b2[:, 0:D], b2f[:, 0, :])
                link(v.tensor_copy(w.b2[:, D:128], b2f[:, 1, :]))
                link(v.tensor_tensor(w.b2[:, D:128], b2f[:, 1, :], w.b2[:, 0:D].bitcast(F32), ALU.subtract))
                dve.wait_ge(roots_ready, 1)
                v.tensor_copy(sqr[:, 0:4 * NP_], psq[0][0:4, 0:4 * NP_])
                link(v.tensor_copy(sqr[:, 4 * NP_:NODES], psq[1][0:4, 0:NODES - 4 * NP_]))
                link(v.tensor_copy(sqh[:, :], sqr[:, :]))
                link(v.tensor_tensor(sql[:, :], sqr[:, :], sqh[:, :].bitcast(F32), ALU.subtract))
                link(v.tensor_scalar(sql[:, :], sql[:, :], rm[:, 1:2], None, ALU.mult))
                v.scalar_tensor_tensor(out=w.sq4[:, :], in0=sqh[:, :].bitcast(F32), scalar=rm[:, 0:1], in1=sql[:, :], op0=ALU.mult, op1=ALU.add)
                link(v.tensor_copy(bgh[:, :], bgr[:, :]))
                link(v.tensor_tensor(bgl[:, :], bgr[:, :], bgh[:, :].bitcast(F32), ALU.subtract))
                link(v.tensor_scalar(bgl[:, :], bgl[:, :], rm[:, 3:4], None, ALU.mult))
                v.scalar_tensor_tensor(out=w.bg4[:, :, :].rearrange("p l n -> p (l n)"), in0=bgh[:, :].bitcast(F32), scalar=rm[:, 2:3], in1=bgl[:, :], op0=ALU.mult, op1=ALU.add)

        with nc.Block() as block:
            lob = ctx.enter_context(nc.sbuf_tensor("lob", [66, NE * HID + 128], F32R))
            moved = sem("moved")
            rounded = sem("rounded")

            @block.vector
            def _(dve):
                nc.vector.tensor_copy(lob[64:65, 0:NE * HID], b1r[64:65, :, :].rearrange("p e h -> p (e h)"))
                nc.vector.tensor_copy(lob[64:65, NE * HID:NE * HID + NPAIR], gd[64:65, 0:NPAIR]).then_inc(rounded, 1)

            @block.sync
            def _(sp):
                sp.wait_ge(rounded, 1)
                sp.dma_start(w.w1b[65:66, :, :].rearrange("p e h -> p (e h)").bitcast(F32), lob[64:65, 0:NE * HID].bitcast(F32)).then_inc(moved, 16)
                sp.dma_start(w.wgb[65:66, 0:NPAIR].bitcast(F32), lob[64:65, NE * HID:NE * HID + NPAIR].bitcast(F32)).then_inc(moved, 16)
                sp.wait_ge(moved, 32)


def tokens(nc, w, ins, s, NB):
    xp = ins["x_patch"]
    with ExitStack() as ctx:
        def sb(name, shape, dt=F32):
            return ctx.enter_context(nc.sbuf_tensor(name, shape, dt))

        def sem(name):
            return ctx.enter_context(nc.semaphore(name))

        px = [sb(f"px{q}", [KP, 2, 2, NODES]) for q in range(2)]
        r = [sb(f"r{q}", [128, NODES]) for q in range(2)]
        g = [sb(f"g{q}", [NP_, NT, 128]) for q in range(2)]
        ghi = [sb(f"ghi{q}", [NP_, NT, 128], F32R) for q in range(2)]
        glo = [sb(f"glo{q}", [NP_, NT, 128], F32R) for q in range(2)]
        ot = [sb(f"ot{q}", [NP_, NT, 128]) for q in range(2)]
        feat = [ctx.enter_context(nc.psum_tensor(f"feat{q}", [128, 2, 512], F32)) for q in range(2)]
        node = [ctx.enter_context(nc.psum_tensor(f"node{q}", [128, 2 * 512], F32)) for q in range(2)]
        px_loaded = [sem(f"px_loaded{q}") for q in range(2)]
        embedded = [sem(f"embedded{q}") for q in range(2)]
        r_ready = [sem(f"r_ready{q}") for q in range(2)]
        node_ready = [sem(f"node_ready{q}") for q in range(2)]
        g_ready = [sem(f"g_ready{q}") for q in range(2)]
        ghi_ready = [sem(f"ghi_ready{q}") for q in range(2)]
        glo_ready = [sem(f"glo_ready{q}") for q in range(2)]
        agg_ready = [sem(f"agg_ready{q}") for q in range(2)]
        out_ready = [sem(f"out_ready{q}") for q in range(2)]
        stored = [sem(f"tok_stored{q}") for q in range(2)]
        LOOPS = NB // 4
        PARTS = range(0, 4), range(4, NT)

        def at_least(eng, semaphore, value):
            if not isinstance(value, int) or value > 0:
                eng.wait_ge(semaphore, value)

        def rounds(eng, step):
            step(0, LOOPS > 1)
            if LOOPS > 2:
                with eng.Fori(1, LOOPS - 1) as m:
                    step(m, True)
            if LOOPS > 1:
                step(LOOPS - 1, False)

        def per_node(ap, n):
            return ap.rearrange("p (i a) -> p i a", a=1).to_broadcast([NP_, n, 128])

        with nc.Block() as block:
            @block.sync
            def _(sp):
                def pixels(m, q):
                    at_least(sp, embedded[q], m)
                    sp.dma_start(px[q][:, :, :, :], xp[:, bass.ds(4 * m + 2 * q, 2), :, :]).then_inc(px_loaded[q], 16)

                def step(m, more):
                    for q in range(2):
                        if more:
                            pixels(m + 1, q)
                    for q in range(2):
                        sp.wait_ge(out_ready[q], m + 1)
                        for e in range(2):
                            sp.dma_start(s["tok"][bass.ds(4 * m + 2 * q + e, 1), 0:NODES, :].rearrange("b (i p) f -> p (b i) f", p=NP_),
                                         ot[q][:, :, 64 * e:64 * e + 64]).then_inc(stored[q], 16)

                for q in range(2):
                    pixels(0, q)
                rounds(sp, step)
                for q in range(2):
                    sp.wait_ge(stored[q], 32 * LOOPS)

            @block.tensor
            def _(pe):
                def embed(m, q):
                    pe.wait_ge(px_loaded[q], 16 * (m + 1))
                    at_least(pe, r_ready[q], 4 * m)
                    for a in range(2):
                        for k in range(2):
                            for e in range(2):
                                mm = nc.tensor.matmul(feat[q][64 * e:64 * e + 64, a, 0:NH], w.we[:, k, :],
                                                      px[q][:, e, k, a * NH:(a + 1) * NH], start=(k == 0), stop=(k == 1))
                    mm.then_inc(embedded[q], 1)

                def weights(m, q, l):
                    pe.wait_ge(r_ready[q], 4 * m + l + 1)
                    if l == 0:
                        at_least(pe, out_ready[q], m)
                    for part in range(2):
                        if l:
                            pe.wait_ge(g_ready[q], 2 * (3 * m + l) + part - 1)
                        for i in PARTS[part]:
                            mm = nc.tensor.matmul(node[q][0:NP_, i * 128:(i + 1) * 128], r[q][:, i * NP_:(i + 1) * NP_],
                                                  w.wg[:, l, :], start=True, stop=(l < 3))
                            if l == 3:
                                mm = nc.tensor.matmul(node[q][0:NP_, i * 128:(i + 1) * 128], w.sq4[:, i * NP_:(i + 1) * NP_],
                                                      w.bg4[:, 3, :], start=False, stop=True)
                        mm.then_inc(node_ready[q], 1)

                def aggregate(m, q, l):
                    for part in range(2):
                        pe.wait_ge(ghi_ready[q], 2 * (3 * m + l) + part + 1)
                        pe.wait_ge(glo_ready[q], 2 * (3 * m + l) + part + 1)
                        for a in range(2):
                            out = feat[q][:, a, 0:NH]
                            if part == 0:
                                nc.tensor.matmul(out, w.bg4[:, l, :], w.sq4[:, a * NH:(a + 1) * NH], start=True, stop=False)
                            for i in PARTS[part]:
                                nc.tensor.matmul(out, ghi[q][:, i, :], w.adj[:, i, a * NH:(a + 1) * NH], start=False, stop=False)
                                mm = nc.tensor.matmul(out, glo[q][:, i, :], w.adj[:, i, a * NH:(a + 1) * NH],
                                                      start=False, stop=(i == NT - 1))
                    mm.then_inc(agg_ready[q], 1)

                def step(m, more):
                    for l in range(3):
                        for q in range(2):
                            weights(m, q, l)
                        for q in range(2):
                            aggregate(m, q, l)
                    for q in range(2):
                        if more and q == 0:
                            embed(m + 1, 0)
                        weights(m, q, 3)
                        if more and q == 0:
                            embed(m + 1, 1)

                for q in range(2):
                    embed(0, q)
                rounds(pe, step)

            @block.vector
            def _(dve):
                def embedding(m, q):
                    dve.wait_ge(embedded[q], m + 1)
                    at_least(dve, node_ready[q], 8 * m)
                    nc.vector.tensor_tensor(r[q][:, :].rearrange("p (a n) -> p a n", a=2), feat[q][:, :, 0:NH],
                                            w.etab[:, :].rearrange("p (a n) -> p a n", a=2), ALU.add).then_inc(r_ready[q], 1)

                def scaled(m, q, l, part):
                    i0, n = PARTS[part][0], len(PARTS[part])
                    dve.wait_ge(node_ready[q], 2 * (4 * m + l) + part + 1)
                    at_least(dve, glo_ready[q], 2 * (3 * m + l) + part - 1)
                    nc.vector.tensor_tensor(g[q][:, i0:i0 + n, :], node[q][0:NP_, i0 * 128:(i0 + n) * 128].rearrange("p (i n) -> p i n", i=n),
                                            per_node((w.invdeg if l else w.dinv)[:, i0:i0 + n], n), ALU.mult).then_inc(g_ready[q], 1)

                def low_half(m, q, l, part):
                    i0, n = PARTS[part][0], len(PARTS[part])
                    dve.wait_ge(ghi_ready[q], 2 * (3 * m + l) + part + 1)
                    nc.vector.tensor_tensor(glo[q][:, i0:i0 + n, :], g[q][:, i0:i0 + n, :], ghi[q][:, i0:i0 + n, :].bitcast(F32),
                                            ALU.subtract).then_inc(glo_ready[q], 1)

                def output(m, q):
                    dve.wait_ge(node_ready[q], 8 * m + 8)
                    at_least(dve, stored[q], 32 * m)
                    nc.vector.tensor_tensor(ot[q][:, :, :], node[q][0:NP_, 0:NT * 128].rearrange("p (i n) -> p i n", i=NT),
                                            per_node(w.dinv[:, :], NT), ALU.mult).then_inc(out_ready[q], 1)

                def step(m, more):
                    for l in range(3):
                        for q in range(2):
                            for part in range(2):
                                scaled(m, q, l, part)
                            for part in range(2):
                                low_half(m, q, l, part)
                    for q in range(2):
                        if more:
                            embedding(m + 1, q)
                        output(m, q)

                for q in range(2):
                    embedding(0, q)
                rounds(dve, step)

            @block.scalar
            def _(act):
                def step(m, more):
                    for l in range(3):
                        for q in range(2):
                            at_least(act, agg_ready[q], 3 * m + l)
                            for part in range(2):
                                i0, n = PARTS[part][0], len(PARTS[part])
                                act.wait_ge(g_ready[q], 2 * (3 * m + l) + part + 1)
                                nc.scalar.activation(ghi[q][:, i0:i0 + n, :], g[q][:, i0:i0 + n, :], ACT.Copy).then_inc(ghi_ready[q], 1)
                        for q in range(2):
                            act.wait_ge(agg_ready[q], 3 * m + l + 1)
                            nc.scalar.activation(r[q][:, :].rearrange("p (a n) -> p a n", a=2), feat[q][:, :, 0:NH],
                                                 ACT.Relu).then_inc(r_ready[q], 1)

                rounds(act, step)


def project(nc, w, s, NB):
    with ExitStack() as ctx:
        def sb(name, shape, dt=F32):
            return ctx.enter_context(nc.sbuf_tensor(name, shape, dt))

        def sem(name):
            return ctx.enter_context(nc.semaphore(name))

        passed = sem("project_passed")

        x = [sb(f"px_{q}", [TP, TT, D]) for q in range(2)]
        xc = [sb(f"xc{k}", [TP, TT, D]) for k in range(2)]
        sq = sb("sqx", [TP, TT, D])
        y1 = sb("y1", [TP, TT, D])
        y2 = sb("y2", [TP, TT, D])
        st = [sb(f"stats{k}", [TP, 5, TT]) for k in range(2)]
        xt = [sb(f"xt{q}", [D + 1, T]) for q in range(2)]
        qkhi = [sb(f"qkhi{q}", [128, T], F32R) for q in range(2)]
        qklo = [sb(f"qklo{q}", [128, T], F32R) for q in range(2)]
        dpm = sb("dpm", [64, T])
        dphi = [sb(f"dphi{q}", [64, T], F32R) for q in range(2)]
        dplo = [sb(f"dplo{q}", [64, T], F32R) for q in range(2)]
        vv = [sb(f"vv{q}", [TP, TT, D]) for q in range(2)]
        psx = ctx.enter_context(nc.psum_tensor("psx", [128, 2, 512], F32))
        psqk = ctx.enter_context(nc.psum_tensor("psqk", [128, 2, 512], F32))
        psdp = ctx.enter_context(nc.psum_tensor("psdp", [128, 2, 512], F32))
        psv = ctx.enter_context(nc.psum_tensor("psv", [128, 512], F32))
        x_loaded = [sem(f"x_loaded{q}") for q in range(2)]
        ones_set = sem("ones_set")
        vars_ = [sem(f"vars{k}") for k in range(2)]
        rstds = [sem(f"rstds{k}") for k in range(2)]
        y1_ready = sem("y1_ready")
        y_ready = sem("y_ready")
        yt_ready = sem("yt_ready")
        xt_ready = sem("xt_ready")
        qk_ready = sem("qk_ready")
        dp_ready = sem("dp_ready")
        v_ready = sem("v_ready")
        qkhi_ready = sem("qkhi_ready")
        qklo_ready = sem("qklo_ready")
        v_taken = sem("v_taken")
        dpm_ready = sem("dpm_ready")
        dphi_ready = sem("dphi_ready")
        dplo_ready = sem("dplo_ready")
        saved = [sem(f"saved{q}") for q in range(2)]
        chain = sem("chainp")
        NSAVE = 8
        NLINK = 10

        def two(ap):
            return ap.rearrange("p (a n) -> p a n", a=2)

        def twice(ap):
            return ap.rearrange("p (a n) -> p a n", a=1).to_broadcast([64, 2, T])

        def at_least(eng, semaphore, value):
            if not isinstance(value, int) or value > 0:
                eng.wait_ge(semaphore, value)

        def after_first(b):
            return not isinstance(b, int) or b > 0

        def steps(eng, step):
            for b in range(4):
                step(b, b % 2, min(NB - 1 - b, 3))
            if NB > 8:
                with eng.Fori(2, NB // 2 - 2) as m:
                    step(2 * m, 0, 3)
                    step(2 * m + 1, 1, 3)
            if NB > 4:
                for b in range(NB - 4, NB):
                    step(b, b % 2, NB - 1 - b)

        with nc.Block() as block:
            @block.sync
            def _(sp):
                def rows(name, b, r0, n):
                    return s[name][bass.ds(b, 1), r0:r0 + n].rearrange("b r h t -> (b r h) t")

                def save_rest(b, q):
                    sp.wait_ge(v_taken, b + 1)
                    sp.dma_start(s["vst"][bass.ds(b, 1)].rearrange("b p j f -> p (b j) f"), vv[q][:, :, :]).then_inc(saved[q], 16)
                    sp.wait_ge(dphi_ready, b + 1)
                    sp.dma_start(rows("qst", b, 64, NBLK), dphi[q][:, :].bitcast(F32)).then_inc(saved[q], 16)
                    sp.wait_ge(dplo_ready, b + 1)
                    sp.dma_start(rows("qst", b, 64 + NBLK, NBLK), dplo[q][:, :].bitcast(F32)).then_inc(saved[q], 16)

                def step(b, q, more):
                    sv = saved[q]
                    if after_first(b):
                        save_rest(b - 1, 1 - q)
                    sp.wait_ge(xt_ready, b + 1)
                    sp.dma_start(s["xt"][bass.ds(b, 1)].rearrange("b f t -> (b f) t"), xt[q][0:D, :]).then_inc(sv, 16)
                    q_rows = s["qst"][bass.ds(b, 1), 0:64].rearrange("b (u g r) h t -> u (r h) (b g) t", u=2, g=2)
                    k_rows = s["kst"][bass.ds(b, 1)].rearrange("b (g u r) h t -> u (r h) (b g) t", g=2, u=2)
                    sp.wait_ge(qkhi_ready, b + 1)
                    sp.dma_start(q_rows[0], twice(qkhi[q][0:64, :].bitcast(F32))).then_inc(sv, 16)
                    sp.dma_start(k_rows[0], twice(qkhi[q][64:128, :].bitcast(F32))).then_inc(sv, 16)
                    sp.wait_ge(qklo_ready, b + 1)
                    sp.dma_start(q_rows[1], twice(qklo[q][0:64, :].bitcast(F32))).then_inc(sv, 16)
                    sp.dma_start(k_rows[1], twice(qklo[q][64:128, :].bitcast(F32))).then_inc(sv, 16)

                steps(sp, step)
                save_rest(NB - 1, 1)
                for q in range(2):
                    sp.wait_ge(saved[q], 16 * NSAVE * (NB // 2))

            @block.vector
            def _(dve):
                v = nc.vector

                def link(ins, value):
                    ins.then_inc(chain, 1)
                    dve.wait_ge(chain, value)

                def moments(k, src, done):
                    sk, xk = st[k], xc[k]
                    link(v.tensor_reduce(sk[:, 0, :], src, AX.X, ALU.add), done + 1)
                    link(v.tensor_scalar(sk[:, 1, :], sk[:, 0, :], -1.0 / D, None, ALU.mult), done + 2)
                    link(v.tensor_tensor(xk[:, :, :], src, sk[:, 1, :].rearrange("p (n a) -> p n a", a=1).to_broadcast([TP, TT, D]), ALU.add), done + 3)
                    link(v.tensor_tensor(sq[:, :, :], xk[:, :, :], xk[:, :, :], ALU.mult), done + 4)
                    link(v.tensor_reduce(sk[:, 2, :], sq[:, :, :], AX.X, ALU.add), done + 5)
                    v.tensor_scalar(sk[:, 4, :], sk[:, 2, :], 1.0 / D, EPS, ALU.mult, ALU.add).then_inc(vars_[k], 1)

                def scaled(b, k, dst):
                    dve.wait_ge(rstds[k], b + 1)
                    return v.tensor_tensor(dst, xc[k][:, :, :], st[k][:, 3, :].rearrange("p (n a) -> p n a", a=1).to_broadcast([TP, TT, D]), ALU.mult)

                def first_moments(b, q):
                    dve.wait_ge(x_loaded[q], 16 * (b // 2 + 1))
                    moments(0, x[q][:, :, :], b * NLINK)

                def second_moments(b):
                    scaled(b, 0, y1[:, :, :]).then_inc(y1_ready, 1)
                    dve.wait_ge(y1_ready, b + 1)
                    moments(1, y1[:, :, :], b * NLINK + 5)

                def normalised(b):
                    at_least(dve, yt_ready, b)
                    scaled(b, 1, y2[:, :, :]).then_inc(y_ready, 1)

                def low_half(b, q):
                    at_least(dve, saved[q], 16 * NSAVE * (b // 2))
                    dve.wait_ge(qkhi_ready, b + 1)
                    v.tensor_tensor(two(qklo[q][:, :]), psqk[:, :, 0:TH], two(qkhi[q][:, :].bitcast(F32)), ALU.subtract).then_inc(qklo_ready, 1)

                def mask_blocks(b):
                    dve.wait_ge(dp_ready, b + 1)
                    at_least(dve, dphi_ready, b)
                    at_least(dve, dplo_ready, b)
                    v.tensor_tensor(two(dpm[:, :]), psdp[0:64, :, 0:TH], two(w.blkmask[:, :]), ALU.mult).then_inc(dpm_ready, 1)

                def step(b, q, more):
                    if after_first(b):
                        mask_blocks(b - 1)
                    if more:
                        second_moments(b + 1)
                    if more > 1:
                        first_moments(b + 2, q)
                    low_half(b, q)
                    if more:
                        normalised(b + 1)

                v.memset(xt[0][D:D + 1, :], 1.0)
                v.memset(xt[1][D:D + 1, :], 1.0).then_inc(ones_set, 1)
                first_moments(0, 0)
                second_moments(0)
                first_moments(1, 1)
                normalised(0)
                steps(dve, step)
                mask_blocks(NB - 1)

            @block.gpsimd
            def _(pool):
                def power(b, k):
                    wait_apart(pool, vars_[k], b + 1, passed)
                    nc.gpsimd.tensor_tensor(st[k][:, 3, :], st[k][:, 4, :], w.mhalf[0:TP, :], ALU.pow).then_inc(rstds[k], 1)

                def low_half(b, q):
                    at_least(pool, saved[q], 16 * NSAVE * (b // 2))
                    wait_apart(pool, dphi_ready, b + 1, passed)
                    nc.gpsimd.tensor_tensor(dplo[q][:, :], dpm[:, :], dphi[q][:, :].bitcast(F32), ALU.subtract).then_inc(dplo_ready, 1)

                def step(b, q, more):
                    if after_first(b):
                        low_half(b - 1, 1 - q)
                    if more:
                        power(b + 1, 1)
                    if more > 1:
                        power(b + 2, 0)

                power(0, 0)
                power(0, 1)
                power(1, 0)
                steps(pool, step)
                low_half(NB - 1, 1)

            @block.scalar
            def _(act):
                def load(b, q):
                    at_least(act, vars_[0], b - 1)
                    act.dma_start(x[q][:, :, :], s["tok"][bass.ds(b, 1)].rearrange("b (j p) f -> p (b j) f", p=TP)).then_inc(x_loaded[q], 16)

                def transposed(b, q):
                    at_least(act, saved[q], 16 * NSAVE * (b // 2))
                    act.wait_ge(yt_ready, b + 1)
                    nc.scalar.activation(two(xt[q][0:D, :]), psx[0:D, :, 0:TH], ACT.Identity, bias=w.lnb[:, 0:1],
                                         scale=w.lng[:, 0:1]).then_inc(xt_ready, 1)

                def high_half(b, q):
                    at_least(act, saved[q], 16 * NSAVE * (b // 2))
                    act.wait_ge(dpm_ready, b + 1)
                    nc.scalar.activation(dphi[q][:, :], dpm[:, :], ACT.Copy).then_inc(dphi_ready, 1)

                def step(b, q, more):
                    if after_first(b):
                        high_half(b - 1, 1 - q)
                    act.wait_ge(qk_ready, b + 1)
                    nc.scalar.activation(two(qkhi[q][:, :]), psqk[:, :, 0:TH], ACT.Copy).then_inc(qkhi_ready, 1)
                    if more > 2:
                        load(b + 3, 1 - q)
                    if more:
                        transposed(b + 1, 1 - q)
                    act.wait_ge(v_ready, b + 1)
                    nc.scalar.activation(vv[q][:, :, :].rearrange("p j f -> p (j f)"), psv[0:TP, :], ACT.Copy).then_inc(v_taken, 1)

                load(0, 0)
                load(1, 1)
                load(2, 0)
                transposed(0, 0)
                steps(act, step)
                high_half(NB - 1, 1)

            @block.tensor
            def _(pe):
                def transposes(b):
                    at_least(pe, xt_ready, b)
                    wait_apart(pe, y_ready, b + 1, passed)
                    for j in range(TT):
                        mm = nc.tensor.transpose(psx[0:D, j // 4, (j % 4) * TP:(j % 4 + 1) * TP], y2[:, j, :], w.ident[0:TP, 0:TP])
                    mm.then_inc(yt_ready, 1)

                def step(b, q, more):
                    pe.wait_ge(xt_ready, b + 1)
                    at_least(pe, qklo_ready, b)
                    for a in range(2):
                        mm = nc.tensor.matmul(psqk[:, a, 0:TH], w.wqk[:, :], xt[q][:, a * TH:(a + 1) * TH], start=True, stop=True)
                    mm.then_inc(qk_ready, 1)
                    at_least(pe, dpm_ready, b)
                    for a in range(2):
                        mm = nc.tensor.matmul(psdp[0:64, a, 0:TH], w.wdp[:, :], xt[q][:, a * TH:(a + 1) * TH], start=True, stop=True)
                    mm.then_inc(dp_ready, 1)
                    at_least(pe, v_taken, b)
                    for half in range(2):
                        for j in range(TT // 2 * half, TT // 2 * (half + 1)):
                            mm = nc.tensor.matmul(psv[0:TP, j * D:(j + 1) * D], xt[q][:, j * TP:(j + 1) * TP], w.wv[:, :], start=True, stop=True)
                        if half == 0 and more:
                            transposes(b + 1)
                    mm.then_inc(v_ready, 1)

                pe.wait_ge(ones_set, 1)
                transposes(0)
                steps(pe, step)


def attend(nc, w, s, NB):
    N = NB * TT
    with ExitStack() as ctx:
        def sb(name, shape, dt=F32):
            return ctx.enter_context(nc.sbuf_tensor(name, shape, dt))

        def sem(name):
            return ctx.enter_context(nc.semaphore(name))

        passed = sem("attend_passed")

        def pb(name, shape):
            return ctx.enter_context(nc.psum_tensor(name, shape, F32))

        qst = [sb(f"qst{q}", [SROWS, HEADS, TP], F32R) for q in range(2)]
        kst = sb("kst_sb", [SROWS, 2, HEADS, T], F32R)
        vs = [sb(f"vs{q}", [TP, TT, D]) for q in range(2)]
        xs = [sb(f"xs{q}", [D + 1, TP]) for q in range(2)]
        res = [sb(f"res{q}", [TP, D]) for q in range(2)]
        farband = sb("farband", [TP, HEADS, NR])
        band = [sb(f"band{q}", [TP, HEADS, NR]) for q in range(2)]
        z = [sb(f"z{q}", [TP, HEADS, WIN]) for q in range(2)]
        nmax = sb("nmax", [TP, HEADS])
        p = [sb(f"p{h}", [TP, T]) for h in range(HEADS)]
        sums_ = [sb(f"sums{q}", [TP, HEADS]) for q in range(2)]
        inv = [sb(f"inv{q}", [TP, HEADS]) for q in range(2)]
        rinv = [sb(f"rinv{q}", [TP, HEADS, 32]) for q in range(2)]
        ones32 = sb("ones32", [TP, HEADS, 32])
        pt = [sb(f"pt{q}", [TP, HEADS, TT, TP]) for q in range(2)]
        ctxs = sb("ctxs", [112, TP])
        ctxn = sb("ctxn", [128, TP])
        o = [sb(f"o{q}", [TP, D]) for q in range(2)]
        pss = [pb(f"pss{q}", [128, 1024]) for q in range(2)]
        pst = [pb(f"pst{q}", [128, 512]) for q in range(2)]
        pso = pb("pso", [128, 512])
        psb = pb("psb", [128, 512])

        qst_loaded = [sem(f"qst_loaded{q}") for q in range(2)]
        kst_loaded = sem("kst_loaded")
        v_loaded = [sem(f"v_loaded{q}") for q in range(2)]
        xs_loaded = [sem(f"xs_loaded{q}") for q in range(2)]
        res_loaded = [sem(f"res_loaded{q}") for q in range(2)]
        ring_written = [sem(f"ring_written{q}") for q in range(2)]
        z_loaded = [sem(f"z_loaded{q}") for q in range(2)]
        stored = [sem(f"tok2_stored{q}") for q in range(2)]
        ready0 = sem("ready0")
        scores_ready = sem("scores_ready")
        window_added = sem("window_added")
        nmax_ready = sem("nmax_ready")
        exp_done = sem("exp_done")
        tr_ready = [sem(f"tr_ready{a}") for a in range(2)]
        tr_taken = [sem(f"tr_taken{a}") for a in range(2)]
        ctx_ready = sem("ctx_ready")
        ctx_taken = sem("ctx_taken")
        inv_ready = sem("inv_ready")
        rinv_ready = sem("rinv_ready")
        rb_ready = sem("rb_ready")
        ctxn_ready = sem("ctxn_ready")
        proj_ready = sem("proj_ready")
        out_ready = sem("out_ready")
        band_ready = sem("band_ready")
        far_ready = sem("far_ready")
        band_done = sem("band_done")

        def at_least(eng, semaphore, value):
            if not isinstance(value, int) or value > 0:
                eng.wait_ge(semaphore, value)

        def pairs(eng, step):
            step(0, 0, True, False, False)
            step(1, 1, True, True, False)
            step(2, 0, True, True, True)
            step(3, 1, True, True, True)
            with eng.Fori(2, N // 2) as m:
                step(2 * m, 0, True, True, True)
                step(2 * m + 1, 1, True, True, True)
            step(N, 0, False, True, True)
            step(N + 1, 1, False, False, True)

        with nc.Block() as block:
            @block.sync
            def _(sp):
                def wait(semaphore, value):
                    if isinstance(value, int):
                        at_least(sp, semaphore, value)
                    else:
                        wait_apart(sp, semaphore, value, passed)

                def place(n):
                    return bass.ds(n // TT, 1), bass.ds((n % TT) * TP, TP)

                def load_xs(n, k):
                    wait(band_done, n - 1)
                    b, t = place(n)
                    sp.dma_start(xs[k][0:D, :], s["xt"][b, :, t].rearrange("b f t -> (b f) t")).then_inc(xs_loaded[k], 16)

                def load_queries(n, k):
                    wait(scores_ready, 4 * n - 4)
                    b, t = place(n)
                    sp.dma_start(qst[k][:, :, :].bitcast(F32), s["qst"][b, :, :, t].rearrange("b r h t -> r (b h) t")).then_inc(qst_loaded[k], 16)

                def load_window(n, k):
                    wait(ring_written[k], 16 * (n // 2 + 1))
                    wait(window_added, 4 * n - 4)
                    sp.dma_start(z[k][:, :, :], s["ring"][k]).then_inc(z_loaded[k], 16)

                def load_values(b, k):
                    wait(v_loaded[k], 16 * b)
                    wait(ctx_ready, TT * b - 1 + k)
                    sp.dma_start(vs[k][:, :, :], s["vst"][bass.ds(b, 1)].rearrange("b p j f -> p (b j) f")).then_inc(v_loaded[k], 16)

                def load_residual(n, k):
                    wait(out_ready, n - 1)
                    b, t = place(n)
                    sp.dma_start(res[k][:, :], s["tok"][b, t, :].rearrange("b t f -> (b t) f")).then_inc(res_loaded[k], 16)

                def store(n, k):
                    wait(out_ready, n + 1)
                    b, t = place(n)
                    sp.dma_start(s["tok2"][b, t, :].rearrange("b t f -> (b t) f"), o[k][:, :]).then_inc(stored[k], 16)

                def step(n, k, more=True):
                    load_xs(n + 2, k)
                    if more:
                        load_queries(n + 1, 1 - k)
                        load_window(n + 1, 1 - k)
                    if not isinstance(n, int) or n > 2:
                        store(n - 3, 1 - k)
                    if not isinstance(n, int) or n > 0:
                        load_residual(n - 1, 1 - k)

                sp.wait_ge(ready0, 1)
                load_xs(0, 0)
                load_xs(1, 1)
                load_queries(0, 0)
                load_window(0, 0)
                def first_steps(b):
                    for k in range(2):
                        step(b * TT + k, k)
                        load_values(b, k)

                def steps_of(b, first, end):
                    with sp.Fori(first, end) as jj:
                        step(b * TT + 2 * jj, 0)
                        step(b * TT + 2 * jj + 1, 1)

                first_steps(0)
                step(2, 0)
                step(3, 1)
                steps_of(0, 2, TT // 2)
                with sp.Fori(1, NB - 1) as b:
                    first_steps(b)
                    steps_of(b, 1, TT // 2)
                first_steps(NB - 1)
                steps_of(NB - 1, 1, TT // 2 - 1)
                step(N - 2, 0)
                step(N - 1, 1, more=False)
                load_residual(N - 1, 1)
                for n in range(N - 3, N):
                    store(n, n % 2)
                for q in range(2):
                    sp.wait_ge(stored[q], 16 * (N // 2))

            @block.gpsimd
            def _(pool):
                def keys(b, slot):
                    pool.dma_start(kst[0:64, slot, :, :].bitcast(F32), s["kst"][b].rearrange("b r h t -> r (b h) t")).then_inc(kst_loaded, 16)

                def skew(n, k):
                    at_least(pool, z_loaded[k], 16 * (n // 2))
                    wait_apart(pool, band_done, n + 1, passed)
                    diag = bass.AP(s["ring"].tensor, k * TP * HEADS * WIN, [[HEADS * WIN + 1, TP], [WIN, HEADS], [1, NR]])
                    pool.dma_start(diag, band[k][:, :, :]).then_inc(ring_written[k], 16)

                def repeat(n, k):
                    at_least(pool, rb_ready, n - 1)
                    wait_apart(pool, inv_ready, n + 1, passed)
                    wide = inv[k][:, :].rearrange("p (h a) -> p h a", a=1).to_broadcast([TP, HEADS, 32])
                    nc.gpsimd.tensor_tensor(rinv[k][:, :, :], wide, ones32[:, :, :], ALU.mult).then_inc(rinv_ready, 1)

                def both(n, k):
                    skew(n, k)
                    repeat(n - 2, k)

                def skews(b, first):
                    with pool.Fori(first, TT // 2) as jj:
                        both(b * TT + 2 * jj, 0)
                        both(b * TT + 2 * jj + 1, 1)

                pool.wait_ge(ready0, 1)
                keys(slice(0, 1), slice(0, 1))
                skew(0, 0)
                skew(1, 1)
                pool.wait_ge(scores_ready, 1)
                keys(slice(1, 2), slice(1, 2))
                both(2, 0)
                both(3, 1)
                skews(0, 2)
                with pool.Fori(1, NB - 1) as b:
                    both(b * TT, 0)
                    both(b * TT + 1, 1)
                    wait_apart(pool, kst_loaded, 16 * (b + 1), passed)
                    wait_apart(pool, scores_ready, 4 * TT * b + 1, passed)
                    keys(bass.ds(b + 1, 1), bass.ds((b + 1) % 2, 1))
                    skews(b, 1)
                skews(NB - 1, 0)
                repeat(N - 2, 0)
                repeat(N - 1, 1)

            @block.tensor
            def _(pe):
                def scores(n, k, h):
                    if h == 0:
                        pe.wait_ge(qst_loaded[k], 16 * (n // 2 + 1))
                        pe.wait_ge(kst_loaded, 16 * (n // TT + 1))
                    at_least(pe, exp_done, 4 * n + h - 1)
                    slot = (n // TT) % 2

                    def ks(a, b_):
                        return kst[:, bass.ds(slot, 1), h, a:b_].rearrange("p a n -> p (a n)")

                    nc.tensor.matmul(pss[h % 2][0:TP, REL:512], qst[k][:, h, :], ks(0, 512 - REL), start=True, stop=True)
                    nc.tensor.matmul(pss[h % 2][0:TP, 512:REL + T], qst[k][:, h, :], ks(512 - REL, T), start=True, stop=True).then_inc(scores_ready, 1)

                def transposes(n, h):
                    for a in range(2):
                        if a == 0:
                            pe.wait_ge(exp_done, 4 * n + h + 1)
                        at_least(pe, tr_taken[a], 4 * n + h)
                        for i in range(4):
                            mm = nc.tensor.transpose(pst[a][0:TP, i * TP:(i + 1) * TP], p[h][:, (4 * a + i) * TP:(4 * a + i + 1) * TP], w.ident[0:TP, 0:TP])
                        mm.then_inc(tr_ready[a], 1)

                def context(n, k, c):
                    if c == 0:
                        pe.wait_ge(tr_taken[0], 4 * n + 4)
                        pe.wait_ge(tr_taken[1], 4 * n + 4)
                        pe.wait_ge(v_loaded[k], 16 * (n // TT + 1))
                        at_least(pe, ctx_taken, n)
                    for i in range(2 * c, 2 * c + 2):
                        for h in range(HEADS):
                            mm = nc.tensor.matmul(pso[32 * h:32 * h + HD, 0:TP], vs[k][:, i, h * HD:(h + 1) * HD],
                                                  pt[k][:, h, i, :], start=(i == 0), stop=(i == TT - 1))
                    if c == TT // 2 - 1:
                        mm.then_inc(ctx_ready, 1)

                def reciprocals(n, k):
                    pe.wait_ge(rinv_ready, n + 1)
                    pe.wait_ge(band_done, min(n + 5, N + 2) if isinstance(n, int) else n + 5)
                    at_least(pe, out_ready, n)
                    nc.tensor.transpose(psb[0:112, 0:TP], rinv[k][:, :, :].rearrange("p h d -> p (h d)")[:, 0:112],
                                        w.ident[0:TP, 0:TP]).then_inc(rb_ready, 1)

                def project_out(n):
                    pe.wait_ge(ctxn_ready, n + 1)
                    nc.tensor.matmul(psb[0:TP, 384:384 + D], ctxn[:, :], w.wo[:, :], start=True, stop=True).then_inc(proj_ready, 1)

                def band_terms(n, k):
                    pe.wait_ge(xs_loaded[k], 16 * (n // 2 + 1))
                    at_least(pe, band_done, n)
                    at_least(pe, out_ready, n - 4)
                    nc.tensor.matmul(psb[0:TP, 128:128 + HEADS * NR], xs[k][:, :], w.gpos[:, :, :].rearrange("p h r -> p (h r)"),
                                     start=True, stop=True).then_inc(band_ready, 1)

                def step(n, k, new, last, older):
                    for h in range(HEADS):
                        if new:
                            scores(n, k, h)
                        if h < 2 and last:
                            transposes(n - 1, 2 + h)
                        if h >= 2 and new:
                            transposes(n, h - 2)
                        if h == 1 and new:
                            band_terms(n + 2, k)
                        if h == 2 and older:
                            reciprocals(n - 2, k)
                        if h == 3 and older:
                            project_out(n - 2)
                        if h < 2 and older:
                            context(n - 2, k, 2 + h)
                        if h >= 2 and last:
                            context(n - 1, 1 - k, h - 2)

                pe.wait_ge(ready0, 1)
                band_terms(0, 0)
                band_terms(1, 1)
                pairs(pe, step)

            @block.vector
            def _(dve):
                v = nc.vector

                def window_and_max(n, k, h):
                    if h == 0:
                        dve.wait_ge(z_loaded[k], 16 * (n // 2 + 1))
                    dve.wait_ge(scores_ready, 4 * n + h + 1)
                    win = pss[h % 2][0:TP, bass.ds((n % TT) * TP, WIN)]
                    v.tensor_tensor(win, win, z[k][:, h, :], ALU.add).then_inc(window_added, 1)
                    dve.wait_ge(window_added, 4 * n + h + 1)
                    v.tensor_reduce(nmax[:, h:h + 1], pss[h % 2][0:TP, REL:REL + T], AX.X, ALU.max, negate=True).then_inc(nmax_ready, 1)

                def copy_out(n, k, h):
                    dve.wait_ge(tr_ready[1], 4 * n + h + 1)
                    at_least(dve, ctx_ready, n - 1)
                    v.tensor_copy(pt[k][:, h, 4:8, :].rearrange("p i t -> p (i t)"), pst[1][0:TP, 0:4 * TP]).then_inc(tr_taken[1], 1)

                def invert(n, k):
                    dve.wait_ge(exp_done, 4 * n + 4)
                    at_least(dve, rinv_ready, n - 1)
                    v.reciprocal(inv[k][:, :], sums_[k][:, :]).then_inc(inv_ready, 1)

                def normalise(n):
                    dve.wait_ge(ctx_taken, n + 1)
                    dve.wait_ge(rb_ready, n + 1)
                    v.tensor_tensor(ctxn[0:112, :], ctxs[:, :], psb[0:112, 0:TP], ALU.mult).then_inc(ctxn_ready, 1)

                def residual(n, k):
                    dve.wait_ge(proj_ready, n + 1)
                    dve.wait_ge(res_loaded[k], 16 * (n // 2 + 1))
                    at_least(dve, stored[k], 16 * (n // 2))
                    v.tensor_tensor(o[k][:, :], psb[0:TP, 384:384 + D], res[k][:, :], ALU.add).then_inc(out_ready, 1)

                def band_out(n, k):
                    dve.wait_ge(band_ready, n + 1)
                    src = psb[0:TP, 128:128 + HEADS * NR].rearrange("p (h r) -> p h r", h=HEADS)
                    v.tensor_tensor(farband[:, :, :], w.bandstep[:, :].rearrange("p (a r) -> p a r", a=1).to_broadcast([TP, HEADS, NR]),
                                    src[:, :, 0:1].to_broadcast([TP, HEADS, NR]), ALU.mult).then_inc(far_ready, 1)
                    dve.wait_ge(far_ready, n + 1)
                    at_least(dve, ring_written[k], 16 * (n // 2))
                    v.tensor_tensor(band[k][:, :, :], src, farband[:, :, :], ALU.subtract).then_inc(band_done, 1)

                def step(n, k, new, last, older):
                    if new:
                        window_and_max(n, k, 0)
                    if last:
                        invert(n - 1, 1 - k)
                    if new:
                        window_and_max(n, k, 1)
                    if new:
                        band_out(n + 2, k)
                    if new:
                        window_and_max(n, k, 2)
                    if older:
                        normalise(n - 2)
                    if new:
                        window_and_max(n, k, 3)
                        copy_out(n, k, 1)
                    if older:
                        residual(n - 2, k)

                for q in range(2):
                    v.memset(pss[q][:, :], 0.0)
                    v.memset(xs[q][D:D + 1, :], 1.0)
                v.memset(pso[:, :], 0.0)
                v.memset(ones32[:, :, :], 1.0)
                v.memset(ctxn[96:128, :], 1.0)
                for q in range(2):
                    for h in range(HEADS):
                        last = v.tensor_copy(kst[64:96, q, h, :], w.step[64:96, :])
                last.then_inc(ready0, 1)
                band_out(0, 0)
                band_out(1, 1)
                pairs(dve, step)

            @block.scalar
            def _(act):
                def softmax(n, k, h):
                    act.wait_ge(nmax_ready, 4 * n + h + 1)
                    at_least(act, tr_ready[1], 4 * n + h - 3)
                    nc.scalar.activation(p[h][:, :], pss[h % 2][0:TP, REL:REL + T], ACT.Exp, bias=nmax[:, h:h + 1],
                                         scale=1.0, accum_out=sums_[k][:, h:h + 1]).then_inc(exp_done, 1)

                def copy_out(n, k, h, halves):
                    if h == 0:
                        at_least(act, ctx_ready, n - 1)
                    for a in halves:
                        act.wait_ge(tr_ready[a], 4 * n + h + 1)
                        nc.scalar.activation(pt[k][:, h, 4 * a:4 * a + 4, :].rearrange("p i t -> p (i t)"), pst[a][0:TP, 0:4 * TP],
                                             ACT.Copy).then_inc(tr_taken[a], 1)

                def context_out(n):
                    act.wait_ge(ctx_ready, n + 1)
                    at_least(act, ctxn_ready, n)
                    nc.scalar.activation(ctxs[:, :], pso[0:112, 0:TP], ACT.Copy).then_inc(ctx_taken, 1)

                def step(n, k, new, last, older):
                    for h in range(HEADS):
                        if h < 2 and last:
                            copy_out(n - 1, 1 - k, 2 + h, (0, 1))
                        if h == 1 and older:
                            context_out(n - 2)
                        if h >= 2 and new:
                            copy_out(n, k, h - 2, (0, 1) if h == 2 else (0,))
                        if new:
                            softmax(n, k, h)

                pairs(act, step)


def experts(nc, w, s, out, NB):
    G = NB * TT // 4
    GT = 4
    GN = GT * TP
    with ExitStack() as ctx:
        def sb(name, shape, dt=F32):
            return ctx.enter_context(nc.sbuf_tensor(name, shape, dt))

        def sem(name):
            return ctx.enter_context(nc.semaphore(name))

        passed = sem("experts_passed")

        def pb(name):
            return ctx.enter_context(nc.psum_tensor(name, [128, 512], F32))

        x = [sb(f"ex{q}", [TP, GT, D]) for q in range(2)]
        res = [sb(f"eres{q}", [TP, GT, D]) for q in range(2)]
        xc = sb("exc", [TP, GT, D])
        sq = sb("esq", [TP, GT, D])
        st = sb("est", [TP, 5, GT])
        y = [sb(f"ey{q}", [TP, GT, 2, D]) for q in range(2)]
        xh = sb("xh", [128, GN], F32R)
        xa = [sb(f"xa{q}", [128, GN], F32R) for q in range(2)]
        xb = [sb(f"xb{q}", [104, GN], F32R) for q in range(2)]
        ge = [sb(f"ge{q}", [NPAIR, GN], BF16) for q in range(2)]
        mk = [sb(f"mk{q}", [NE, GN], F32R) for q in range(2)]
        hs = [sb(f"hs{i}", [HID, GN]) for i in range(4)]
        os_ = [sb(f"os{q}", [128, GN]) for q in range(2)]
        o = [sb(f"eo{q}", [TP, GT, D]) for q in range(2)]
        psy, psg, psr, psf = pb("psy"), pb("psg"), pb("psr"), pb("psf")
        psh = [pb(f"psh{q}") for q in range(2)]
        pso = [pb(f"epso{q}") for q in range(2)]

        x_loaded = [sem(f"ex_loaded{q}") for q in range(2)]
        r_loaded = [sem(f"er_loaded{q}") for q in range(2)]
        stored = [sem(f"out_stored{q}") for q in range(2)]
        ones_set = sem("eones_set")
        chain = sem("echain")
        vars_ = sem("evars")
        rstds = sem("erstds")
        y_ready = sem("ey_ready")
        yt_ready = sem("eyt_ready")
        xh_ready = sem("xh_ready")
        xl_ready = sem("xl_ready")
        gate_ready = sem("gate_ready")
        ge_ready = sem("ge_ready")
        rank_ready = sem("rank_ready")
        masks_ready = sem("masks_ready")
        hid_ready = sem("hid_ready")
        hid_done = sem("hid_done")
        exp_ready = sem("exp_ready")
        os_ready = sem("os_ready")
        fold_ready = sem("fold_ready")
        o_ready = sem("o_ready")
        NLINK = 5

        tok2 = s["tok2"].rearrange("b (g j p) f -> (b g) p j f", j=GT, p=TP)
        outv = out.rearrange("b (g j p) f -> (b g) p j f", j=GT, p=TP)

        def at_least(eng, semaphore, value):
            if not isinstance(value, int) or value > 0:
                eng.wait_ge(semaphore, value)

        def steps(eng, step):
            step(0, 0, True, False, False, True)
            step(1, 1, True, True, False, True)
            step(2, 0, True, True, True, True)
            step(3, 1, True, True, True, True)
            with eng.Fori(2, G // 2 - 1) as m:
                for k in range(2):
                    step(2 * m + k, k, True, True, True, True)
            step(G - 2, 0, True, True, True, True)
            step(G - 1, 1, True, True, True, False)
            step(G, 0, False, True, True, False)
            step(G + 1, 1, False, False, True, False)

        with nc.Block() as block:
            @block.sync
            def _(sp):
                def load_x(g, q):
                    at_least(sp, y_ready, g - 1)
                    sp.dma_start(x[q][:, :, :], tok2[bass.ds(g, 1)].rearrange("g p j f -> p (g j) f")).then_inc(x_loaded[q], 16)

                def load_residual(g, q):
                    at_least(sp, o_ready, g - 1)
                    sp.dma_start(res[q][:, :, :], tok2[bass.ds(g, 1)].rearrange("g p j f -> p (g j) f")).then_inc(r_loaded[q], 16)

                def store(g, q):
                    sp.wait_ge(o_ready, g + 1)
                    sp.dma_start(outv[bass.ds(g, 1)].rearrange("g p j f -> p (g j) f"), o[q][:, :, :]).then_inc(stored[q], 16)

                def step(g, k, new, running, finishing, ahead):
                    if ahead:
                        load_x(g + 1, 1 - k)
                    if running:
                        load_residual(g - 1, 1 - k)
                    if finishing:
                        store(g - 2, k)

                load_x(0, 0)
                steps(sp, step)
                for q in range(2):
                    sp.wait_ge(stored[q], 16 * (G // 2))

            @block.vector
            def _(dve):
                v = nc.vector

                def moments(g, q):
                    n = [0]

                    def link(ins):
                        n[0] += 1
                        ins.then_inc(chain, 1)
                        dve.wait_ge(chain, g * NLINK + n[0])

                    dve.wait_ge(x_loaded[q], 16 * (g // 2 + 1))
                    link(v.tensor_reduce(st[:, 0, :], x[q][:, :, :], AX.X, ALU.add))
                    link(v.tensor_scalar(st[:, 1, :], st[:, 0, :], -1.0 / D, None, ALU.mult))
                    link(v.tensor_tensor(xc[:, :, :], x[q][:, :, :], st[:, 1, :].rearrange("p (n a) -> p n a", a=1).to_broadcast([TP, GT, D]), ALU.add))
                    link(v.tensor_tensor(sq[:, :, :], xc[:, :, :], xc[:, :, :], ALU.mult))
                    link(v.tensor_reduce(st[:, 2, :], sq[:, :, :], AX.X, ALU.add))
                    v.tensor_scalar(st[:, 4, :], st[:, 2, :], 1.0 / D, EPS, ALU.mult, ALU.add).then_inc(vars_, 1)

                def scaled(g, q):
                    at_least(dve, yt_ready, g - 1)
                    dve.wait_ge(rstds, g + 1)
                    rstd = st[:, 3, :].rearrange("p (n a) -> p n a", a=1).to_broadcast([TP, GT, D])
                    for t in range(2):
                        last = v.tensor_tensor(y[q][:, :, t, :], xc[:, :, :], rstd, ALU.mult)
                    last.then_inc(y_ready, 1)

                def low_half(g, q):
                    dve.wait_ge(xh_ready, g + 1)
                    at_least(dve, hid_ready, NE * (g - 1))
                    v.tensor_tensor(xa[q][64:128, :], psy[64:128, 0:GN], xh[64:128, :].bitcast(F32), ALU.subtract).then_inc(xl_ready, 1)

                def gate(g, q):
                    dve.wait_ge(gate_ready, g + 1)
                    v.tensor_scalar(ge[q][:, :], psg[0:NPAIR, 0:GN], 0.0, None, ALU.is_ge).then_inc(ge_ready, 1)

                def masks(g, q):
                    dve.wait_ge(rank_ready, g + 1)
                    v.tensor_scalar(xb[q][96:96 + NE, :], psr[0:NE, 0:GN], w.thr[:, 0:1], None, ALU.is_ge)
                    v.tensor_scalar(mk[q][:, :], psr[0:NE, 0:GN], w.thr[:, 0:1], None, ALU.is_lt).then_inc(masks_ready, 1)

                def residual(g, q):
                    dve.wait_ge(fold_ready, g + 1)
                    dve.wait_ge(r_loaded[q], 16 * (g // 2 + 1))
                    at_least(dve, stored[q], 16 * (g // 2))
                    v.tensor_tensor(o[q][:, :, :], psf[0:TP, 0:GT * D].rearrange("p (j f) -> p j f", j=GT), res[q][:, :, :], ALU.add).then_inc(o_ready, 1)

                def step(g, k, new, running, finishing, ahead):
                    if new:
                        low_half(g, k)
                    if ahead:
                        moments(g + 1, 1 - k)
                    if new:
                        gate(g, k)
                    if ahead:
                        scaled(g + 1, 1 - k)
                    if finishing:
                        residual(g - 2, k)
                    if new:
                        masks(g, k)

                for q in range(2):
                    v.memset(xb[q][D:96, :].bitcast(F32), 0.0).then_inc(ones_set, 1)
                dve.wait_ge(ones_set, 2)
                for q in range(2):
                    v.memset(xb[q][D:D + 2, :].bitcast(F32), 1.0).then_inc(ones_set, 1)
                moments(0, 0)
                scaled(0, 0)
                steps(dve, step)

            @block.gpsimd
            def _(pool):
                def power(g):
                    wait_apart(pool, vars_, g + 1, passed)
                    nc.gpsimd.tensor_tensor(st[:, 3, :], st[:, 4, :], w.mhalf[0:TP, 0:GT], ALU.pow).then_inc(rstds, 1)

                def step(g, k, new, running, finishing, ahead):
                    if ahead:
                        power(g + 1)

                power(0)
                steps(pool, step)

            @block.scalar
            def _(act):
                def high_half(g, q):
                    act.wait_ge(yt_ready, g + 1)
                    at_least(act, xl_ready, g)
                    at_least(act, hid_ready, NE * (g - 1))
                    nc.scalar.activation(xh[64:128, :], psy[64:128, 0:GN], ACT.Copy)
                    nc.scalar.activation(xa[q][0:D, :], psy[0:D, 0:GN], ACT.Copy)
                    nc.scalar.activation(xb[q][0:D, :], psy[0:D, 0:GN], ACT.Copy).then_inc(xh_ready, 1)

                def gelus(g):
                    for e in range(NE):
                        act.wait_ge(hid_ready, g * NE + e + 1)
                        nc.scalar.activation(hs[e % 4][:, :], psh[e % 2][:, 0:GN], ACT.Gelu).then_inc(hid_done, 1)

                def sums_out(g, q):
                    act.wait_ge(exp_ready, g + 1)
                    at_least(act, fold_ready, g - 1)
                    nc.scalar.activation(os_[q][:, :], pso[q][:, 0:GN], ACT.Copy).then_inc(os_ready, 1)

                def step(g, k, new, running, finishing, ahead):
                    if finishing:
                        sums_out(g - 2, k)
                    if new:
                        high_half(g, k)
                    if running:
                        gelus(g - 1)

                steps(act, step)

            @block.tensor
            def _(pe):
                def transposes(g, q):
                    pe.wait_ge(y_ready, g + 1)
                    at_least(pe, xh_ready, g)
                    at_least(pe, xl_ready, g)
                    for j in range(GT):
                        mm = nc.tensor.transpose(psy[:, j * TP:(j + 1) * TP], y[q][:, j, :, :].rearrange("p a f -> p (a f)"), w.ident[0:TP, 0:TP])
                    mm.then_inc(yt_ready, 1)

                def differences(g, q):
                    pe.wait_ge(xh_ready, g + 1)
                    pe.wait_ge(xl_ready, g + 1)
                    nc.tensor.matmul(psg[:, 0:GN], w.wga[:, :], xa[q][:, :], start=True, stop=False)
                    nc.tensor.matmul(psg[:, 0:GN], w.wgb[:, :], xb[q][0:D + 2, :], start=False, stop=True).then_inc(gate_ready, 1)

                def ranks(g, q):
                    wait_apart(pe, ge_ready, g + 1, passed)
                    nc.tensor.matmul(psr[0:NE, 0:GN], w.rank[:, :], ge[q][:, :], start=True, stop=True).then_inc(rank_ready, 1)

                def biases(g, q):
                    pe.wait_ge(masks_ready, g + 1)
                    at_least(pe, os_ready, g - 1)
                    nc.tensor.matmul(pso[q][:, 0:GN], w.b2[:, :], mk[q][:, :], start=True, stop=False)

                def hidden(g, q, e):
                    at_least(pe, hid_done, g * NE + e - 1)
                    nc.tensor.matmul(psh[e % 2][:, 0:GN], w.w1a[:, e, :], xa[q][:, :], start=True, stop=False)
                    nc.tensor.matmul(psh[e % 2][:, 0:GN], w.w1b[:, e, :], xb[q][:, :], start=False, stop=True).then_inc(hid_ready, 1)

                def outputs(g, q, e):
                    pe.wait_ge(hid_done, g * NE + e + 1)
                    mm = nc.tensor.matmul(pso[q][64 * (e % 2):64 * (e % 2) + 64, 0:GN], w.w2[:, e, :], hs[e % 4][:, :],
                                          start=False, stop=(e >= NE - 2))
                    if e == NE - 1:
                        mm.then_inc(exp_ready, 1)

                def folds(g, q):
                    pe.wait_ge(os_ready, g + 1)
                    at_least(pe, o_ready, g)
                    for j in range(GT):
                        mm = nc.tensor.matmul(psf[0:TP, j * D:(j + 1) * D], os_[q][:, j * TP:(j + 1) * TP], w.fold[:, :], start=True, stop=True)
                    mm.then_inc(fold_ready, 1)

                def step(g, k, new, running, finishing, ahead):
                    if new:
                        transposes(g, k)
                    if running:
                        biases(g - 1, 1 - k)
                        hidden(g - 1, 1 - k, 0)
                        hidden(g - 1, 1 - k, 1)
                    if finishing:
                        folds(g - 2, k)
                    for e2 in range(2, NE + 2, 2):
                        if new and e2 == 4:
                            differences(g, k)
                        if new and e2 == 6:
                            ranks(g, k)
                        for e in (e2, e2 + 1):
                            if running and e < NE:
                                hidden(g - 1, 1 - k, e)
                        for e in (e2 - 2, e2 - 1):
                            if running:
                                outputs(g - 1, 1 - k, e)

                pe.wait_ge(ones_set, 4)
                steps(pe, step)


def constants():
    f = np.float32

    def encoding(n):
        div = np.exp(np.arange(0, D, 2, dtype=f) * f(-np.log(10000.0) / D)).astype(f)
        ang = np.arange(n, dtype=f)[:, None] * div
        out = np.zeros((n, D), f)
        out[:, 0::2], out[:, 1::2] = np.sin(ang), np.cos(ang)
        return out

    t = np.arange(T)
    theta = BLK * np.arange(NBLK) + REL - 2
    step = (t[None, :] < theta[:, None]).astype(f)
    tau, r = np.arange(TP)[:, None], np.arange(NR)[None, :]
    off = np.zeros((NE, NE, HID), f)
    off[np.arange(NE), np.arange(NE), :] = OFF
    rank = np.zeros((NPAIR, NE), f)
    m = 0
    for a in range(NE - 1):
        for b in range(a + 1, NE):
            rank[m, a], rank[m, b] = -1, 1
            m += 1
    shift = np.zeros((NP_, NT, NODES), f)
    for i in range(NT):
        shift[np.arange(NP_), i, i * NP_ + np.arange(NP_)] = 1
    return dict(
        c_ident=np.eye(128, dtype=f), c_iota=np.tile(np.arange(NODES, dtype=f), (128, 1)),
        c_shift=shift.reshape(NP_, -1), c_pe=np.tile(encoding(NODES).T, (2, 1)),
        c_rel=np.concatenate([encoding(NR).T, np.ones((1, NR), f)]),
        c_headmask=np.repeat(np.eye(HEADS, dtype=f), HD, axis=0),
        c_blkmask=np.repeat((t[None, :] // BLK == np.arange(NBLK)[:, None]).astype(f), HEADS, axis=0),
        c_step=np.concatenate([step, step]),
        c_bandstep=(tau + r - REL < BLK * (tau // BLK) + REL - 2).astype(f),
        c_off=off.reshape(NE, -1), c_rank=rank, c_thr=(np.arange(NE, dtype=f) - 5)[:, None],
        c_fold=np.concatenate([np.eye(D, dtype=f)] * 2),
        c_rows4=np.array([[1, 0, 1, 0], [0, 1, 1, 0], [1, 0, 0, 1], [0, 1, 0, 1]], f),
    )


def layouts(a):
    NB = a["x"].shape[0]

    def by_dim(m):
        return np.ascontiguousarray(m.reshape(HEADS, HD, -1).transpose(1, 0, 2).reshape(D, -1))

    x = a["x"].reshape(NB, CH, GRID, PATCH, GRID, PATCH).transpose(1, 3, 5, 0, 2, 4).reshape(2, KP, NB, NODES)
    return dict(
        x_patch=np.ascontiguousarray(x.transpose(1, 2, 0, 3)), txt=a["txt"],
        w_embed=a["L0_tok_W_embed"], b_embed=a["L0_tok_b_embed"], w_gcn=a["L0_tok_W_gcn"], b_gcn=a["L0_tok_b_gcn"],
        w_out=a["L0_tok_W_out"], b_out=a["L0_tok_b_out"], edge_index=a["L0_tok_edge_index"],
        ln_gamma=a["L0_attn_ln_gamma"], ln_beta=a["L0_attn_ln_beta"],
        wq=a["L0_attn_Wq"], wq_t=np.ascontiguousarray(by_dim(a["L0_attn_Wq"]).T), bq=a["L0_attn_bq"],
        bq_perm=by_dim(a["L0_attn_bq"]).ravel(), u_perm=by_dim(a["L0_attn_u_bias"]).ravel(),
        wk_t=np.ascontiguousarray(by_dim(a["L0_attn_Wk"]).T), bk=by_dim(a["L0_attn_bk"]).ravel(),
        wv_t=np.ascontiguousarray(a["L0_attn_Wv"].T), bv=a["L0_attn_bv"],
        wpos_t=np.ascontiguousarray(a["L0_attn_Wpos"].T), bpos=a["L0_attn_bpos"],
        wo_t=np.ascontiguousarray(a["L0_attn_Wo"].T), bo=a["L0_attn_bo"], v_bias=a["L0_attn_v_bias"],
        wg=a["L0_ffn_Wg"], bg=a["L0_ffn_bg"], w1=a["L0_ffn_W1"], b1=a["L0_ffn_b1"], w2=a["L0_ffn_W2"], b2=a["L0_ffn_b2"],
    )


def build(nc, ins, out, NB):
    s = scratch_tensors(nc, NB)
    with ExitStack() as ctx:
        w = alloc_weights(nc, ctx)
        prepare(nc, w, ins, s, NB)
        tokens(nc, w, ins, s, NB)
        project(nc, w, s, NB)
        attend(nc, w, s, NB)
        experts(nc, w, s, out, NB)


def kernel(**inputs):
    import concourse.bacc as bacc
    from concourse.bass_utils import run_bass_kernel_spmd

    nc = bacc.Bacc("TRN2", target_bir_lowering=False, num_devices=1)
    a = {k: np.asarray(v) for k, v in inputs.items()}
    arrays = {**layouts(a), **constants()}
    import ml_dtypes
    arrays["c_shift"] = arrays["c_shift"].astype(ml_dtypes.bfloat16)
    arrays = {f"in_{k}": np.ascontiguousarray(v) for k, v in arrays.items()}
    ins = {k[3:]: nc.dram_tensor(k, v.shape, mybir.dt.from_np(v.dtype), kind="ExternalInput").ap() for k, v in arrays.items()}
    NB = a["x"].shape[0]
    out = nc.dram_tensor("out_tokens", (NB, T, D), F32, kind="ExternalOutput").ap()
    build(nc, ins, out, NB)
    r = run_bass_kernel_spmd(nc, [arrays], core_ids=[0])
    return r.results[0]["out_tokens"]
```
